# Optimizing a Trainium2 kernel written in Bass

```python
import numpy as np
import jax
import jax.numpy as jnp

def _softmax(x, axis=-1):
    return jax.nn.softmax(x, axis=axis)

def _gelu(x):
    return jax.nn.gelu(x, approximate=True)

def _silu(x):
    return jax.nn.silu(x)

def _sigmoid(x):
    return jax.nn.sigmoid(x)

def _layernorm(x, axis=-1, eps=1e-05):
    m = jnp.mean(x, axis=axis, keepdims=True)
    v = jnp.var(x, axis=axis, keepdims=True)
    return (x - m) / jnp.sqrt(v + eps)

def _scatter_add(tgt, idx, src, axis=0):
    return tgt.at[idx].add(src)

def _segment_sum(src, seg, n):
    return jax.ops.segment_sum(src, seg, n)
kernel_name = 'mk_adaln_d2_jaxref_r8_9ed50a'

def setup_inputs(seed: int=0):
    np.random.seed(seed)
    _w = jnp.asarray

    def _L0_attn_setup():
        import jax, jax.numpy as jnp
        import numpy as np
        D_MODEL = 128
        MAX_LEN = 256
        ORDER = 2
        BATCH = 4
        SEQ = 256
        key = jax.random.key(seed)
        k1, k2, k3, k4 = jax.random.split(key, 4)
        x = jax.random.normal(k1, (BATCH, SEQ, D_MODEL), dtype=jnp.float32)
        proj_w = jax.random.normal(k2, (D_MODEL, D_MODEL * (ORDER + 1)), dtype=jnp.float32) * D_MODEL ** (-0.5)
        proj_b = jax.random.normal(k3, (D_MODEL * (ORDER + 1),), dtype=jnp.float32) * 0.02
        filter_time = jax.random.normal(k4, (ORDER, 1, MAX_LEN, D_MODEL), dtype=jnp.float32) / MAX_LEN ** 0.5
        return {'x': x, 'proj_w': proj_w, 'proj_b': proj_b, 'filter_time': filter_time}
    _L0_attn_in = _L0_attn_setup()

    def _L0_ffn_setup():
        import jax, jax.numpy as jnp
        import numpy as np
        B, T, H = (2, 256, 128)
        I = 512
        HEADS = 4
        RET = 128
        NUM_EXPERTS = 512
        NUM_KEYS = 64
        K = 8
        key = jax.random.key(seed)
        ks = jax.random.split(key, 7)
        return {'hidden_states': jax.random.normal(ks[0], (B, T, H), jnp.float32), 'W_up': jax.random.normal(ks[1], (I, H), jnp.float32) * 0.02, 'W_down': jax.random.normal(ks[2], (H, I), jnp.float32) * 0.02, 'W_q': jax.random.normal(ks[3], (HEADS * RET, H), jnp.float32) * 0.02, 'keys': jax.random.normal(ks[4], (HEADS, NUM_KEYS, 2, RET // 2), jnp.float32) * 0.02, 'down_embed': jax.random.normal(ks[5], (NUM_EXPERTS, H), jnp.float32) * 0.02, 'up_embed': jax.random.normal(ks[6], (NUM_EXPERTS, H), jnp.float32) * 0.02}
    _L0_ffn_in = _L0_ffn_setup()
    _L0_c = _w((lambda *s: np.random.randn(*s).astype(np.float32) * 0.05)(4, 128))
    _L0_wmod = _w((lambda *s: np.random.randn(*s).astype(np.float32) * 0.05)(128, 6 * 128) * 128 ** (-0.5))

    def _L1_attn_setup():
        import jax, jax.numpy as jnp
        import numpy as np
        D_MODEL = 128
        N_HEADS = 16
        D_HEAD = 64
        LAMBDA_INIT = 0.8
        key = jax.random.key(seed)
        ks = jax.random.split(key, 6)
        B, S = (2, 256)
        std = 0.02
        x = jax.random.normal(ks[0], (B, S, D_MODEL), dtype=jnp.float32)
        Wq = jax.random.normal(ks[1], (D_MODEL, 2 * N_HEADS * D_HEAD), dtype=jnp.float32) * std
        Wk = jax.random.normal(ks[2], (D_MODEL, 2 * N_HEADS * D_HEAD), dtype=jnp.float32) * std
        Wv = jax.random.normal(ks[3], (D_MODEL, 2 * N_HEADS * D_HEAD), dtype=jnp.float32) * std
        Wo = jax.random.normal(ks[4], (N_HEADS * D_HEAD, D_MODEL), dtype=jnp.float32) * std
        lq1 = jnp.zeros((D_HEAD,), dtype=jnp.float32)
        lk1 = jnp.zeros((D_HEAD,), dtype=jnp.float32)
        lq2 = jnp.zeros((D_HEAD,), dtype=jnp.float32)
        lk2 = jnp.zeros((D_HEAD,), dtype=jnp.float32)
        return {'x': x, 'Wq': Wq, 'Wk': Wk, 'Wv': Wv, 'Wo': Wo, 'lq1': lq1, 'lk1': lk1, 'lq2': lq2, 'lk2': lk2}
    _L1_attn_in = _L1_attn_setup()

    def _L1_ffn_setup():
        import jax, jax.numpy as jnp
        import numpy as np
        from jax.scipy.linalg import expm
        B, S, D, E, K, NROT = (2, 256, 128, 8, 2, 3)
        EPS = 1e-05

        def _gelu(x):
            return jax.nn.gelu(x, approximate=False)

        def _forward(x, ln_gamma, ln_beta, abel_w, abel_b, moe_gate_w, moe_gate_b, ew1, eb1, ew2, eb2, gens, gc_w, gc_b):
            residual = x
            mu = jnp.mean(x, axis=-1, keepdims=True)
            var = jnp.mean((x - mu) ** 2, axis=-1, keepdims=True)
            xn = (x - mu) * jax.lax.rsqrt(var + EPS) * ln_gamma + ln_beta
            abel_out = _gelu(xn @ abel_w + abel_b)
            logits = xn @ moe_gate_w + moe_gate_b
            topw, topi = jax.lax.top_k(logits, K)
            topw = jax.nn.softmax(topw, axis=-1)
            w_dense = jnp.sum(jax.nn.one_hot(topi, E, dtype=xn.dtype) * topw[..., None], axis=-2)
            h = _gelu(jnp.einsum('bsd,edh->ebsh', xn, ew1) + eb1[:, None, None, :])
            eo = jnp.einsum('ebsh,ehd->ebsd', h, ew2) + eb2[:, None, None, :]
            moe_out = jnp.einsum('ebsd,bse->bsd', eo, w_dense)
            for i in range(NROT):
                moe_out = moe_out @ expm(gens[i])
            combined = jnp.concatenate([abel_out, moe_out], axis=-1)
            gate = jax.nn.sigmoid(combined @ gc_w + gc_b)
            mixed = abel_out * (1.0 - gate) + moe_out * gate
            return residual + mixed
        key = jax.random.key(seed)
        ks = jax.random.split(key, 16)
        sc = 0.02
        x = jax.random.normal(ks[0], (B, S, D), jnp.float32)
        ln_gamma = 1.0 + sc * jax.random.normal(ks[1], (D,), jnp.float32)
        ln_beta = sc * jax.random.normal(ks[2], (D,), jnp.float32)
        abel_w = sc * jax.random.normal(ks[3], (D, D), jnp.float32)
        abel_b = sc * jax.random.normal(ks[4], (D,), jnp.float32)
        moe_gate_w = sc * jax.random.normal(ks[5], (D, E), jnp.float32)
        moe_gate_b = sc * jax.random.normal(ks[6], (E,), jnp.float32)
        ew1 = sc * jax.random.normal(ks[7], (E, D, 2 * D), jnp.float32)
        eb1 = sc * jax.random.normal(ks[8], (E, 2 * D), jnp.float32)
        ew2 = sc * jax.random.normal(ks[9], (E, 2 * D, D), jnp.float32)
        eb2 = sc * jax.random.normal(ks[10], (E, D), jnp.float32)
        g = sc * jax.random.normal(ks[11], (NROT, D, D), jnp.float32)
        gens = 0.5 * (g - jnp.swapaxes(g, -1, -2))
        gc_w = sc * jax.random.normal(ks[12], (2 * D, 1), jnp.float32)
        gc_b = sc * jax.random.normal(ks[13], (1,), jnp.float32)
        return dict(x=x, ln_gamma=ln_gamma, ln_beta=ln_beta, abel_w=abel_w, abel_b=abel_b, moe_gate_w=moe_gate_w, moe_gate_b=moe_gate_b, ew1=ew1, eb1=eb1, ew2=ew2, eb2=eb2, gens=gens, gc_w=gc_w, gc_b=gc_b)
    _L1_ffn_in = _L1_ffn_setup()
    _L1_c = _w((lambda *s: np.random.randn(*s).astype(np.float32) * 0.05)(4, 128))
    _L1_wmod = _w((lambda *s: np.random.randn(*s).astype(np.float32) * 0.05)(128, 6 * 128) * 128 ** (-0.5))
    _d = {'L0_attn_x': _L0_attn_in['x'], 'L0_attn_proj_w': _L0_attn_in['proj_w'], 'L0_attn_proj_b': _L0_attn_in['proj_b'], 'L0_attn_filter_time': _L0_attn_in['filter_time'], 'L0_ffn_W_up': _L0_ffn_in['W_up'], 'L0_ffn_W_down': _L0_ffn_in['W_down'], 'L0_ffn_W_q': _L0_ffn_in['W_q'], 'L0_ffn_keys': _L0_ffn_in['keys'], 'L0_ffn_down_embed': _L0_ffn_in['down_embed'], 'L0_ffn_up_embed': _L0_ffn_in['up_embed'], 'L0_c': _L0_c, 'L0_wmod': _L0_wmod, 'L1_attn_Wq': _L1_attn_in['Wq'], 'L1_attn_Wk': _L1_attn_in['Wk'], 'L1_attn_Wv': _L1_attn_in['Wv'], 'L1_attn_Wo': _L1_attn_in['Wo'], 'L1_attn_lq1': _L1_attn_in['lq1'], 'L1_attn_lk1': _L1_attn_in['lk1'], 'L1_attn_lq2': _L1_attn_in['lq2'], 'L1_attn_lk2': _L1_attn_in['lk2'], 'L1_ffn_ln_gamma': _L1_ffn_in['ln_gamma'], 'L1_ffn_ln_beta': _L1_ffn_in['ln_beta'], 'L1_ffn_abel_w': _L1_ffn_in['abel_w'], 'L1_ffn_abel_b': _L1_ffn_in['abel_b'], 'L1_ffn_moe_gate_w': _L1_ffn_in['moe_gate_w'], 'L1_ffn_moe_gate_b': _L1_ffn_in['moe_gate_b'], 'L1_ffn_ew1': _L1_ffn_in['ew1'], 'L1_ffn_eb1': _L1_ffn_in['eb1'], 'L1_ffn_ew2': _L1_ffn_in['ew2'], 'L1_ffn_eb2': _L1_ffn_in['eb2'], 'L1_ffn_gens': _L1_ffn_in['gens'], 'L1_ffn_gc_w': _L1_ffn_in['gc_w'], 'L1_ffn_gc_b': _L1_ffn_in['gc_b'], 'L1_c': _L1_c, 'L1_wmod': _L1_wmod}
    _x0 = _d['L0_attn_x']
    _d['L0_attn_x'] = jax.random.normal(jax.random.fold_in(jax.random.key(seed), 1), (4, 512, 128), dtype=_x0.dtype)
    del _x0
    return _d

def reference(L0_attn_x, L0_attn_proj_w, L0_attn_proj_b, L0_attn_filter_time, L0_ffn_W_up, L0_ffn_W_down, L0_ffn_W_q, L0_ffn_keys, L0_ffn_down_embed, L0_ffn_up_embed, L0_c, L0_wmod, L1_attn_Wq, L1_attn_Wk, L1_attn_Wv, L1_attn_Wo, L1_attn_lq1, L1_attn_lk1, L1_attn_lq2, L1_attn_lk2, L1_ffn_ln_gamma, L1_ffn_ln_beta, L1_ffn_abel_w, L1_ffn_abel_b, L1_ffn_moe_gate_w, L1_ffn_moe_gate_b, L1_ffn_ew1, L1_ffn_eb1, L1_ffn_ew2, L1_ffn_eb2, L1_ffn_gens, L1_ffn_gc_w, L1_ffn_gc_b, L1_c, L1_wmod):

    def _L0_attn_ref(x, proj_w, proj_b, filter_time):
        import jax, jax.numpy as jnp
        import numpy as np
        D_MODEL = 128
        MAX_LEN = 256
        ORDER = 2
        BATCH = 4
        SEQ = 256
        B, L, D = x.shape
        order, _, max_length, _ = filter_time.shape
        fft_size = 2 * max_length
        p = (jnp.einsum('bld,de->ble', x, proj_w) + proj_b).reshape(B, L, order + 1, D)
        v = p[:, :, 0, :]
        for stage in range(order):
            vf = jnp.fft.rfft(v, n=fft_size, axis=1)
            ff = jnp.fft.rfft(filter_time[stage], n=fft_size, axis=1)
            conv = jnp.fft.irfft(vf * ff, n=fft_size, axis=1)[:, :L, :]
            v = conv * p[:, :, stage + 1, :]
        return v

    def _L0_ffn_ref(hidden_states, W_up, W_down, W_q, keys, down_embed, up_embed):
        import jax, jax.numpy as jnp
        import numpy as np
        B, T, H = (2, 256, 128)
        I = 512
        HEADS = 4
        RET = 128
        NUM_EXPERTS = 512
        NUM_KEYS = 64
        K = 8
        b, t, hd = hidden_states.shape
        h, nk, _, n = keys.shape
        q = jnp.einsum('btd,ed->bte', hidden_states, W_q)
        q = q.reshape(b, t, 2, h, n).transpose(2, 0, 1, 3, 4)
        sim = jnp.einsum('pbthn,hkpn->pbthk', q, keys)
        scores_xy, idx_xy = jax.lax.top_k(sim, K)
        sx, sy = (scores_xy[0], scores_xy[1])
        ix, iy = (idx_xy[0], idx_xy[1])
        all_scores = (sx[..., :, None] + sy[..., None, :]).reshape(b, t, h, K * K)
        all_idx = (ix[..., :, None] * nk + iy[..., None, :]).reshape(b, t, h, K * K)
        scores, pk = jax.lax.top_k(all_scores, K)
        indices = jnp.take_along_axis(all_idx, pk, axis=-1)
        de = down_embed[indices]
        ue = up_embed[indices]
        w = jax.nn.silu(jnp.einsum('btd,bthkd->bthk', hidden_states, de) * jax.nn.softmax(scores, axis=-1))
        experts_states = jnp.einsum('bthk,bthkd->btd', w, ue)
        dense = jnp.einsum('bti,di->btd', jax.nn.silu(jnp.einsum('btd,id->bti', hidden_states, W_up)), W_down)
        return dense + experts_states

    def _L1_attn_ref(x, Wq, Wk, Wv, Wo, lq1, lk1, lq2, lk2):
        import jax, jax.numpy as jnp
        import numpy as np
        D_MODEL = 128
        N_HEADS = 16
        D_HEAD = 64
        LAMBDA_INIT = 0.8
        B, S, D = x.shape
        h, dh = (N_HEADS, D_HEAD)
        q = (x @ Wq).reshape(B, S, 2, h, dh)
        k = (x @ Wk).reshape(B, S, 2, h, dh)
        v = (x @ Wv).reshape(B, S, 2, h, dh)
        q1, q2 = (q[:, :, 0], q[:, :, 1])
        k1, k2 = (k[:, :, 0], k[:, :, 1])
        v1, v2 = (v[:, :, 0], v[:, :, 1])
        scale = 1.0 / jnp.sqrt(jnp.asarray(dh, dtype=x.dtype))
        lam = jnp.exp(jnp.dot(lq1, lk1)) - jnp.exp(jnp.dot(lq2, lk2)) + LAMBDA_INIT
        causal = jnp.tril(jnp.ones((S, S), dtype=bool))
        neg_inf = jnp.asarray(-1e+30, dtype=x.dtype)
        s1 = jnp.einsum('bshd,bthd->bhst', q1, k1) * scale
        s2 = jnp.einsum('bshd,bthd->bhst', q2, k2) * scale
        s1 = jnp.where(causal, s1, neg_inf)
        s2 = jnp.where(causal, s2, neg_inf)
        a1 = jax.nn.softmax(s1, axis=-1)
        a2 = jax.nn.softmax(s2, axis=-1)
        o = jnp.einsum('bhst,bthd->bshd', a1, v1) - lam * jnp.einsum('bhst,bthd->bshd', a2, v2)
        o = o.reshape(B, S, h * dh) * (1.0 - LAMBDA_INIT)
        return o @ Wo

    def _L1_ffn_ref(x, ln_gamma, ln_beta, abel_w, abel_b, moe_gate_w, moe_gate_b, ew1, eb1, ew2, eb2, gens, gc_w, gc_b):
        import jax, jax.numpy as jnp
        import numpy as np
        from jax.scipy.linalg import expm
        B, S, D, E, K, NROT = (2, 256, 128, 8, 2, 3)
        EPS = 1e-05

        def _gelu(x):
            return jax.nn.gelu(x, approximate=False)

        def _forward(x, ln_gamma, ln_beta, abel_w, abel_b, moe_gate_w, moe_gate_b, ew1, eb1, ew2, eb2, gens, gc_w, gc_b):
            residual = x
            mu = jnp.mean(x, axis=-1, keepdims=True)
            var = jnp.mean((x - mu) ** 2, axis=-1, keepdims=True)
            xn = (x - mu) * jax.lax.rsqrt(var + EPS) * ln_gamma + ln_beta
            abel_out = _gelu(xn @ abel_w + abel_b)
            logits = xn @ moe_gate_w + moe_gate_b
            topw, topi = jax.lax.top_k(logits, K)
            topw = jax.nn.softmax(topw, axis=-1)
            w_dense = jnp.sum(jax.nn.one_hot(topi, E, dtype=xn.dtype) * topw[..., None], axis=-2)
            h = _gelu(jnp.einsum('bsd,edh->ebsh', xn, ew1) + eb1[:, None, None, :])
            eo = jnp.einsum('ebsh,ehd->ebsd', h, ew2) + eb2[:, None, None, :]
            moe_out = jnp.einsum('ebsd,bse->bsd', eo, w_dense)
            for i in range(NROT):
                moe_out = moe_out @ expm(gens[i])
            combined = jnp.concatenate([abel_out, moe_out], axis=-1)
            gate = jax.nn.sigmoid(combined @ gc_w + gc_b)
            mixed = abel_out * (1.0 - gate) + moe_out * gate
            return residual + mixed
        return _forward(x, ln_gamma, ln_beta, abel_w, abel_b, moe_gate_w, moe_gate_b, ew1, eb1, ew2, eb2, gens, gc_w, gc_b)
    x = L0_attn_x
    mod = (_silu(L0_c) @ L0_wmod).reshape(L0_c.shape[0], 6, 1, -1)
    sa, ca, ga, sb, cb, gb = (mod[:, 0], mod[:, 1], mod[:, 2], mod[:, 3], mod[:, 4], mod[:, 5])
    ga = (2 * (ga >= 0) - 1) * jnp.maximum(jnp.abs(ga), 0.25)
    gb = (2 * (gb >= 0) - 1) * jnp.maximum(jnp.abs(gb), 0.25)
    h = _layernorm(x, axis=-1) * (1 + ca) + sa
    x = x + ga * _L0_attn_ref(h, L0_attn_proj_w, L0_attn_proj_b, L0_attn_filter_time)
    h = _layernorm(x, axis=-1) * (1 + cb) + sb
    x = x + gb * _L0_ffn_ref(h, L0_ffn_W_up, L0_ffn_W_down, L0_ffn_W_q, L0_ffn_keys, L0_ffn_down_embed, L0_ffn_up_embed)
    mod = (_silu(L1_c) @ L1_wmod).reshape(L1_c.shape[0], 6, 1, -1)
    sa, ca, ga, sb, cb, gb = (mod[:, 0], mod[:, 1], mod[:, 2], mod[:, 3], mod[:, 4], mod[:, 5])
    ga = (2 * (ga >= 0) - 1) * jnp.maximum(jnp.abs(ga), 0.25)
    gb = (2 * (gb >= 0) - 1) * jnp.maximum(jnp.abs(gb), 0.25)
    h = _layernorm(x, axis=-1) * (1 + ca) + sa
    x = x + ga * _L1_attn_ref(h, L1_attn_Wq, L1_attn_Wk, L1_attn_Wv, L1_attn_Wo, L1_attn_lq1, L1_attn_lk1, L1_attn_lq2, L1_attn_lk2)
    h = _layernorm(x, axis=-1) * (1 + cb) + sb
    x = x + gb * _L1_ffn_ref(h, L1_ffn_ln_gamma, L1_ffn_ln_beta, L1_ffn_abel_w, L1_ffn_abel_b, L1_ffn_moe_gate_w, L1_ffn_moe_gate_b, L1_ffn_ew1, L1_ffn_eb1, L1_ffn_ew2, L1_ffn_eb2, L1_ffn_gens, L1_ffn_gc_w, L1_ffn_gc_b)
    return x

_drawn_inputs = setup_inputs


def setup_inputs(seed=0):
    import zlib

    import numpy as np

    out = dict(_drawn_inputs(seed))
    spreads = {'L1_attn_lq1': (0.0, 2.0),
     'L1_attn_lk1': (0.0, 2.0),
     'L1_attn_lq2': (0.0, 0.8),
     'L1_attn_lk2': (0.0, 0.8)}
    factors = {'L0_attn_proj_b': 6.864,
     'L0_ffn_W_up': 4.287,
     'L0_ffn_W_down': 4.107,
     'L0_ffn_W_q': 8.0,
     'L0_ffn_keys': 8.0,
     'L0_ffn_down_embed': 8.0,
     'L0_ffn_up_embed': 8.0,
     'L1_attn_Wq': 8.0,
     'L1_attn_Wk': 8.0,
     'L1_attn_Wv': 8.0,
     'L1_attn_Wo': 8.0,
     'L1_ffn_ln_gamma': 58.317,
     'L1_ffn_ln_beta': 41.416,
     'L1_ffn_abel_w': 4.114,
     'L1_ffn_abel_b': 200.0,
     'L1_ffn_moe_gate_w': 8.0,
     'L1_ffn_moe_gate_b': 64.0,
     'L1_ffn_ew1': 8.0,
     'L1_ffn_eb1': 64.0,
     'L1_ffn_ew2': 8.0,
     'L1_ffn_eb2': 200.0,
     'L1_ffn_gens': 8.0,
     'L1_ffn_gc_w': 8.0}
    for name, (base, spread) in spreads.items():
        noise = np.random.default_rng([zlib.crc32(name.encode()), seed]).standard_normal(out[name].shape)
        drawn = base * np.exp(spread * noise) if base else spread * noise
        out[name] = jnp.asarray(drawn.astype(out[name].dtype))
    for name, factor in factors.items():
        out[name] = (out[name] * factor).astype(out[name].dtype)
    return out
```

```python
from contextlib import ExitStack, contextmanager

import numpy as np

import concourse.bass as bass
from concourse import mybir
from concourse.alu_op_type import AluOpType as ALU

F32 = mybir.dt.float32
BF16 = mybir.dt.bfloat16
U32 = mybir.dt.uint32
ACT = mybir.ActivationFunctionType
AX = mybir.AxisListType
MAX_REDUCE = bass.bass_isa.ReduceOp.max

P = 128
B, S, D = 4, 512, 128
NT = S // P
TAPS = 256
ORDER = 2
I_UP = 512
PH, KEYS, TOP, PN = 4, 64, 8, 64
EXPERTS = 512
XROWS = EXPERTS // KEYS
H1, DH = 16, 64
PAIRS = H1 // 2
LAMBDA_INIT = 0.8
E1, HID1, K1 = 8, 256, 2
HC = HID1 // P
NROT = 3
EPS = 1e-5
MAX_SQUARINGS = 16
EXPM_THETA = 0.5
TAYLOR = [1.0, 1.0, 1 / 2, 1 / 6, 1 / 24, 1 / 120, 1 / 720, 1 / 5040, 1 / 40320]
CAUSAL_FILL = -1e30


class Mark:

    def __init__(self, sem, base, n):
        self.sem, self.value = sem, base + n


class Progress:

    def __init__(self, name, sem, engine, step=1):
        self.name, self.sem, self.engine, self.step = name, sem, engine, step
        self.base, self.n = 0, 0

    def did(self, instruction):
        instruction.then_inc(self.sem, self.step)
        self.n += self.step
        return self.now()

    def now(self):
        return Mark(self.sem, self.base, self.n)

    def after(self, *marks):
        for m in marks:
            self.engine.wait_ge(m.sem, m.value)


class Loops:

    def __init__(self, nc, progresses, per):
        self.nc, self.progresses, self.per, self.seen = nc, progresses, per, {}

    @contextmanager
    def clearing(self, name, end, cleared):
        sems = [p.sem for p in cleared]
        first = min(s.num for s in sems)
        assert sorted(s.num for s in sems) == list(range(first, first + len(sems)))
        clear = range(first, first + len(sems))
        self.nc.all_engine_barrier(sems_to_clear=clear)
        for p in cleared:
            p.n = 0
        with self.loop(name, 0, end) as i:
            yield i
            self.nc.all_engine_barrier(sems_to_clear=clear)
            for p in cleared:
                p.n = 0
        for p in cleared:
            p.n = 0

    @contextmanager
    def loop(self, name, start, end):
        before = [(p.base, p.n) for p in self.progresses]
        turn = self.per.get(name, [0] * len(before))
        with self.nc.Fori(start, end) as i:
            for p, k in zip(self.progresses, turn):
                if k:
                    p.base = p.base + (i - start) * k if start else p.base + i * k
            yield i
        self.seen[name] = [p.n - n for p, (_, n) in zip(self.progresses, before)]
        for p, (base, n), k in zip(self.progresses, before, self.seen[name]):
            p.base, p.n = base, n + (end - start) * k


def host_constants():
    n = 2 * TAPS
    k = np.concatenate([np.arange(0, TAPS, 2), np.arange(1, TAPS, 2)])
    t = np.arange(n)
    ang = 2 * np.pi * ((k[:, None] * t[None, :]) % n) / n
    cos, sin = np.cos(ang), np.sin(ang)
    alt = np.where(t % 2 == 0, 1.0, -1.0)
    imag = -sin
    imag[0] = alt
    fwd = np.concatenate([cos, imag])
    inv_r, inv_i = 2 * cos / n, -2 * sin / n
    inv_r[0], inv_i[0] = 1 / n, alt / n
    inv = np.concatenate([inv_r, inv_i])
    fd = cos.copy()
    fd[0] = alt
    filt = np.stack([cos, -sin, fd])[:, :, :TAPS]
    f = np.float32
    fwd_half = fwd[:, :TAPS]
    sel = np.zeros((XROWS + KEYS, XROWS, KEYS))
    for i in range(XROWS):
        sel[i, i, :] = 1
    for j in range(KEYS):
        sel[XROWS + j, :, j] = -1
    small = np.zeros((1, 256))
    small[0, 0:TOP] = np.arange(TOP)
    small[0, 8:16] = np.arange(TOP) + 1
    small[0, 16:80] = 32.0 * np.arange(KEYS)
    small[0, 80:96] = EXPM_THETA * 2.0 ** np.arange(MAX_SQUARINGS)
    small[0, 96:113] = 2.0 ** -np.arange(MAX_SQUARINGS + 1)
    small[0, 113:130] = np.arange(MAX_SQUARINGS + 1)
    small[0, 130:134] = -0.5
    small[0, 134:142] = np.arange(E1)
    q = np.arange(P)
    return {
        "c_fwd": fwd_half.T.astype(f),
        "c_inv": inv.astype(f),
        "c_filt": filt.transpose(0, 2, 1).astype(f).copy(),
        "c_ident": np.eye(P, dtype=f),
        "c_mask": np.where(q[None, :] > q[:, None], CAUSAL_FILL, 0.0).astype(f),
        "c_sel": sel.reshape(XROWS + KEYS, EXPERTS).astype(f),
        "c_small": small.astype(f),
    }


def build(nc, per, a, out):
    es = ExitStack()
    with es:
        def sb(name, shape, dt=F32):
            return es.enter_context(nc.sbuf_tensor(name, shape, dt))

        def progress(name, engine, step=1):
            return Progress(name, es.enter_context(nc.semaphore(name)), engine, step)

        bank = [es.enter_context(nc.psum_tensor(f"bank{i}", [P, 512], F32)) for i in range(8)]

        pe = progress("pe_done", nc.tensor)
        dve = progress("dve_done", nc.vector)
        act = progress("act_done", nc.scalar)
        pool = progress("pool_done", nc.gpsimd)
        weights_in = progress("weights_in", nc.sync, 16)
        x_in = progress("x_in", nc.sync, 16)
        stage_in = [progress(f"stage_in{i}", nc.sync, 16) for i in range(2)]
        out_stored = progress("out_stored", nc.sync, 16)
        V, A, T, G = nc.vector, nc.scalar, nc.tensor, nc.gpsimd
        loops = Loops(nc, [pe, dve, act, pool, x_in, out_stored, *stage_in], per)

        arena = [sb(f"arena{i}", [P, 8192]) for i in range(2)]
        carved = {}

        def carve(i, phase, shape):
            words = int(np.prod(shape[1:]))
            at = carved.get((i, phase), 0)
            carved[i, phase] = at + words
            assert at + words <= 8192, (i, phase)
            names = "abcd"[:len(shape) - 1]
            v = arena[i][:, at:at + words]
            if len(shape) == 2:
                return v
            return v.rearrange(f"p ({' '.join(names)}) -> p {' '.join(names)}", **dict(zip(names, shape[1:])))

        def load(name, shape, src, place=None):
            tile = sb(name, shape) if place is None else place
            weights_in.did(nc.sync.dma_start(tile[tuple(slice(None) for _ in shape)], src))
            return tile

        small = load("small", [P, 256], a["c_small"][0:1, :].broadcast_to([P, 256]))
        ident = load("ident", [P, P], a["c_ident"])
        cT = [load(f"cT{l}", [P, B], a[f"cT{l}"]) for l in range(2)]
        wmod = [load(f"wmod{l}", [P, 6 * D], a[f"wmod{l}"], carve(1, "setup", [P, 6 * D])) for l in range(2)]
        proj_w = load("proj_w", [P, (ORDER + 1) * D], a["proj_w"])
        proj_b = load("proj_b", [P, (ORDER + 1) * D], a["proj_b"][0:1, :].broadcast_to([P, 3 * D]))
        taps = load("taps", [P, ORDER, TAPS // P, D], a["filter"].rearrange("o (c p) d -> p o c d", p=P), carve(1, "setup", [P, ORDER, TAPS // P, D]))
        c_filt = load("c_filt_sb", [P, 3, TAPS // P, TAPS], a["c_filt"].rearrange("m (c p) r -> p m c r", p=P), carve(0, "setup", [P, 3, TAPS // P, TAPS]))
        c_fwd = load("c_fwd_sb", [P, TAPS // P, S], a["c_fwd"].rearrange("(c p) r -> p c r", p=P))
        c_inv = load("c_inv_sb", [P, S // P, S], a["c_inv"].rearrange("(c p) t -> p c t", p=P))
        w_up = load("w_up", [P, I_UP], a["W_upT"])
        w_down = load("w_down", [P, I_UP // P, D], a["W_downT"].rearrange("(c p) d -> p c d", p=P))
        w_q = load("w_q", [P, 4, D], a["W_q"].rearrange("(c p) d -> p c d", p=P), carve(1, "setup", [P, 4, D]))
        keysT = load("keysT", [P, 4, KEYS], a["keysT"].rearrange("(c p) k -> p c k", p=P), carve(1, "setup", [P, 4, KEYS]))
        downT = load("downT", [P, EXPERTS], a["downT"])
        up_e = load("up_e", [P, EXPERTS // P, D], a["up_embed"].rearrange("(c p) d -> p c d", p=P))
        wv = load("wv", [P, H1, 2 * DH], a["Wv"].rearrange("d (h c) -> d h c", h=H1))
        wo = load("wo", [P, PAIRS, D], a["Wo"].rearrange("(g p) d -> p g d", p=P))
        lam_in = load("lam_in", [P, 4, DH], a["lam"].rearrange("(o q) c -> o q c", o=1).broadcast_to([P, 4, DH]), carve(1, "setup", [P, 4, DH]))
        gammaT = load("gammaT", [P, 2], a["gammabetaT"])
        abel_w = load("abel_w", [P, D], a["abel_w"])
        abel_b = load("abel_b", [P, D], a["abel_b"][0:1, :].broadcast_to([P, D]))
        gate_w = load("gate_w", [P, E1], a["gate_w"])
        gate_b = load("gate_b", [P, E1], a["gate_b"][0:1, :].broadcast_to([P, E1]))
        ew1 = load("ew1", [P, E1, HID1], a["ew1"].rearrange("e d h -> d e h"))
        eb1T = load("eb1T", [P, E1 * HC], a["eb1T"])
        ew2T = load("ew2T", [P, E1, HID1], a["ew2T"].rearrange("e m k -> m e k"), carve(0, "setup", [P, E1, HID1]))
        eb2T = load("eb2T", [P, E1], a["eb2T"])
        gens = load("gens_sb", [P, NROT, 2, D], a["gens2"].rearrange("i t p d -> p i t d"), carve(0, "setup", [P, NROT, 2, D]))
        gc_w = load("gc_w", [P, 2 * D], a["gc_w"][0:1, :].broadcast_to([P, 2 * D]))
        gc_b = load("gc_b", [P, 1], a["gc_b"][0:1, :].broadcast_to([P, 1]))
        maskf = load("maskf", [P, P], a["c_mask"], carve(1, "setup", [P, P]))
        self_ = load("self", [XROWS + KEYS, EXPERTS], a["c_sel"], carve(1, "setup", [P, EXPERTS])[0:XROWS + KEYS, :])
        weights = weights_in.now()

        identb = sb("identb", [P, P], BF16)
        mask = sb("mask", [P, P], BF16)
        sel = sb("sel", [XROWS + KEYS, EXPERTS], BF16)
        silT = sb("silT", [P, 2, B])
        silB = carve(1, "setup", [P, 2, B, P])
        modT = [sb(f"modT{l}", [P, 6, B]) for l in range(2)]
        modB = [sb(f"modB{l}", [P, B, 4, D]) for l in range(2)]
        signs = carve(1, "setup", [P, 2, B, D])
        gate_neg = carve(1, "setup", [P, 2, B, D])
        filt = sb("filt", [P, ORDER, 3, 2, D])
        msim = sb("msim", [P, 2, PH, KEYS])
        mpair = sb("mpair", [P, PH, XROWS, KEYS])
        lam_p = sb("lam_p", [P, 2, DH])
        lam_s = sb("lam_s", [P, 2])
        lam_row = sb("lam_row", [P, 2, DH])
        ew2R = sb("ew2R", [P, E1, HC, D])
        eb2R = sb("eb2R", [E1, D])

        for e in (pe, dve, act, pool):
            e.after(weights)
        A.preload_act_table_set("silu_and_others") if False else None
        m_sil = [act.did(A.activation(silT[:, l, :], cT[l][:, :], ACT.Silu)) for l in range(2)]
        dve.did(V.tensor_copy(identb[:, :], ident[:, :]))
        dve.did(V.tensor_copy(mask[:, :], maskf[:, :]))
        dve.did(V.tensor_copy(sel[:, :], self_[:, :]))
        dve.after(m_sil[1])
        m_silB = dve.did(V.tensor_copy(silB[:, :, :, :].rearrange("p l b q -> p (l b) q"),
                                       silT[:, :, :].rearrange("p l b -> p (l b)").unsqueeze(2).broadcast_to([P, 2 * B, P])))
        pe.after(m_sil[1], m_silB)
        for l in range(2):
            for s in range(6):
                T.matmul(bank[0][:, (l * 6 + s) * B:(l * 6 + s + 1) * B], wmod[l][:, s * D:(s + 1) * D],
                         silT[:, l, :], start=True, stop=True)
        m_bc = []
        for l in range(2):
            for b in range(B):
                m_bc.append(pe.did(T.matmul(bank[1 + (l * B + b) % 4][:, :], silB[:, l, b, :], wmod[l][:, 2 * D:6 * D],
                                            start=True, stop=True)))
                if l == 0 and b == B - 1:
                    m_first = [None] * B
                    for bb in range(B):
                        dve.after(m_bc[bb])
                        m_first[bb] = dve.did(V.tensor_copy(modB[0][:, bb, :, :], bank[1 + bb][:, :].rearrange("p (s d) -> p s d", s=4)))
                    pe.after(m_first[B - 1])
        for bb in range(B):
            dve.after(m_bc[B + bb])
            dve.did(V.tensor_copy(modB[1][:, bb, :, :], bank[1 + bb][:, :].rearrange("p (s d) -> p s d", s=4)))
        for l in range(2):
            m_t = dve.did(V.tensor_copy(modT[l][:, :, :], bank[0][:, l * 6 * B:(l + 1) * 6 * B].rearrange("p (s b) -> p s b", s=6)))
        dve.after(m_t)
        for l in range(2):
            for s in (1, 4):
                dve.did(V.tensor_scalar(modT[l][:, s, :], modT[l][:, s, :], 1.0, None, ALU.add))
        dve.did(V.tensor_scalar(modB[1][:, :, 2, :], modB[1][:, :, 2, :], 1.0, None, ALU.add))
        for l in range(2):
            for k, s in enumerate((0, 3)):
                g = modB[l][:, :, s, :]
                m = dve.did(V.tensor_scalar(signs[:, k, :, :], g, 0.0, 2.0, ALU.is_ge, ALU.mult))
                neg = gate_neg[:, k, :, :]
                dve.after(dve.did(V.tensor_scalar(neg, g, -1.0, 0.25, ALU.mult, ALU.max)))
                m = dve.did(V.tensor_tensor(g, g, neg, ALU.max))
                dve.after(m)
                m = dve.did(V.scalar_tensor_tensor(g, signs[:, k, :, :], -1.0, g, ALU.add, ALU.mult))
                dve.after(m)

        dve.after(dve.did(V.tensor_tensor(lam_p[:, :, :], lam_in[:, 0::2, :], lam_in[:, 1::2, :], ALU.mult)))
        m = dve.did(V.tensor_reduce(lam_s[:, :], lam_p[:, :, :], AX.X, ALU.add))
        act.after(m)
        m = act.did(A.activation(lam_s[:, :], lam_s[:, :], ACT.Exp))
        dve.after(m)
        m = dve.did(V.tensor_tensor(lam_s[:, 0:1], lam_s[:, 1:2], lam_s[:, 0:1], ALU.subtract))
        dve.did(V.memset(lam_row[:, 0, :], 1.0))
        dve.did(V.memset(lam_row[:, 1, :], -LAMBDA_INIT))
        dve.after(dve.now())
        dve.did(V.tensor_scalar(lam_row[:, 1, :], lam_row[:, 1, :], lam_s[:, 0:1], None, ALU.add))

        for o in range(ORDER):
            for f in range(3):
                for c in range(2):
                    for kt in range(TAPS // P):
                        last = T.matmul(bank[5 + o][:, ((f * 2 + c) % 4) * D:((f * 2 + c) % 4 + 1) * D] if f < 2 else
                                        bank[7][:, (o * 2 + c) * D:(o * 2 + c + 1) * D],
                                        c_filt[:, f, kt, c * P:(c + 1) * P], taps[:, o, kt, :],
                                        start=(kt == 0), stop=(kt == TAPS // P - 1))
        m = pe.did(last)
        dve.after(m)
        for o in range(ORDER):
            dve.did(V.tensor_copy(filt[:, o, 0:2, :, :], bank[5 + o][:, :].rearrange("p (f c d) -> p f c d", f=2, c=2)))
            dve.did(V.tensor_copy(filt[:, o, 2, :, :], bank[7][:, o * 2 * D:(o + 1) * 2 * D].rearrange("p (c d) -> p c d", c=2)))
        m_filt = dve.now()

        pe.after(m_filt)
        for ph in range(2):
            for h in range(PH):
                r = slice(PN * (h % 2), PN * (h % 2) + PN)
                c = ph * 2 + h // 2
                last = T.matmul(bank[5 + h % 2][:, (ph * PH + h) // 2 * KEYS:((ph * PH + h) // 2 + 1) * KEYS],
                                w_q[r, c, :], keysT[r, c, :], start=True, stop=True)
        m = pe.did(last)
        dve.after(m)
        for h2 in range(2):
            dve.did(V.tensor_copy(msim[:, :, h2::2, :].rearrange("p a h k -> p (a h) k") if False else
                                  msim[:, 0, h2::2, :], bank[5 + h2][:, 0:2 * KEYS].rearrange("p (h k) -> p h k", h=2)))
            dve.did(V.tensor_copy(msim[:, 1, h2::2, :], bank[5 + h2][:, 2 * KEYS:4 * KEYS].rearrange("p (h k) -> p h k", h=2)))
        dve.after(dve.now())
        for h in range(PH):
            dve.did(V.tensor_tensor(mpair[:, h, :, :],
                                    msim[:, 0, h, 0:XROWS].unsqueeze(2).broadcast_to([P, XROWS, KEYS]),
                                    msim[:, 1, h, :].unsqueeze(1).broadcast_to([P, XROWS, KEYS]), ALU.add))

        NG2 = NROT * 2
        xb = carve(0, "setup", [P, NROT, 2, D])
        xb2 = carve(0, "setup", [P, NROT, 2, D])
        xb3 = carve(0, "setup", [P, NROT, 2, D])
        xp = carve(0, "setup", [P, NROT, 2, D])
        xe = carve(0, "setup", [P, NROT, 2, D])
        norm = sb("xm_norm", [P, NROT])
        over = sb("xm_over", [P, MAX_SQUARINGS, NROT])
        steps = sb("xm_steps", [P, NROT])
        onehot = sb("xm_onehot", [P, NROT, MAX_SQUARINGS + 1])
        scale = sb("xm_scale", [P, NROT])
        m = dve.did(V.tensor_reduce(norm[:, :], gens[:, :, 0, :], AX.X, ALU.add, apply_absolute_value=True))
        pool.after(m)
        normall = sb("xm_normall", [P, NROT])
        m = pool.did(G.partition_all_reduce(normall[:, :], norm[:, :], P, MAX_REDUCE))
        dve.after(m)
        dve.after(dve.did(V.tensor_tensor(over[:, :, :], normall[:, :].unsqueeze(1).broadcast_to([P, MAX_SQUARINGS, NROT]),
                                          small[:, 80:96].unsqueeze(2).broadcast_to([P, MAX_SQUARINGS, NROT]), ALU.is_gt)))
        dve.after(dve.did(V.tensor_reduce(steps[:, :], over[:, :, :].rearrange("p k g -> p g k"), AX.X, ALU.add)))
        dve.after(dve.did(V.tensor_tensor(onehot[:, :, :], steps[:, :].unsqueeze(2).broadcast_to([P, NROT, MAX_SQUARINGS + 1]),
                                          small[:, 113:130].unsqueeze(1).broadcast_to([P, NROT, MAX_SQUARINGS + 1]), ALU.is_equal)))
        dve.after(dve.did(V.tensor_tensor(onehot[:, :, :], onehot[:, :, :],
                                          small[:, 96:113].unsqueeze(1).broadcast_to([P, NROT, MAX_SQUARINGS + 1]), ALU.mult)))
        dve.after(dve.did(V.tensor_reduce(scale[:, :], onehot[:, :, :], AX.X, ALU.add)))
        for i in range(NROT):
            dve.did(V.tensor_scalar(xb[:, i, :, :], gens[:, i, :, :], scale[:, i:i + 1], None, ALU.mult))
        m = dve.now()

        def products(left, right, ready, into=(0, 1)):
            pe.after(ready)
            for side in range(2):
                for i in range(NROT):
                    last = T.matmul(bank[into[side]][:, i * D:(i + 1) * D], left[:, i, 1 - side, :], right[:, i, side, :],
                                    start=True, stop=True)
            return pe.did(last)

        def psum_of(side, into=(0, 1)):
            return bank[into[side]][:, 0:NROT * D].rearrange("p (i d) -> p i d", i=NROT)

        done = products(xb, xb, m)
        dve.after(done)
        for side in range(2):
            dve.did(V.tensor_copy(xb2[:, :, side, :], psum_of(side)))
        done = products(xb2, xb, dve.now())
        dve.after(done)
        for side in range(2):
            dve.did(V.tensor_copy(xb3[:, :, side, :], psum_of(side)))
        dve.after(dve.now())

        def poly(dst, c0, c1, c2):
            flat = lambda t: t[:, :, :, :].rearrange("p i s d -> p (i s) d")
            m1 = dve.did(V.tensor_scalar(flat(dst), flat(xb), c1, None, ALU.mult))
            dve.after(m1)
            m2 = dve.did(V.scalar_tensor_tensor(flat(dst), flat(xb2), c2, flat(dst), ALU.mult, ALU.add))
            dve.after(m2)
            for j in range(NG2):
                v = flat(dst)[:, j, :]
                m3 = dve.did(V.scalar_tensor_tensor(v, ident[:, :], c0, v, ALU.mult, ALU.add))
            return m3

        m = poly(xp, *TAYLOR[6:9])
        done = products(xb3, xp, m)
        m = poly(xe, *TAYLOR[3:6])
        dve.after(m, done)
        for side in range(2):
            dve.did(V.tensor_tensor(xe[:, :, side, :], xe[:, :, side, :], psum_of(side), ALU.add))
        m = dve.now()
        done = products(xb3, xe, m)
        dve.after(done)
        m = poly(xp, *TAYLOR[0:3])
        dve.after(m)
        for side in range(2):
            dve.did(V.tensor_tensor(xe[:, :, side, :], xp[:, :, side, :], psum_of(side), ALU.add))

        pe.after(dve.now())
        keep = sb("xm_keep", [P, MAX_SQUARINGS, NROT])
        dve.did(V.tensor_scalar(keep[:, :, :], over[:, :, :], -1.0, 1.0, ALU.mult, ALU.add))
        dve.after(dve.now())
        with loops.loop("squarings", 0, MAX_SQUARINGS) as k:
            done = products(xe, xe, dve.now())
            dve.after(done)
            for side in range(2):
                dve.did(V.tensor_tensor(xp[:, :, side, :], psum_of(side), over[:, k, :].unsqueeze(2).broadcast_to([P, NROT, D]), ALU.mult))
                dve.did(V.tensor_tensor(xe[:, :, side, :], xe[:, :, side, :], keep[:, k, :].unsqueeze(2).broadcast_to([P, NROT, D]), ALU.mult))
            dve.after(dve.now())
            dve.did(V.tensor_tensor(xe[:, :, :, :], xe[:, :, :, :], xp[:, :, :, :], ALU.add))
        rot = sb("rot", [P, D])
        rotT = sb("rotT", [P, D])
        pe.after(dve.now())
        m = pe.did(T.matmul(bank[2][:, 0:D], xe[:, 1, 0, :], xe[:, 0, 1, :], start=True, stop=True))
        dve.after(m)
        m = dve.did(V.tensor_copy(rotT[:, :], bank[2][:, 0:D]))
        pe.after(m)
        m = pe.did(T.matmul(bank[2][:, 0:D], rotT[:, :], xe[:, 2, 0, :], start=True, stop=True))
        dve.after(m)
        m = dve.did(V.tensor_copy(rot[:, :], bank[2][:, 0:D]))
        pe.after(m)
        for e in range(E1):
            for c in range(HC):
                j = e * HC + c
                last = T.matmul(bank[3 + j // 4][:, (j % 4) * D:(j % 4 + 1) * D], ew2T[:, e, c * P:(c + 1) * P], rot[:, :],
                                start=True, stop=True)
        m = pe.did(last)
        m2 = pe.did(T.matmul(bank[7][0:E1, 0:D], eb2T[:, :], rot[:, :], start=True, stop=True))
        dve.after(m2)
        for j in range(4):
            dve.did(V.tensor_copy(ew2R[:, 2 * j:2 * j + 2, :, :], bank[3 + j][:, :].rearrange("p (e c d) -> p e c d", e=2, c=HC)))
        dve.did(V.tensor_copy(eb2R[:, :], bank[7][0:E1, 0:D]))

        x = sb("x", [P, NT, D])
        modc = [sb(f"modc{l}", [P, 6]) for l in range(2)]
        modr = [sb(f"modr{l}", [P, 4, D]) for l in range(2)]
        stats = sb("stats", [P, NT, 6])
        mv = sb("mv", [P, NT, 2])
        rstd = sb("rstd", [P, NT])
        xhat = sb("xhat", [P, NT, D])
        hT = sb("hT", [P, S])
        pv = carve(0, "conv", [P, NT, ORDER + 1, D])
        fold_s = carve(0, "conv", [P, 2, 2, D])
        spec = carve(0, "conv", [P, 2, 2, D])
        spec_t = carve(0, "conv", [P, 2, 2, D])
        spec_o = carve(0, "conv", [P, 2, 2, D])
        gT = sb("gT", [P, I_UP // P, S])

        def layernorm(src):
            for t in range(NT):
                dve.did(V.bn_stats(stats[:, t, :], src[:, t, :]))
            dve.after(dve.now())
            for t in range(NT):
                dve.did(V.bn_aggr(mv[:, t, :], stats[:, t, :]))
            dve.after(dve.now())
            m = dve.did(V.tensor_scalar(rstd[:, :], mv[:, :, 1], EPS, None, ALU.add))
            pool.after(m)
            m = pool.did(G.tensor_tensor(rstd[:, :], rstd[:, :], small[:, 130:134], ALU.pow))
            dve.after(m)
            for t in range(NT):
                m = dve.did(V.tensor_scalar(xhat[:, t, :], src[:, t, :], mv[:, t, 0:1], rstd[:, t:t + 1], ALU.subtract, ALU.mult))
            return m

        def transposed(dst, src, ready, scale_ap, shift_ap, into=0):
            pe.after(ready)
            for t in range(NT):
                last = T.transpose(bank[into][:, t * P:(t + 1) * P], src[:, t, :], ident[:, :])
            m = pe.did(last)
            dve.after(m)
            return dve.did(V.tensor_scalar(dst[:, :], bank[into][:, :], scale_ap, shift_ap, ALU.mult, ALU.add))

        def rows(ap):
            return ap.unsqueeze(1).broadcast_to([P, NT, D])

        sim = sb("sim", [P, 2 * PH, KEYS])
        gd = carve(1, "experts", [P, NT, EXPERTS])
        tops = sb("tops", [P, 2 * PH, TOP])
        topi = sb("topi", [P, 2 * PH, TOP], U32)
        topf = sb("topf", [P, 2 * PH, TOP])
        pair = carve(1, "experts", [P, PH, TOP, TOP])
        pair_r = carve(1, "experts", [P, PH, TOP * TOP])
        best = sb("best", [P, PH, TOP])
        negbest = sb("negbest", [P, PH])
        chosen = carve(1, "experts", [P, PH, TOP, TOP])
        cnt = sb("cnt", [P, PH, TOP])
        eqx = carve(1, "experts", [P, PH, XROWS, TOP])
        yval = sb("yval", [P, PH, TOP])
        ydiff = carve(1, "experts", [P, PH, KEYS, TOP])
        code = sb("code", [P, PH, XROWS + KEYS], BF16)
        codeT = sb("codeT", [XROWS + KEYS, PH, P], BF16)
        epair = carve(1, "experts", [P, PH, TOP * TOP])
        esum = sb("esum", [P, PH])
        rsum = sb("rsum", [P, NT, PH])
        past = sb("past", [P, PH, TOP])
        zpast = carve(1, "experts", [P, NT, PH, TOP * TOP])
        wpast = sb("wpast", [P, NT])
        junk = carve(1, "experts", [P, PH * TOP * TOP])
        prob = carve(0, "experts", [P, NT, PH, EXPERTS])
        wsum = carve(1, "experts", [P, 2, EXPERTS])
        wT = sb("wT", [P, EXPERTS // P, P])

        wq_s = [sb(f"wq_s{i}", [P, 2 * DH]) for i in range(2)]
        wk_s = [sb(f"wk_s{i}", [P, 2 * DH]) for i in range(2)]
        qT = [carve(1, "attention", [P, S]) for i in range(2)]
        kT = [carve(1, "attention", [P, S]) for i in range(2)]
        vv = [carve(1, "attention", [P, NT, 2, DH]) for i in range(2)]
        TRI = P * NT * (NT + 1) // 2
        prb = [carve(1, "attention", [P, TRI]) for i in range(2)]
        prbT = [carve(1, "attention", [P, TRI]) for i in range(2)]
        negmax = [sb(f"negmax{i}", [P, NT]) for i in range(2)]
        rowsum = [sb(f"rowsum{i}", [P, NT]) for i in range(2)]
        rnorm = [sb(f"rnorm{i}", [P, NT]) for i in range(2)]
        oT = sb("oT", [P, S])
        attn = sb("attn", [P, NT, D])

        res = carve(1, "mixture", [P, NT, D])
        abel = carve(1, "mixture", [P, NT, D])
        logit = sb("logit", [P, NT, E1])
        ltop = sb("ltop", [P, NT, TOP])
        lidx = sb("lidx", [P, NT, TOP], U32)
        lidf = sb("lidf", [P, NT, 2])
        lw = sb("lw", [P, NT, 2])
        wde = sb("wde", [P, 2, NT, E1])
        wdT = sb("wdT", [E1, S])
        h1 = carve(0, "mixture", [P, E1 * HC, S])
        moe = carve(1, "mixture", [P, NT, D])
        gdot = sb("gdot", [P, NT, 2])
        gate = sb("gate", [P, NT])
        outb = carve(1, "mixture", [P, NT, D])

        for e in (pe, dve, act, pool):
            e.after(e.now())
        with loops.clearing("batches", B, [pe, dve, act, pool]) as b:
            m_x = x_in.did(nc.sync.dma_start(x[:, :, :], a["x"][b].rearrange("(t p) d -> p t d", p=P)))
            for l in range(2):
                pool.did(G.tensor_copy(modc[l][:, :], modT[l][:, :, b]))
                pool.did(G.tensor_copy(modr[l][:, :, :], modB[l][:, b, :, :]))
            m_mod = pool.now()
            dve.after(m_x, m_mod)

            m = layernorm(x)
            m_hT = transposed(hT, xhat, m, modc[0][:, 1:2], modc[0][:, 0:1])
            pe.after(m_hT)
            for t in range(NT):
                m = pe.did(T.matmul(bank[1 + t % 4][:, 0:3 * D], hT[:, t * P:(t + 1) * P], proj_w[:, :], start=True, stop=True))
                dve.after(m)
                m_pv = dve.did(V.tensor_tensor(pv[:, t, :, :].rearrange("p o d -> p (o d)"), bank[1 + t % 4][:, 0:3 * D], proj_b[:, :], ALU.add))
            for o in range(ORDER):
                v = pv[:, :, o, :]
                dve.after(dve.now())
                dve.did(V.tensor_tensor(fold_s[:, 0, :, :], v[:, 0:2, :], v[:, 2:4, :], ALU.add))
                m = dve.did(V.tensor_tensor(fold_s[:, 1, :, :], v[:, 0:2, :], v[:, 2:4, :], ALU.subtract))
                pe.after(m)
                for c in range(4):
                    for kt in range(2):
                        last = T.matmul(bank[5][:, c * D:(c + 1) * D], c_fwd[:, kt, c * P:(c + 1) * P], fold_s[:, c % 2, kt, :],
                                        start=(kt == 0), stop=(kt == 1))
                m = pe.did(last)
                act.after(m)
                m = act.did(A.activation(spec[:, :, :, :].rearrange("p r c d -> p (r c d)"), bank[5][:, :], ACT.Copy))
                dve.after(m)
                re, im = spec[:, 0, :, :], spec[:, 1, :, :]
                fa, fb, fd = (filt[:, o, i, :, :] for i in range(3))
                dve.did(V.tensor_tensor(spec_o[:, 0, :, :], re, fa, ALU.mult))
                dve.did(V.tensor_tensor(spec_t[:, 0, :, :], im, fb, ALU.mult))
                dve.did(V.tensor_tensor(spec_o[:, 1, :, :], re, fb, ALU.mult))
                m = dve.did(V.tensor_tensor(spec_t[:, 1, :, :], im, fd, ALU.mult))
                dve.after(m)
                dve.did(V.tensor_tensor(spec_o[:, 0, :, :], spec_o[:, 0, :, :], spec_t[:, 0, :, :], ALU.subtract))
                m = dve.did(V.tensor_tensor(spec_o[:, 1, :, :], spec_o[:, 1, :, :], spec_t[:, 1, :, :], ALU.add))
                pe.after(m)
                for t in range(NT):
                    for c in range(4):
                        last = T.matmul(bank[6][:, t * D:(t + 1) * D], c_inv[:, c, t * P:(t + 1) * P], spec_o[:, c // 2, c % 2, :],
                                        start=(c == 0), stop=(c == 3))
                m = pe.did(last)
                dve.after(m)
                m = dve.did(V.tensor_tensor(pv[:, :, o + 1, :], bank[6][:, :].rearrange("p (t d) -> p t d", t=NT), pv[:, :, o + 1, :], ALU.mult))
            dve.after(m)
            dve.after(dve.did(V.tensor_tensor(attn[:, :, :], pv[:, :, ORDER, :], rows(modr[0][:, 0, :]), ALU.mult)))
            dve.after(dve.did(V.tensor_tensor(x[:, :, :], x[:, :, :], attn[:, :, :], ALU.add)))

            m = layernorm(x)
            m_hT = transposed(hT, xhat, m, modc[0][:, 4:5], modc[0][:, 3:4])
            pe.after(m_hT)
            for c in range(I_UP // P):
                m = pe.did(T.matmul(bank[1 + c][:, :], w_up[:, c * P:(c + 1) * P], hT[:, :], start=True, stop=True))
                act.after(m)
                m_gT = act.did(A.activation(gT[:, c, :], bank[1 + c][:, :], ACT.Silu))

            m_z, m_zp = [None] * NT, [None] * NT
            pe.after(m_gT)
            m_free = {5: m_hT, 6: m_hT, 1: m_gT, 2: m_gT, 3: m_gT, 4: m_gT}
            m_code_free = m_hT
            for t in range(NT):
                tok = slice(t * P, (t + 1) * P)
                pe.after(m_free[5], m_free[6])
                m_s = pe.did(T.matmul(bank[5][:, :], hT[:, tok], msim[:, :, :, :].rearrange("p a h k -> p (a h k)"), start=True, stop=True))
                m_g = pe.did(T.matmul(bank[6][:, :], hT[:, tok], downT[:, :], start=True, stop=True))
                act.after(m_s, dve.now())
                m_sim = act.did(A.activation(sim[:, :, :].rearrange("p g k -> p (g k)"), bank[5][:, :], ACT.Copy))
                act.after(m_g)
                m_gd = act.did(A.activation(gd[:, t, :], bank[6][:, :], ACT.Copy))
                m_free[5] = m_free[6] = m_gd
                dve.after(m_sim)
                for g in range(2 * PH):
                    dve.did(V.max(tops[:, g, :], sim[:, g, :]))
                dve.after(dve.now())
                for g in range(2 * PH):
                    dve.did(V.max_index(topi[:, g, :], tops[:, g, :], sim[:, g, :]))
                m_idx = dve.now()
                m = dve.did(V.tensor_tensor(pair[:, :, :, :], tops[:, 0:PH, :].unsqueeze(3).broadcast_to([P, PH, TOP, TOP]),
                                            tops[:, PH:, :].unsqueeze(2).broadcast_to([P, PH, TOP, TOP]), ALU.add))
                dve.after(m)
                dve.did(V.tensor_copy(topf[:, :, :], topi[:, :, :]))
                pflat = pair[:, :, :, :].rearrange("p h a b -> p h (a b)")
                for h in range(PH):
                    dve.did(V.max(best[:, h, :], pflat[:, h, :]))
                dve.after(dve.now())
                for h in range(PH):
                    dve.did(V.match_replace(pair_r[:, h, :], best[:, h, :], pflat[:, h, :], -3e38))
                m_nb = dve.did(V.tensor_scalar(negbest[:, :], best[:, :, 0], -1.0, None, ALU.mult))
                m_yv = dve.did(V.scalar_tensor_tensor(yval[:, :, :], topf[:, PH:, :], 32.0,
                                               small[:, 8:16].unsqueeze(1).broadcast_to([P, PH, TOP]), ALU.mult, ALU.add))
                dve.after(m_yv)
                chf = chosen[:, :, :, :].rearrange("p h a b -> p h (a b)")
                m_ch = dve.did(V.tensor_tensor(chf, pair_r[:, :, :], pflat, ALU.is_lt))
                dve.after(m_ch)
                m = dve.did(V.tensor_reduce(cnt[:, :, :], chosen[:, :, :, :], AX.X, ALU.add))
                for h in range(PH):
                    dve.did(V.tensor_tensor(eqx[:, h, :, :], topf[:, h, :].unsqueeze(1).broadcast_to([P, XROWS, TOP]),
                                            small[:, 0:XROWS].unsqueeze(2).broadcast_to([P, XROWS, TOP]), ALU.is_equal))
                dve.after(dve.now())
                m = dve.did(V.tensor_tensor(eqx[:, :, :, :], eqx[:, :, :, :],
                                            cnt[:, :, :].unsqueeze(2).broadcast_to([P, PH, XROWS, TOP]), ALU.mult))
                for h in range(PH):
                    pool.after(m_yv) if h == 0 else None
                    m_yd = pool.did(G.tensor_tensor(ydiff[:, h, :, :], yval[:, h, :].unsqueeze(1).broadcast_to([P, KEYS, TOP]),
                                                    small[:, 16:80].unsqueeze(2).broadcast_to([P, KEYS, TOP]), ALU.subtract))
                dve.after(m, m_code_free)
                with nc.allow_low_precision(reason="counts and ranks up to 8 are exact; what is larger stays above 8"):
                    dve.did(V.tensor_reduce(code[:, :, 0:XROWS], eqx[:, :, :, :], AX.X, ALU.add))
                    dve.after(m_yd)
                    m_code = dve.did(V.tensor_reduce(code[:, :, XROWS:], ydiff[:, :, :, :], AX.X, ALU.min, apply_absolute_value=True))
                act.after(m_nb)
                for h in range(PH):
                    m = act.did(A.activation(epair[:, h, :], pflat[:, h, :], ACT.Exp, bias=negbest[:, h:h + 1]))
                dve.after(m)
                dve.did(V.tensor_scalar(past[:, :, :], topf[:, 0:PH, :], float(XROWS), None, ALU.is_ge))
                dve.after(dve.did(V.tensor_tensor(epair[:, :, :], epair[:, :, :], chf, ALU.mult)))
                dve.after(dve.did(V.tensor_reduce(esum[:, :], epair[:, :, :], AX.X, ALU.add)))
                m = dve.did(V.reciprocal(rsum[:, t, :], esum[:, :]))
                m = dve.did(V.tensor_tensor(zpast[:, t, :, :].rearrange("p h (a b) -> p h a b", a=TOP),
                                        epair[:, :, :].rearrange("p h (a b) -> p h a b", a=TOP),
                                        past[:, :, :].unsqueeze(3).broadcast_to([P, PH, TOP, TOP]), ALU.mult))
                dve.after(m)
                m_zp[t] = dve.did(V.tensor_tensor(zpast[:, t, :, :], zpast[:, t, :, :],
                                                  rsum[:, t, :].unsqueeze(2).broadcast_to([P, PH, TOP * TOP]), ALU.mult))
                pe.after(m_code, m_gd)
                psT = bank[5][0:XROWS + KEYS, 0:PH * P // 2].bitcast(BF16).rearrange("q (h t) -> q h t", h=PH)
                for h in range(PH):
                    last = T.transpose(psT[:, h, :], code[:, h, :], identb[:, :])
                m = pe.did(last)
                m_code_free = m
                act.after(m)
                m_ct = act.did(A.activation(codeT[:, :, :], psT, ACT.Copy))
                m_free[5] = m_ct
                pe.after(m_ct)
                for h in range(PH):
                    bd, bl = 1 + h % 2, 3 + h % 2
                    pe.after(m_free[bd], m_free[bl])
                    m_l = pe.did(T.matmul(bank[bl][:, :], hT[:, tok], mpair[:, h, :, :].rearrange("p i j -> p (i j)"), start=True, stop=True))
                    m_d = pe.did(T.matmul(bank[bd][:, :], codeT[:, h, :], sel[:, :], start=True, stop=True))
                    act.after(m_l)
                    m_p = act.did(A.activation(prob[:, t, h, :], bank[bl][:, :], ACT.Exp, bias=negbest[:, h:h + 1]))
                    m_free[bl] = m_p
                    dve.after(m_p, m_d, m_gd)
                    m = dve.did(V.scalar_tensor_tensor(prob[:, t, h, :], bank[bd][:, :], 0.0, prob[:, t, h, :], ALU.is_ge, ALU.mult))
                    m_free[bd] = m
                    dve.after(m)
                    m_z[t] = dve.did(V.scalar_tensor_tensor(prob[:, t, h, :], prob[:, t, h, :], rsum[:, t, h:h + 1], gd[:, t, :], ALU.mult, ALU.mult))
            m_turned = []
            for t in range(NT):
                act.after(m_z[t], m_zp[t])
                m_w = act.did(A.activation(prob[:, t, :, :].rearrange("p h e -> p (h e)"), prob[:, t, :, :].rearrange("p h e -> p (h e)"), ACT.Silu))
                act.after(act.now())
                m_wp = act.did(A.activation(junk[:, :], zpast[:, t, :, :].rearrange("p h c -> p (h c)"), ACT.Silu,
                                            scale=gd[:, t, EXPERTS - 1:EXPERTS], accum_out=wpast[:, t:t + 1]))
                if t >= 2:
                    pool.after(m_turned[t - 2])
                pool.after(m_w)
                pool.after(pool.did(G.tensor_tensor(prob[:, t, 0:2, :], prob[:, t, 0:2, :], prob[:, t, 2:4, :], ALU.add)))
                pool.after(pool.did(G.tensor_tensor(wsum[:, t % 2, :], prob[:, t, 0, :], prob[:, t, 1, :], ALU.add)))
                pool.after(m_wp)
                m_ws = pool.did(G.tensor_tensor(wsum[:, t % 2, EXPERTS - 1:EXPERTS], wsum[:, t % 2, EXPERTS - 1:EXPERTS], wpast[:, t:t + 1], ALU.add))
                pe.after(m_ws, m_free[5] if t == 0 else m_wT)
                for c in range(4):
                    last = T.transpose(bank[5][:, c * P:(c + 1) * P], wsum[:, t % 2, c * P:(c + 1) * P], ident[:, :])
                m = pe.did(last)
                m_turned.append(m)
                dve.after(m)
                m_wT = dve.did(V.tensor_copy(wT[:, :, :], bank[5][:, :].rearrange("p (c t) -> p c t", c=4)))
                pe.after(m_wT)
                if t == 0:
                    pe.after(dve.now(), act.now())
                for c in range(4):
                    T.matmul(bank[7][:, t * D:(t + 1) * D], gT[:, c, t * P:(t + 1) * P], w_down[:, c, :], start=(c == 0), stop=False)
                for c in range(4):
                    last = T.matmul(bank[7][:, t * D:(t + 1) * D], wT[:, c, :], up_e[:, c, :], start=False, stop=(c == 3))
                m_o = pe.did(last)
                dve.after(m_o)
            m = dve.did(V.tensor_tensor(attn[:, :, :], bank[7][:, :].rearrange("p (t d) -> p t d", t=NT), rows(modr[0][:, 3, :]), ALU.mult))
            dve.after(m)
            dve.after(dve.did(V.tensor_tensor(x[:, :, :], x[:, :, :], attn[:, :, :], ALU.add)))

            m = layernorm(x)
            m_hT = transposed(hT, xhat, m, modc[1][:, 1:2], modc[1][:, 0:1])
            m_zero = dve.did(V.memset(attn[:, :, :], 0.0))
            S3, S02, S1, T0, T1, T2, BO, BM = bank
            s_of = [S02[:, 0:P], S1[:, 0:2 * P], S02[:, P:4 * P], S3[:, :]]
            p_at = [0, P, 3 * P, 6 * P]
            t_of = lambda kc, qc: [T0, T1, T2, T2][kc][:, (qc - kc) * P + (2 * P if kc == 3 else 0):][:, 0:P]
            pt_at = [0, 4 * P, 7 * P, 9 * P]

            st = {}

            def entry():
                e = {"pe": pe.now(), "dve": dve.now(), "act": act.now(), "pool": pool.now(), ("stage", 0): stage_in[0].now(), ("stage", 1): stage_in[1].now()}
                st.clear()
                st["entry"] = e
                return e

            def got(key, engine):
                return st.get(key) or st["entry"][engine]

            def stage_weights(par, h):
                s = stage_in[par]
                s.after(got(("proj", par), "pe"))
                s.did(nc.sync.dma_start(wq_s[par][:, :], a["Wq"][:, bass.ts(h, 2 * DH)]))
                st["staged", par] = s.did(nc.sync.dma_start(wk_s[par][:, :], a["Wk"][:, bass.ts(h, 2 * DH)]))

            def project(kind, par, h):
                pe.after(got("bm_free", "dve"), got("bm_free2", "act"))
                if kind == "v":
                    for t in range(NT):
                        last = T.matmul(BM[:, t * P:(t + 1) * P], hT[:, t * P:(t + 1) * P], wv[:, h, :], start=True, stop=True)
                    m = pe.did(last)
                    st["proj", par] = m
                    dve.after(m, got(("av", par), "pe"))
                    st["v", par] = st["bm_free"] = dve.did(V.tensor_tensor(
                        vv[par][:, :, :, :].rearrange("p t m c -> p t (m c)"), BM[:, :].rearrange("p (t c) -> p t c", t=NT),
                        lam_row[:, :, :].rearrange("p m c -> p (m c)").unsqueeze(1).broadcast_to([P, NT, 2 * DH]), ALU.mult))
                    return
                w, dst, k = (wq_s, qT, DH ** -0.5) if kind == "q" else (wk_s, kT, 1.0)
                pe.after(got(("staged", par), ("stage", par)))
                m = pe.did(T.matmul(BM[:, :], w[par][:, :], hT[:, :], start=True, stop=True))
                act.after(m, got(("scores", par), "pe"))
                st[kind, par] = st["bm_free2"] = act.did(A.activation(dst[par][:, :], BM[:, :], ACT.Copy, scale=k))

            def scores(u):
                par, mp, buf = u // 2 % 2, u % 2, u % 2
                r = slice(DH * mp, DH * mp + DH)
                pe.after(got(("q", par), "act"), got(("k", par), "act"))
                ready = [None] * NT
                order = (3, 1, 2, 0)
                for qc in order:
                    pe.after(got(("exp", 0 if qc == 2 else qc), "act"))
                    T.matmul(s_of[qc], qT[par][r, qc * P:(qc + 1) * P], kT[par][r, 0:(qc + 1) * P], start=True, stop=False)
                    ready[qc] = pe.did(T.matmul(s_of[qc][:, qc * P:(qc + 1) * P], identb[:, :], mask[:, :], start=False, stop=True))
                st["scores", par] = ready[0]
                ready[2] = ready[0]
                for qc in order:
                    dve.after(ready[qc], got(("exp", qc), "act"))
                    ready[qc] = dve.did(V.tensor_reduce(negmax[buf][:, qc:qc + 1], s_of[qc], AX.X, ALU.max, negate=True))
                ready[2] = ready[0]
                for qc in order:
                    act.after(ready[qc], got(("tr", buf), "pe"))
                    ready[qc] = act.did(A.activation(prb[buf][:, p_at[qc]:p_at[qc] + (qc + 1) * P], s_of[qc], ACT.Exp,
                                                     bias=negmax[buf][:, qc:qc + 1], accum_out=rowsum[buf][:, qc:qc + 1]))
                    st["exp", qc] = ready[qc]
                return ready

            def normalise(u, ready):
                buf = u % 2
                dve.after(*ready)
                dve.after(dve.did(V.reciprocal(rnorm[buf][:, :], rowsum[buf][:, :])), )
                m = dve.did(V.tensor_scalar(rnorm[buf][:, :], rnorm[buf][:, :], 1.0 - LAMBDA_INIT, None, ALU.mult))
                pool.after(m)
                for qc in range(NT):
                    v = prb[buf][:, p_at[qc]:p_at[qc] + (qc + 1) * P]
                    m = pool.did(G.tensor_tensor(v, v, rnorm[buf][:, qc:qc + 1].broadcast_to([P, (qc + 1) * P]), ALU.mult))
                st["norm", buf] = m

            def turn(u):
                buf = u % 2
                pe.after(got(("norm", buf), "pool"), got("pt_dve", "dve"), got("pt_act", "act"))
                m = [None] * NT
                for kc in range(NT):
                    for qc in range(kc, NT):
                        last = T.transpose(t_of(kc, qc), prb[buf][:, p_at[qc] + kc * P:p_at[qc] + (kc + 1) * P], ident[:, :])
                    m[kc] = pe.did(last)
                st["tr", buf] = m[3]
                dve.after(m[0], got(("pv", buf), "pe"))
                dve.did(V.tensor_copy(prbT[buf][:, 0:4 * P], T0[:, :]))
                dve.after(m[1])
                st["pt_dve"] = dve.did(V.tensor_copy(prbT[buf][:, 4 * P:7 * P], T1[:, 0:3 * P]))
                act.after(m[3], got(("pv", buf), "pe"))
                st["pt_act"] = act.did(A.activation(prbT[buf][:, 7 * P:10 * P], T2[:, 0:3 * P], ACT.Copy))

            def apply(u):
                par, mp, buf = u // 2 % 2, u % 2, u % 2
                pe.after(st["pt_dve"], st["pt_act"], got(("v", par), "dve"), got(("o", par), "act"))
                rows_o = slice(DH * par, DH * par + DH)
                for kc in range(NT):
                    last = T.matmul(BO[rows_o, kc * P:S], vv[par][:, kc, mp, :], prbT[buf][:, pt_at[kc]:pt_at[kc] + (NT - kc) * P],
                                    start=(kc == 0 and mp == 0), stop=(kc == NT - 1 and mp == 1))
                st["pv", buf] = m = pe.did(last)
                if mp == 1:
                    st["av", par] = m
                    act.after(m, got("wo", "pe"))
                    st["o", par] = act.did(A.activation(oT[rows_o, :], BO[rows_o, :], ACT.Copy))

            def project_out(g):
                pe.after(st["o", 0], st["o", 1], got("bm_free", "dve"), got("bm_free2", "act"))
                for t in range(NT):
                    last = T.matmul(BM[:, t * D:(t + 1) * D], oT[:, t * P:(t + 1) * P], wo[:, g, :], start=True, stop=True)
                st["wo"] = m = pe.did(last)
                dve.after(m)
                st["bm_free"] = dve.did(V.tensor_tensor(attn[:, :, :], attn[:, :, :], BM[:, :].rearrange("p (t d) -> p t d", t=NT), ALU.add))

            def pair_of_heads(g, last):
                entry()
                h = g * 2
                stage_weights(1, h + 1)
                e1 = scores(1)
                project("q", 1, h + 1)
                turn(0)
                normalise(1, e1)
                project("k", 1, h + 1)
                apply(0)
                project("v", 1, h + 1)
                if not last:
                    stage_weights(0, h + 2)
                e2 = scores(2)
                turn(1)
                normalise(2, e2)
                apply(1)
                e3 = scores(3)
                if not last:
                    project("q", 0, h + 2)
                turn(2)
                normalise(3, e3)
                if not last:
                    project("k", 0, h + 2)
                apply(2)
                if not last:
                    e4 = scores(4)
                turn(3)
                if not last:
                    normalise(4, e4)
                apply(3)
                if not last:
                    project("v", 0, h + 2)
                project_out(g)

            pe.after(m_hT)
            entry()
            stage_weights(0, 0)
            project("q", 0, 0)
            project("k", 0, 0)
            project("v", 0, 0)
            normalise(0, scores(0))
            with loops.loop("pairs", 0, PAIRS - 1) as g:
                pair_of_heads(g, False)
            pair_of_heads(PAIRS - 1, True)
            dve.after(dve.now())
            dve.after(dve.did(V.tensor_tensor(attn[:, :, :], attn[:, :, :], rows(modr[1][:, 0, :]), ALU.mult)))
            dve.after(dve.did(V.tensor_tensor(x[:, :, :], x[:, :, :], attn[:, :, :], ALU.add)))

            m = layernorm(x)
            dve.after(m)
            dve.after(dve.did(V.tensor_tensor(res[:, :, :], xhat[:, :, :], rows(modr[1][:, 2, :]), ALU.mult)))
            dve.after(dve.did(V.tensor_tensor(res[:, :, :], res[:, :, :], rows(modr[1][:, 1, :]), ALU.add)))
            m = layernorm(res)
            m_hT = transposed(hT, xhat, m, gammaT[:, 0:1], gammaT[:, 1:2])
            pe.after(m_hT, act.now())
            for t in range(NT):
                T.matmul(bank[1][:, t * D:(t + 1) * D], hT[:, t * P:(t + 1) * P], abel_w[:, :], start=True, stop=True)
            m_ab = pe.now()
            for t in range(NT):
                last = T.matmul(bank[2][:, t * E1:(t + 1) * E1], hT[:, t * P:(t + 1) * P], gate_w[:, :], start=True, stop=True)
            m_lg = pe.did(last)
            dve.after(m_lg)
            m = dve.did(V.tensor_tensor(abel[:, :, :], bank[1][:, :].rearrange("p (t d) -> p t d", t=NT), rows(abel_b[:, :]), ALU.add))
            act.after(m)
            m_abel = act.did(A.activation(abel[:, :, :], abel[:, :, :], ACT.Gelu))
            dve.after(dve.did(V.tensor_tensor(logit[:, :, :], bank[2][:, 0:NT * E1].rearrange("p (t e) -> p t e", t=NT),
                                              gate_b[:, :].unsqueeze(1).broadcast_to([P, NT, E1]), ALU.add)))
            for t in range(NT):
                dve.did(V.max(ltop[:, t, :], logit[:, t, :]))
            dve.after(dve.now())
            for t in range(NT):
                dve.did(V.max_index(lidx[:, t, :], ltop[:, t, :], logit[:, t, :]))
            dve.did(V.tensor_tensor(lw[:, :, 1], ltop[:, :, 1], ltop[:, :, 0], ALU.subtract))
            dve.after(dve.now())
            m = dve.did(V.tensor_copy(lidf[:, :, :], lidx[:, :, 0:2]))
            act.after(m)
            m = act.did(A.activation(lw[:, :, 1], lw[:, :, 1], ACT.Exp))
            for j in range(E1 * HC):
                bk = bank[3 + j % 4]
                if j >= 4:
                    pe.after(m_h1[j - 4])
                else:
                    m_h1 = [] if j == 0 else m_h1
                mm = pe.did(T.matmul(bk[:, :], ew1[:, j // HC, (j % HC) * P:(j % HC + 1) * P], hT[:, :], start=True, stop=True))
                act.after(mm)
                m_h1.append(act.did(A.activation(h1[:, j, :], bk[:, :], ACT.Gelu, bias=eb1T[:, j:j + 1])))
            dve.after(m)
            dve.after(dve.did(V.tensor_scalar(lw[:, :, 0], lw[:, :, 1], 1.0, None, ALU.add)))
            dve.after(dve.did(V.reciprocal(lw[:, :, 0], lw[:, :, 0])))
            dve.after(dve.did(V.tensor_tensor(lw[:, :, 1], lw[:, :, 1], lw[:, :, 0], ALU.mult)))
            for k in range(K1):
                dve.after(dve.did(V.tensor_tensor(wde[:, k, :, :], lidf[:, :, k].unsqueeze(2).broadcast_to([P, NT, E1]),
                                                  small[:, 134:142].unsqueeze(1).broadcast_to([P, NT, E1]), ALU.is_equal)))
                dve.after(dve.did(V.tensor_tensor(wde[:, k, :, :], wde[:, k, :, :],
                                                  lw[:, :, k].unsqueeze(2).broadcast_to([P, NT, E1]), ALU.mult)))
            m = dve.did(V.tensor_tensor(wde[:, 0, :, :], wde[:, 0, :, :], wde[:, 1, :, :], ALU.add))
            pe.after(m)
            for t in range(NT):
                last = T.transpose(bank[2][0:E1, t * P:(t + 1) * P], wde[:, 0, t, :], ident[:, :])
            m = pe.did(last)
            dve.after(m)
            m_wdT = dve.did(V.tensor_copy(wdT[:, :], bank[2][0:E1, :]))
            pe.after(m_wdT, *m_h1[-4:])
            for t in range(NT):
                m_b = pe.did(T.matmul(bank[7][:, t * D:(t + 1) * D], wdT[:, t * P:(t + 1) * P], eb2R[:, :], start=True, stop=True))
            dve.after(m_b)
            m_bias = dve.did(V.tensor_copy(moe[:, :, :], bank[7][:, :].rearrange("p (t d) -> p t d", t=NT)))
            dve.after(m_bias)
            m_free_b = [m_wdT] * 2
            for t in range(NT):
                tok = slice(t * P, (t + 1) * P)
                pe.after(m_free_b[t % 2])
                bks = (3, 4) if t % 2 == 0 else (5, 6)
                for e in range(E1):
                    for c in range(HC):
                        last = T.matmul(bank[bks[e // 4]][:, (e % 4) * D:(e % 4 + 1) * D], h1[:, e * HC + c, tok], ew2R[:, e, c, :],
                                        start=(c == 0), stop=(c == HC - 1))
                m_e = pe.did(last)
                dve.after(m_e)
                for e in range(E1):
                    m = dve.did(V.scalar_tensor_tensor(moe[:, t, :], bank[bks[e // 4]][:, (e % 4) * D:(e % 4 + 1) * D],
                                                       wde[:, 0, t, e:e + 1], moe[:, t, :], ALU.mult, ALU.add))
                    dve.after(m)
                m_free_b[t % 2] = m
            dve.after(m_abel)
            prod = xhat
            for k, src in enumerate((abel, moe)):
                dve.after(dve.did(V.tensor_tensor(prod[:, :, :], src[:, :, :], rows(gc_w[:, k * D:(k + 1) * D]), ALU.mult)))
                dve.after(dve.did(V.tensor_reduce(gdot[:, :, k], prod[:, :, :], AX.X, ALU.add)))
            m = dve.did(V.tensor_scalar(gate[:, :], gdot[:, :, 0], gc_b[:, 0:1], None, ALU.add))
            dve.after(m)
            m = dve.did(V.tensor_tensor(gate[:, :], gate[:, :], gdot[:, :, 1], ALU.add))
            act.after(m)
            m = act.did(A.activation(gate[:, :], gate[:, :], ACT.Tanh, scale=0.5))
            dve.after(m)
            dve.after(dve.did(V.tensor_scalar(gate[:, :], gate[:, :], 1.0, 0.5, ALU.add, ALU.mult)))
            dve.after(dve.did(V.tensor_tensor(moe[:, :, :], moe[:, :, :], abel[:, :, :], ALU.subtract)))
            dve.after(dve.did(V.tensor_tensor(moe[:, :, :], moe[:, :, :], gate[:, :].unsqueeze(2).broadcast_to([P, NT, D]), ALU.mult)))
            dve.after(dve.did(V.tensor_tensor(moe[:, :, :], moe[:, :, :], abel[:, :, :], ALU.add)))
            dve.after(dve.did(V.tensor_tensor(moe[:, :, :], moe[:, :, :], res[:, :, :], ALU.add)))
            dve.after(dve.did(V.tensor_tensor(moe[:, :, :], moe[:, :, :], rows(modr[1][:, 3, :]), ALU.mult)))
            dve.after(out_stored.now())
            m = dve.did(V.tensor_tensor(outb[:, :, :], moe[:, :, :], x[:, :, :], ALU.add))
            out_stored.after(m)
            out_stored.did(nc.sync.dma_start(out[b].rearrange("(t p) d -> p t d", p=P), outb[:, :, :]))
            for e in (pe, dve, act, pool):
                e.after(e.now())
        out_stored.after(out_stored.now())
        return loops.seen


_INS = {}


def _layout(i):
    c = np.ascontiguousarray
    head_major = lambda w: c(w.reshape(D, 2, H1, DH).transpose(0, 2, 1, 3).reshape(D, 2 * H1 * DH))
    g = i["L1_ffn_gens"]
    return {
        "x": i["L0_attn_x"], "cT0": c(i["L0_c"].T), "cT1": c(i["L1_c"].T), "wmod0": i["L0_wmod"], "wmod1": i["L1_wmod"],
        "proj_w": i["L0_attn_proj_w"], "proj_b": i["L0_attn_proj_b"].reshape(1, -1),
        "filter": i["L0_attn_filter_time"].reshape(ORDER, TAPS, D),
        "W_upT": c(i["L0_ffn_W_up"].T), "W_downT": c(i["L0_ffn_W_down"].T), "W_q": i["L0_ffn_W_q"],
        "keysT": c(i["L0_ffn_keys"].transpose(2, 0, 3, 1).reshape(2 * PH * PN, KEYS)),
        "downT": c(i["L0_ffn_down_embed"].T), "up_embed": i["L0_ffn_up_embed"],
        "Wq": head_major(i["L1_attn_Wq"]), "Wk": head_major(i["L1_attn_Wk"]), "Wv": head_major(i["L1_attn_Wv"]),
        "Wo": i["L1_attn_Wo"],
        "lam": c(np.stack([i["L1_attn_lq1"], i["L1_attn_lk1"], i["L1_attn_lq2"], i["L1_attn_lk2"]])),
        "gammabetaT": c(np.stack([i["L1_ffn_ln_gamma"], i["L1_ffn_ln_beta"]], axis=1)),
        "abel_w": i["L1_ffn_abel_w"], "abel_b": i["L1_ffn_abel_b"].reshape(1, -1),
        "gate_w": i["L1_ffn_moe_gate_w"], "gate_b": i["L1_ffn_moe_gate_b"].reshape(1, -1),
        "ew1": i["L1_ffn_ew1"], "eb1T": c(i["L1_ffn_eb1"].reshape(E1 * HC, P).T),
        "ew2T": c(i["L1_ffn_ew2"].transpose(0, 2, 1)), "eb2T": c(i["L1_ffn_eb2"].T),
        "gens2": c(np.stack([g, g.transpose(0, 2, 1)], axis=1)),
        "gc_w": i["L1_ffn_gc_w"].reshape(1, -1), "gc_b": i["L1_ffn_gc_b"].reshape(1, 1),
    }


def kernel(**inputs):
    import concourse.bacc as bacc
    from concourse.bass_utils import run_bass_kernel_spmd

    arrays = {f"in_{k}": np.ascontiguousarray(v) for k, v in
              {**_layout({k: np.asarray(v) for k, v in inputs.items()}), **host_constants()}.items()}

    def program(per):
        nc = bacc.Bacc("TRN2", target_bir_lowering=False, num_devices=1)
        aps = {name[3:]: nc.dram_tensor(name, v.shape, mybir.dt.from_np(v.dtype), kind="ExternalInput").ap()
               for name, v in arrays.items()}
        out = nc.dram_tensor("out_0", (B, S, D), F32, kind="ExternalOutput").ap()
        return nc, build(nc, per, aps, out)

    _, per = program({})
    nc, _ = program(per)
    r = run_bass_kernel_spmd(nc, [arrays], core_ids=[0])
    return r.results[0]["out_0"]
```

```python
from contextlib import ExitStack, contextmanager

import numpy as np

import concourse.bass as bass
from concourse import mybir
from concourse.alu_op_type import AluOpType as ALU

F32 = mybir.dt.float32
BF16 = mybir.dt.bfloat16
U32 = mybir.dt.uint32
ACT = mybir.ActivationFunctionType
AX = mybir.AxisListType
MAX_REDUCE = bass.bass_isa.ReduceOp.max

P = 128
B, S, D = 4, 512, 128
NT = S // P
TAPS = 256
ORDER = 2
I_UP = 512
PH, KEYS, TOP, PN = 4, 64, 8, 64
EXPERTS = 512
XROWS = EXPERTS // KEYS
H1, DH = 16, 64
PAIRS = H1 // 2
LAMBDA_INIT = 0.8
E1, HID1, K1 = 8, 256, 2
HC = HID1 // P
NROT = 3
EPS = 1e-5
MAX_SQUARINGS = 16
EXPM_THETA = 0.5
TAYLOR = [1.0, 1.0, 1 / 2, 1 / 6, 1 / 24, 1 / 120, 1 / 720, 1 / 5040, 1 / 40320]
CAUSAL_FILL = -1e30
PACE = 0.75


class Mark:

    def __init__(self, sem, base, n):
        self.sem, self.value = sem, base + n


class Progress:

    def __init__(self, name, sem, engine, step=1):
        self.name, self.sem, self.engine, self.step = name, sem, engine, step
        self.base, self.n = 0, 0

    def did(self, instruction):
        instruction.then_inc(self.sem, self.step)
        self.n += self.step
        return self.now()

    def now(self):
        return Mark(self.sem, self.base, self.n)

    def after(self, *marks):
        for m in marks:
            self.engine.wait_ge(m.sem, m.value)


class Loops:

    def __init__(self, nc, progresses, per):
        self.nc, self.progresses, self.per, self.seen = nc, progresses, per, {}

    @contextmanager
    def clearing(self, name, end, cleared):
        sems = [p.sem for p in cleared]
        first = min(s.num for s in sems)
        assert sorted(s.num for s in sems) == list(range(first, first + len(sems)))
        clear = range(first, first + len(sems))
        self.nc.all_engine_barrier(sems_to_clear=clear)
        for p in cleared:
            p.n = 0
        with self.loop(name, 0, end) as i:
            yield i
            self.nc.all_engine_barrier(sems_to_clear=clear)
            for p in cleared:
                p.n = 0
        for p in cleared:
            p.n = 0

    @contextmanager
    def loop(self, name, start, end):
        before = [(p.base, p.n) for p in self.progresses]
        turn = self.per.get(name, [0] * len(before))
        with self.nc.Fori(start, end) as i:
            for p, k in zip(self.progresses, turn):
                if k:
                    p.base = p.base + (i - start) * k if start else p.base + i * k
            yield i
        self.seen[name] = [p.n - n for p, (_, n) in zip(self.progresses, before)]
        for p, (base, n), k in zip(self.progresses, before, self.seen[name]):
            p.base, p.n = base, n + (end - start) * k


def host_constants():
    n = 2 * TAPS
    k = np.concatenate([np.arange(0, TAPS, 2), np.arange(1, TAPS, 2)])
    t = np.arange(n)
    ang = 2 * np.pi * ((k[:, None] * t[None, :]) % n) / n
    cos, sin = np.cos(ang), np.sin(ang)
    alt = np.where(t % 2 == 0, 1.0, -1.0)
    imag = -sin
    imag[0] = alt
    fwd = np.concatenate([cos, imag])
    inv_r, inv_i = 2 * cos / n, -2 * sin / n
    inv_r[0], inv_i[0] = 1 / n, alt / n
    inv = np.concatenate([inv_r, inv_i])
    fd = cos.copy()
    fd[0] = alt
    filt = np.stack([cos, -sin, fd])[:, :, :TAPS]
    f = np.float32
    fwd_half = fwd[:, :TAPS]
    sel = np.zeros((XROWS + KEYS, XROWS, KEYS))
    for i in range(XROWS):
        sel[i, i, :] = 1
    for j in range(KEYS):
        sel[XROWS + j, :, j] = -1
    small = np.zeros((1, 256))
    small[0, 0:TOP] = np.arange(TOP)
    small[0, 8:16] = np.arange(TOP) + 1
    small[0, 16:80] = 32.0 * np.arange(KEYS)
    small[0, 80:96] = EXPM_THETA * 2.0 ** np.arange(MAX_SQUARINGS)
    small[0, 96:113] = 2.0 ** -np.arange(MAX_SQUARINGS + 1)
    small[0, 113:130] = np.arange(MAX_SQUARINGS + 1)
    small[0, 130:134] = -0.5
    small[0, 134:142] = np.arange(E1)
    q = np.arange(P)
    return {
        "c_fwd": fwd_half.T.astype(f),
        "c_inv": inv.astype(f),
        "c_filt": filt.transpose(0, 2, 1).astype(f).copy(),
        "c_ident": np.eye(P, dtype=f),
        "c_mask": np.where(q[None, :] > q[:, None], CAUSAL_FILL, 0.0).astype(f),
        "c_sel": sel.reshape(XROWS + KEYS, EXPERTS).astype(f),
        "c_small": small.astype(f),
    }


def build(nc, per, a, out):
    es = ExitStack()
    with es:
        def sb(name, shape, dt=F32):
            return es.enter_context(nc.sbuf_tensor(name, shape, dt))

        def progress(name, engine, step=1):
            return Progress(name, es.enter_context(nc.semaphore(name)), engine, step)

        bank = [es.enter_context(nc.psum_tensor(f"bank{i}", [P, 512], F32)) for i in range(8)]

        pe = progress("pe_done", nc.tensor)
        dve = progress("dve_done", nc.vector)
        act = progress("act_done", nc.scalar)
        pool = progress("pool_done", nc.gpsimd)
        weights_in = progress("weights_in", nc.sync, 16)
        x_in = progress("x_in", nc.sync, 16)
        out_stored = progress("out_stored", nc.sync, 16)
        V, A, T, G = nc.vector, nc.scalar, nc.tensor, nc.gpsimd
        loops = Loops(nc, [pe, dve, act, pool, x_in, out_stored], per)

        ARENA = (8192, 8192)
        arena = [sb(f"arena{i}", [P, words]) for i, words in enumerate(ARENA)]
        carved = {}

        def carve(i, phase, shape):
            words = int(np.prod(shape[1:]))
            at = carved.get((i, phase), 0)
            carved[i, phase] = at + words
            assert at + words <= ARENA[i], (i, phase)
            names = "abcd"[:len(shape) - 1]
            v = arena[i][:, at:at + words]
            if len(shape) == 2:
                return v
            return v.rearrange(f"p ({' '.join(names)}) -> p {' '.join(names)}", **dict(zip(names, shape[1:])))

        def load(name, shape, src, place=None):
            tile = sb(name, shape) if place is None else place
            weights_in.did(nc.sync.dma_start(tile[tuple(slice(None) for _ in shape)], src))
            return tile

        small = load("small", [P, 256], a["c_small"][0:1, :].broadcast_to([P, 256]))
        ident = load("ident", [P, P], a["c_ident"])
        cT = [load(f"cT{l}", [P, B], a[f"cT{l}"]) for l in range(2)]
        wmod = [load(f"wmod{l}", [P, 6 * D], a[f"wmod{l}"], carve(1, "setup", [P, 6 * D])) for l in range(2)]
        proj_w = load("proj_w", [P, (ORDER + 1) * D], a["proj_w"])
        proj_b = load("proj_b", [P, (ORDER + 1) * D], a["proj_b"][0:1, :].broadcast_to([P, 3 * D]))
        taps = load("taps", [P, ORDER, TAPS // P, D], a["filter"].rearrange("o (c p) d -> p o c d", p=P), carve(1, "setup", [P, ORDER, TAPS // P, D]))
        c_filt = load("c_filt_sb", [P, 3, TAPS // P, TAPS], a["c_filt"].rearrange("m (c p) r -> p m c r", p=P), carve(0, "setup", [P, 3, TAPS // P, TAPS]))
        c_fwd = load("c_fwd_sb", [P, TAPS // P, S], a["c_fwd"].rearrange("(c p) r -> p c r", p=P))
        c_inv = load("c_inv_sb", [P, S // P, S], a["c_inv"].rearrange("(c p) t -> p c t", p=P))
        w_up = load("w_up", [P, I_UP], a["W_upT"])
        w_down = load("w_down", [P, I_UP // P, D], a["W_downT"].rearrange("(c p) d -> p c d", p=P))
        w_q = load("w_q", [P, 4, D], a["W_q"].rearrange("(c p) d -> p c d", p=P), carve(1, "setup", [P, 4, D]))
        keysT = load("keysT", [P, 4, KEYS], a["keysT"].rearrange("(c p) k -> p c k", p=P), carve(1, "setup", [P, 4, KEYS]))
        downT = load("downT", [P, EXPERTS], a["downT"])
        up_e = load("up_e", [P, EXPERTS // P, D], a["up_embed"].rearrange("(c p) d -> p c d", p=P))
        wq = load("wq", [P, H1, 2 * DH], a["Wq"].rearrange("d (h c) -> d h c", h=H1))
        wk = load("wk", [P, H1, 2 * DH], a["Wk"].rearrange("d (h c) -> d h c", h=H1))
        wv = load("wv", [P, H1, 2 * DH], a["Wv"].rearrange("d (h c) -> d h c", h=H1))
        wo = load("wo", [P, PAIRS, D], a["Wo"].rearrange("(g p) d -> p g d", p=P))
        lam_in = load("lam_in", [P, 4, DH], a["lam"].rearrange("(o q) c -> o q c", o=1).broadcast_to([P, 4, DH]), carve(1, "setup", [P, 4, DH]))
        gammaT = load("gammaT", [P, 2], a["gammabetaT"])
        abel_w = load("abel_w", [P, D], a["abel_w"])
        abel_b = load("abel_b", [P, D], a["abel_b"][0:1, :].broadcast_to([P, D]))
        gate_w = load("gate_w", [P, E1], a["gate_w"])
        gate_b = load("gate_b", [P, E1], a["gate_b"][0:1, :].broadcast_to([P, E1]))
        ew1 = load("ew1", [P, E1, HID1], a["ew1"].rearrange("e d h -> d e h"))
        eb1T = load("eb1T", [P, E1 * HC], a["eb1T"])
        ew2T = load("ew2T", [P, E1, HID1], a["ew2T"].rearrange("e m k -> m e k"), carve(0, "setup", [P, E1, HID1]))
        eb2T = load("eb2T", [P, E1], a["eb2T"])
        gens = load("gens_sb", [P, NROT, 2, D], a["gens2"].rearrange("i t p d -> p i t d"), carve(0, "setup", [P, NROT, 2, D]))
        gc_w = load("gc_w", [P, 2 * D], a["gc_w"][0:1, :].broadcast_to([P, 2 * D]))
        gc_b = load("gc_b", [P, 1], a["gc_b"][0:1, :].broadcast_to([P, 1]))
        maskf = load("maskf", [P, P], a["c_mask"], carve(1, "setup", [P, P]))
        self_ = load("self", [XROWS + KEYS, EXPERTS], a["c_sel"], carve(1, "setup", [P, EXPERTS])[0:XROWS + KEYS, :])
        weights = weights_in.now()

        identb = sb("identb", [P, P], BF16)
        mask = sb("mask", [P, P], BF16)
        sel = sb("sel", [XROWS + KEYS, EXPERTS], BF16)
        silT = sb("silT", [P, 2, B])
        silB = carve(1, "setup", [P, 2, B, P])
        modT = [sb(f"modT{l}", [P, 6, B]) for l in range(2)]
        modB = [sb(f"modB{l}", [P, B, 4, D]) for l in range(2)]
        signs = carve(1, "setup", [P, 2, B, D])
        gate_neg = carve(1, "setup", [P, 2, B, D])
        filt = sb("filt", [P, ORDER, 3, 2, D])
        msim = sb("msim", [P, 2, PH, KEYS])
        mpair = sb("mpair", [P, PH, XROWS, KEYS])
        lam_p = sb("lam_p", [P, 2, DH])
        lam_s = sb("lam_s", [P, 2])
        lam_row = sb("lam_row", [P, 2, DH])
        ew2R = sb("ew2R", [P, E1, HC, D])
        eb2R = sb("eb2R", [E1, D])

        for e in (pe, dve, act, pool):
            e.after(weights)
        A.preload_act_table_set("silu_and_others") if False else None
        m_sil = [act.did(A.activation(silT[:, l, :], cT[l][:, :], ACT.Silu)) for l in range(2)]
        dve.did(V.tensor_copy(identb[:, :], ident[:, :]))
        dve.did(V.tensor_copy(mask[:, :], maskf[:, :]))
        dve.did(V.tensor_copy(sel[:, :], self_[:, :]))
        dve.after(m_sil[1])
        m_silB = dve.did(V.tensor_copy(silB[:, :, :, :].rearrange("p l b q -> p (l b) q"),
                                       silT[:, :, :].rearrange("p l b -> p (l b)").unsqueeze(2).broadcast_to([P, 2 * B, P])))
        pe.after(m_sil[1], m_silB)
        for l in range(2):
            for s in range(6):
                T.matmul(bank[0][:, (l * 6 + s) * B:(l * 6 + s + 1) * B], wmod[l][:, s * D:(s + 1) * D],
                         silT[:, l, :], start=True, stop=True)
        m_bc = []
        for l in range(2):
            for b in range(B):
                m_bc.append(pe.did(T.matmul(bank[1 + (l * B + b) % 4][:, :], silB[:, l, b, :], wmod[l][:, 2 * D:6 * D],
                                            start=True, stop=True)))
                if l == 0 and b == B - 1:
                    m_first = [None] * B
                    for bb in range(B):
                        dve.after(m_bc[bb])
                        m_first[bb] = dve.did(V.tensor_copy(modB[0][:, bb, :, :], bank[1 + bb][:, :].rearrange("p (s d) -> p s d", s=4)))
                    pe.after(m_first[B - 1])
        for bb in range(B):
            dve.after(m_bc[B + bb])
            dve.did(V.tensor_copy(modB[1][:, bb, :, :], bank[1 + bb][:, :].rearrange("p (s d) -> p s d", s=4)))
        for l in range(2):
            m_t = dve.did(V.tensor_copy(modT[l][:, :, :], bank[0][:, l * 6 * B:(l + 1) * 6 * B].rearrange("p (s b) -> p s b", s=6)))
        dve.after(m_t)
        for l in range(2):
            for s in (1, 4):
                dve.did(V.tensor_scalar(modT[l][:, s, :], modT[l][:, s, :], 1.0, None, ALU.add))
        dve.did(V.tensor_scalar(modB[1][:, :, 2, :], modB[1][:, :, 2, :], 1.0, None, ALU.add))
        for l in range(2):
            for k, s in enumerate((0, 3)):
                g = modB[l][:, :, s, :]
                m = dve.did(V.tensor_scalar(signs[:, k, :, :], g, 0.0, 2.0, ALU.is_ge, ALU.mult))
                neg = gate_neg[:, k, :, :]
                dve.after(dve.did(V.tensor_scalar(neg, g, -1.0, 0.25, ALU.mult, ALU.max)))
                m = dve.did(V.tensor_tensor(g, g, neg, ALU.max))
                dve.after(m)
                m = dve.did(V.scalar_tensor_tensor(g, signs[:, k, :, :], -1.0, g, ALU.add, ALU.mult))
                dve.after(m)

        dve.after(dve.did(V.tensor_tensor(lam_p[:, :, :], lam_in[:, 0::2, :], lam_in[:, 1::2, :], ALU.mult)))
        m = dve.did(V.tensor_reduce(lam_s[:, :], lam_p[:, :, :], AX.X, ALU.add))
        act.after(m)
        m = act.did(A.activation(lam_s[:, :], lam_s[:, :], ACT.Exp))
        dve.after(m)
        m = dve.did(V.tensor_tensor(lam_s[:, 0:1], lam_s[:, 1:2], lam_s[:, 0:1], ALU.subtract))
        dve.did(V.memset(lam_row[:, 0, :], 1.0))
        dve.did(V.memset(lam_row[:, 1, :], -LAMBDA_INIT))
        dve.after(dve.now())
        dve.did(V.tensor_scalar(lam_row[:, 1, :], lam_row[:, 1, :], lam_s[:, 0:1], None, ALU.add))

        for o in range(ORDER):
            for f in range(3):
                for c in range(2):
                    for kt in range(TAPS // P):
                        last = T.matmul(bank[5 + o][:, ((f * 2 + c) % 4) * D:((f * 2 + c) % 4 + 1) * D] if f < 2 else
                                        bank[7][:, (o * 2 + c) * D:(o * 2 + c + 1) * D],
                                        c_filt[:, f, kt, c * P:(c + 1) * P], taps[:, o, kt, :],
                                        start=(kt == 0), stop=(kt == TAPS // P - 1))
        m = pe.did(last)
        dve.after(m)
        for o in range(ORDER):
            dve.did(V.tensor_copy(filt[:, o, 0:2, :, :], bank[5 + o][:, :].rearrange("p (f c d) -> p f c d", f=2, c=2)))
            dve.did(V.tensor_copy(filt[:, o, 2, :, :], bank[7][:, o * 2 * D:(o + 1) * 2 * D].rearrange("p (c d) -> p c d", c=2)))
        m_filt = dve.now()

        pe.after(m_filt)
        for ph in range(2):
            for h in range(PH):
                r = slice(PN * (h % 2), PN * (h % 2) + PN)
                c = ph * 2 + h // 2
                last = T.matmul(bank[5 + h % 2][:, (ph * PH + h) // 2 * KEYS:((ph * PH + h) // 2 + 1) * KEYS],
                                w_q[r, c, :], keysT[r, c, :], start=True, stop=True)
        m = pe.did(last)
        dve.after(m)
        for h2 in range(2):
            dve.did(V.tensor_copy(msim[:, :, h2::2, :].rearrange("p a h k -> p (a h) k") if False else
                                  msim[:, 0, h2::2, :], bank[5 + h2][:, 0:2 * KEYS].rearrange("p (h k) -> p h k", h=2)))
            dve.did(V.tensor_copy(msim[:, 1, h2::2, :], bank[5 + h2][:, 2 * KEYS:4 * KEYS].rearrange("p (h k) -> p h k", h=2)))
        dve.after(dve.now())
        for h in range(PH):
            dve.did(V.tensor_tensor(mpair[:, h, :, :],
                                    msim[:, 0, h, 0:XROWS].unsqueeze(2).broadcast_to([P, XROWS, KEYS]),
                                    msim[:, 1, h, :].unsqueeze(1).broadcast_to([P, XROWS, KEYS]), ALU.add))

        NG2 = NROT * 2
        xb = carve(0, "setup", [P, NROT, 2, D])
        xb2 = carve(0, "setup", [P, NROT, 2, D])
        xb3 = carve(0, "setup", [P, NROT, 2, D])
        xp = carve(0, "setup", [P, NROT, 2, D])
        xe = carve(0, "setup", [P, NROT, 2, D])
        norm = sb("xm_norm", [P, NROT])
        over = sb("xm_over", [P, MAX_SQUARINGS, NROT])
        steps = sb("xm_steps", [P, NROT])
        onehot = sb("xm_onehot", [P, NROT, MAX_SQUARINGS + 1])
        scale = sb("xm_scale", [P, NROT])
        m = dve.did(V.tensor_reduce(norm[:, :], gens[:, :, 0, :], AX.X, ALU.add, apply_absolute_value=True))
        pool.after(m)
        normall = sb("xm_normall", [P, NROT])
        m = pool.did(G.partition_all_reduce(normall[:, :], norm[:, :], P, MAX_REDUCE))
        dve.after(m)
        dve.after(dve.did(V.tensor_tensor(over[:, :, :], normall[:, :].unsqueeze(1).broadcast_to([P, MAX_SQUARINGS, NROT]),
                                          small[:, 80:96].unsqueeze(2).broadcast_to([P, MAX_SQUARINGS, NROT]), ALU.is_gt)))
        dve.after(dve.did(V.tensor_reduce(steps[:, :], over[:, :, :].rearrange("p k g -> p g k"), AX.X, ALU.add)))
        dve.after(dve.did(V.tensor_tensor(onehot[:, :, :], steps[:, :].unsqueeze(2).broadcast_to([P, NROT, MAX_SQUARINGS + 1]),
                                          small[:, 113:130].unsqueeze(1).broadcast_to([P, NROT, MAX_SQUARINGS + 1]), ALU.is_equal)))
        dve.after(dve.did(V.tensor_tensor(onehot[:, :, :], onehot[:, :, :],
                                          small[:, 96:113].unsqueeze(1).broadcast_to([P, NROT, MAX_SQUARINGS + 1]), ALU.mult)))
        dve.after(dve.did(V.tensor_reduce(scale[:, :], onehot[:, :, :], AX.X, ALU.add)))
        for i in range(NROT):
            dve.did(V.tensor_scalar(xb[:, i, :, :], gens[:, i, :, :], scale[:, i:i + 1], None, ALU.mult))
        m = dve.now()

        def products(left, right, ready, into=(0, 1)):
            pe.after(ready)
            for side in range(2):
                for i in range(NROT):
                    last = T.matmul(bank[into[side]][:, i * D:(i + 1) * D], left[:, i, 1 - side, :], right[:, i, side, :],
                                    start=True, stop=True)
            return pe.did(last)

        def psum_of(side, into=(0, 1)):
            return bank[into[side]][:, 0:NROT * D].rearrange("p (i d) -> p i d", i=NROT)

        done = products(xb, xb, m)
        dve.after(done)
        for side in range(2):
            dve.did(V.tensor_copy(xb2[:, :, side, :], psum_of(side)))
        done = products(xb2, xb, dve.now())
        dve.after(done)
        for side in range(2):
            dve.did(V.tensor_copy(xb3[:, :, side, :], psum_of(side)))
        dve.after(dve.now())

        def poly(dst, c0, c1, c2):
            flat = lambda t: t[:, :, :, :].rearrange("p i s d -> p (i s) d")
            m1 = dve.did(V.tensor_scalar(flat(dst), flat(xb), c1, None, ALU.mult))
            dve.after(m1)
            m2 = dve.did(V.scalar_tensor_tensor(flat(dst), flat(xb2), c2, flat(dst), ALU.mult, ALU.add))
            dve.after(m2)
            for j in range(NG2):
                v = flat(dst)[:, j, :]
                m3 = dve.did(V.scalar_tensor_tensor(v, ident[:, :], c0, v, ALU.mult, ALU.add))
            return m3

        m = poly(xp, *TAYLOR[6:9])
        done = products(xb3, xp, m)
        m = poly(xe, *TAYLOR[3:6])
        dve.after(m, done)
        for side in range(2):
            dve.did(V.tensor_tensor(xe[:, :, side, :], xe[:, :, side, :], psum_of(side), ALU.add))
        m = dve.now()
        done = products(xb3, xe, m)
        dve.after(done)
        m = poly(xp, *TAYLOR[0:3])
        dve.after(m)
        for side in range(2):
            dve.did(V.tensor_tensor(xe[:, :, side, :], xp[:, :, side, :], psum_of(side), ALU.add))

        pe.after(dve.now())
        keep = sb("xm_keep", [P, MAX_SQUARINGS, NROT])
        dve.did(V.tensor_scalar(keep[:, :, :], over[:, :, :], -1.0, 1.0, ALU.mult, ALU.add))
        dve.after(dve.now())
        with loops.loop("squarings", 0, MAX_SQUARINGS) as k:
            done = products(xe, xe, dve.now())
            dve.after(done)
            for side in range(2):
                dve.did(V.tensor_tensor(xp[:, :, side, :], psum_of(side), over[:, k, :].unsqueeze(2).broadcast_to([P, NROT, D]), ALU.mult))
                dve.did(V.tensor_tensor(xe[:, :, side, :], xe[:, :, side, :], keep[:, k, :].unsqueeze(2).broadcast_to([P, NROT, D]), ALU.mult))
            dve.after(dve.now())
            dve.did(V.tensor_tensor(xe[:, :, :, :], xe[:, :, :, :], xp[:, :, :, :], ALU.add))
        rot = sb("rot", [P, D])
        rotT = sb("rotT", [P, D])
        pe.after(dve.now())
        m = pe.did(T.matmul(bank[2][:, 0:D], xe[:, 1, 0, :], xe[:, 0, 1, :], start=True, stop=True))
        dve.after(m)
        m = dve.did(V.tensor_copy(rotT[:, :], bank[2][:, 0:D]))
        pe.after(m)
        m = pe.did(T.matmul(bank[2][:, 0:D], rotT[:, :], xe[:, 2, 0, :], start=True, stop=True))
        dve.after(m)
        m = dve.did(V.tensor_copy(rot[:, :], bank[2][:, 0:D]))
        pe.after(m)
        for e in range(E1):
            for c in range(HC):
                j = e * HC + c
                last = T.matmul(bank[3 + j // 4][:, (j % 4) * D:(j % 4 + 1) * D], ew2T[:, e, c * P:(c + 1) * P], rot[:, :],
                                start=True, stop=True)
        m = pe.did(last)
        m2 = pe.did(T.matmul(bank[7][0:E1, 0:D], eb2T[:, :], rot[:, :], start=True, stop=True))
        dve.after(m2)
        for j in range(4):
            dve.did(V.tensor_copy(ew2R[:, 2 * j:2 * j + 2, :, :], bank[3 + j][:, :].rearrange("p (e c d) -> p e c d", e=2, c=HC)))
        dve.did(V.tensor_copy(eb2R[:, :], bank[7][0:E1, 0:D]))

        x0 = sb("x0", [P, NT, D])
        x1 = sb("x1", [P, NT, D])
        hT0 = sb("hT0", [P, S])
        hT1 = sb("hT1", [P, S])
        attn = sb("attn", [P, NT, D])
        ln = [{"stats": sb(f"stats{l}", [P, NT, 6]), "mv": sb(f"mv{l}", [P, NT, 2]), "rstd": sb(f"rstd{l}", [P, NT]),
               "xhat": sb(f"xhat{l}", [P, NT, D])} for l in range(2)]

        pv = carve(0, "conv", [P, NT, ORDER + 1, D])
        fold_s = carve(0, "conv", [P, 2, 2, D])
        spec = carve(0, "conv", [P, 2, 2, D])
        spec_t = carve(0, "conv", [P, 2, 2, D])
        spec_o = carve(0, "conv", [P, 2, 2, D])

        ex = lambda shape: carve(0, "experts", shape)
        gT = ex([P, I_UP // P, S])
        sim = ex([P, 2 * PH, KEYS])
        gd = ex([P, EXPERTS])
        pair = ex([P, PH, TOP, TOP])
        pair_r = ex([P, PH, TOP * TOP])
        chosen = ex([P, PH, TOP, TOP])
        eqx = ex([P, PH, XROWS, TOP])
        ydiff = ex([P, PH, KEYS, TOP])
        epair = ex([P, PH, TOP * TOP])
        zpast = ex([P, PH, TOP * TOP])
        wsum = ex([P, EXPERTS])
        wT = gdT = sb("wT", [P, EXPERTS // P, P])
        prob = sb("prob", [P, PH, EXPERTS])
        tops = sb("tops", [P, 2 * PH, TOP])
        topi = sb("topi", [P, 2 * PH, TOP], U32)
        topf = sb("topf", [P, 2 * PH, TOP])
        best = sb("best", [P, PH, TOP])
        negbest = sb("negbest", [P, PH])
        cnt = sb("cnt", [P, PH, TOP])
        yval = sb("yval", [P, PH, TOP])
        code = sb("code", [P, PH, XROWS + KEYS], BF16)
        codeT = sb("codeT", [XROWS + KEYS, PH, P], BF16)
        esum = sb("esum", [P, PH])
        rsum = sb("rsum", [P, PH])
        past = sb("past", [P, PH, TOP])
        wpast = sb("wpast", [P, 1])
        gated = sb("gated", [P, D])

        at = lambda shape: carve(1, "attention", shape)
        TRI = P * NT * (NT + 1) // 2
        qT = [at([P, S]) for _ in range(2)]
        kT = [at([P, S]) for _ in range(2)]
        vv = [at([P, NT, 2, DH]) for _ in range(2)]
        prb = [at([P, TRI]) for _ in range(2)]
        prbT = [at([P, TRI]) for _ in range(2)]
        negmax = [sb(f"negmax{i}", [P, NT]) for i in range(2)]
        rowsum = [sb(f"rowsum{i}", [P, NT]) for i in range(2)]
        rnorm = [sb(f"rnorm{i}", [P, NT]) for i in range(2)]
        oT = sb("oT", [P, S])

        h1 = carve(1, "mixture", [P, E1 * HC, S])
        res = sb("res", [P, NT, D])
        abel = oT[:, :].rearrange("p (t d) -> p t d", t=NT)
        moe = attn
        logit = sb("logit", [P, NT, E1])
        ltop = sb("ltop", [P, NT, TOP])
        lidx = sb("lidx", [P, NT, TOP], U32)
        lidf = sb("lidf", [P, NT, 2])
        lw = sb("lw", [P, NT, 2])
        wde = sb("wde", [P, 2, NT, E1])
        gdot = sb("gdot", [P, NT, 2])
        gate = sb("gate", [P, NT])

        BANK_S, BANK_T, BO, BM, BANK_0 = bank[0:2], bank[2:4], bank[4], bank[5], bank[6:8]

        def tiles(ap):
            return ap.rearrange("p (t d) -> p t d", t=NT)

        def rows(ap):
            return ap.unsqueeze(1).broadcast_to([P, NT, D])

        def layernorm(src, buf):
            stats, mv, rstd, xhat = buf["stats"], buf["mv"], buf["rstd"], buf["xhat"]
            for t in range(NT):
                dve.did(V.bn_stats(stats[:, t, :], src[:, t, :]))
            dve.after(dve.now())
            for t in range(NT):
                dve.did(V.bn_aggr(mv[:, t, :], stats[:, t, :]))
            dve.after(dve.now())
            m = dve.did(V.tensor_scalar(rstd[:, :], mv[:, :, 1], EPS, None, ALU.add))
            pool.after(m)
            m = pool.did(G.tensor_tensor(rstd[:, :], rstd[:, :], small[:, 130:134], ALU.pow))
            yield
            dve.after(m)
            for t in range(NT):
                m = dve.did(V.tensor_scalar(xhat[:, t, :], src[:, t, :], mv[:, t, 0:1], rstd[:, t:t + 1], ALU.subtract, ALU.mult))
            yield
            return m

        def transposed(dst, src, ready, scale_ap, shift_ap, into):
            pe.after(*ready)
            for t in range(NT):
                last = T.transpose(into[:, t * P:(t + 1) * P], src[:, t, :], ident[:, :])
            m = pe.did(last)
            yield
            dve.after(m)
            m = dve.did(V.tensor_scalar(dst[:, :], into[:, :], scale_ap, shift_ap, ALU.mult, ALU.add))
            yield
            return m

        def convolutions(b):
            bf, bi = BANK_0
            m = yield from layernorm(x0, ln[0])
            m = yield from transposed(hT0, ln[0]["xhat"], [m], modT[0][:, 1, bass.ds(b, 1)], modT[0][:, 0, bass.ds(b, 1)], bf)
            pe.after(m)
            freed = [m, m]
            for t in range(NT):
                bk = BANK_0[t % 2]
                pe.after(freed[t % 2])
                m = pe.did(T.matmul(bk[:, 0:3 * D], hT0[:, t * P:(t + 1) * P], proj_w[:, :], start=True, stop=True))
                yield
                dve.after(m)
                freed[t % 2] = dve.did(V.tensor_tensor(pv[:, t, :, :].rearrange("p o d -> p (o d)"), bk[:, 0:3 * D], proj_b[:, :], ALU.add))
            for o in range(ORDER):
                v = pv[:, :, o, :]
                dve.after(dve.now())
                dve.did(V.tensor_tensor(fold_s[:, 0, :, :], v[:, 0:2, :], v[:, 2:4, :], ALU.add))
                m = dve.did(V.tensor_tensor(fold_s[:, 1, :, :], v[:, 0:2, :], v[:, 2:4, :], ALU.subtract))
                yield
                pe.after(m)
                for c in range(4):
                    for kt in range(2):
                        last = T.matmul(bf[:, c * D:(c + 1) * D], c_fwd[:, kt, c * P:(c + 1) * P], fold_s[:, c % 2, kt, :],
                                        start=(kt == 0), stop=(kt == 1))
                m = pe.did(last)
                yield
                act.after(m)
                m = act.did(A.activation(spec[:, :, :, :].rearrange("p r c d -> p (r c d)"), bf[:, :], ACT.Copy))
                yield
                dve.after(m)
                re, im = spec[:, 0, :, :], spec[:, 1, :, :]
                fa, fb, fd = (filt[:, o, i, :, :] for i in range(3))
                dve.did(V.tensor_tensor(spec_o[:, 0, :, :], re, fa, ALU.mult))
                dve.did(V.tensor_tensor(spec_t[:, 0, :, :], im, fb, ALU.mult))
                dve.did(V.tensor_tensor(spec_o[:, 1, :, :], re, fb, ALU.mult))
                m = dve.did(V.tensor_tensor(spec_t[:, 1, :, :], im, fd, ALU.mult))
                yield
                dve.after(m)
                dve.did(V.tensor_tensor(spec_o[:, 0, :, :], spec_o[:, 0, :, :], spec_t[:, 0, :, :], ALU.subtract))
                m = dve.did(V.tensor_tensor(spec_o[:, 1, :, :], spec_o[:, 1, :, :], spec_t[:, 1, :, :], ALU.add))
                yield
                pe.after(m)
                for t in range(NT):
                    for c in range(4):
                        last = T.matmul(bi[:, t * D:(t + 1) * D], c_inv[:, c, t * P:(t + 1) * P], spec_o[:, c // 2, c % 2, :],
                                        start=(c == 0), stop=(c == 3))
                    m = pe.did(last)
                    yield
                dve.after(m)
                m = dve.did(V.tensor_tensor(pv[:, :, o + 1, :], tiles(bi[:, :]), pv[:, :, o + 1, :], ALU.mult))
                yield
            dve.after(m)
            dve.after(dve.did(V.tensor_tensor(pv[:, :, 0, :], pv[:, :, ORDER, :], rows(modB[0][:, b, 0, :]), ALU.mult)))
            dve.after(dve.did(V.tensor_tensor(x0[:, :, :], x0[:, :, :], pv[:, :, 0, :], ALU.add)))
            yield

        def feed_forward(b):
            b6, b7 = BANK_0
            m = yield from layernorm(x0, ln[0])
            m_hT = yield from transposed(hT0, ln[0]["xhat"], [m], modT[0][:, 4, bass.ds(b, 1)], modT[0][:, 3, bass.ds(b, 1)], b6)
            pe.after(m_hT)
            freed = [m_hT, m_hT]
            for c in range(I_UP // P):
                bk = BANK_0[c % 2]
                pe.after(freed[c % 2])
                m = pe.did(T.matmul(bk[:, :], w_up[:, c * P:(c + 1) * P], hT0[:, :], start=True, stop=True))
                yield
                act.after(m)
                freed[c % 2] = m_gT = act.did(A.activation(gT[:, c, :], bk[:, :], ACT.Silu))
            for t in range(NT):
                tok = slice(t * P, (t + 1) * P)
                pe.after(dve.now(), act.now())
                m_s = pe.did(T.matmul(b6[:, :], hT0[:, tok], msim[:, :, :, :].rearrange("p a h k -> p (a h k)"), start=True, stop=True))
                m_g = pe.did(T.matmul(b7[:, :], hT0[:, tok], downT[:, :], start=True, stop=True))
                yield
                act.after(m_s, dve.now())
                m_sim = act.did(A.activation(sim[:, :, :].rearrange("p g k -> p (g k)"), b6[:, :], ACT.Copy))
                act.after(m_g)
                m_gd = act.did(A.activation(gd[:, :], b7[:, :], ACT.Copy))
                yield
                dve.after(m_sim)
                for g in range(2 * PH):
                    dve.did(V.max(tops[:, g, :], sim[:, g, :]))
                yield
                dve.after(dve.now())
                for g in range(2 * PH):
                    dve.did(V.max_index(topi[:, g, :], tops[:, g, :], sim[:, g, :]))
                m = dve.did(V.tensor_tensor(pair[:, :, :, :], tops[:, 0:PH, :].unsqueeze(3).broadcast_to([P, PH, TOP, TOP]),
                                            tops[:, PH:, :].unsqueeze(2).broadcast_to([P, PH, TOP, TOP]), ALU.add))
                yield
                dve.after(m)
                dve.did(V.tensor_copy(topf[:, :, :], topi[:, :, :]))
                pflat = pair[:, :, :, :].rearrange("p h a b -> p h (a b)")
                for h in range(PH):
                    dve.did(V.max(best[:, h, :], pflat[:, h, :]))
                dve.after(dve.now())
                m_yv = dve.did(V.scalar_tensor_tensor(yval[:, :, :], topf[:, PH:, :], 32.0,
                                               small[:, 8:16].unsqueeze(1).broadcast_to([P, PH, TOP]), ALU.mult, ALU.add))
                m_nb = dve.did(V.tensor_scalar(negbest[:, :], best[:, :, 0], -1.0, None, ALU.mult))
                yield
                for h in range(PH):
                    dve.did(V.match_replace(pair_r[:, h, :], best[:, h, :], pflat[:, h, :], -3e38))
                pool.after(m_yv)
                for h in range(PH):
                    m_yd = pool.did(G.tensor_tensor(ydiff[:, h, :, :], yval[:, h, :].unsqueeze(1).broadcast_to([P, KEYS, TOP]),
                                                    small[:, 16:80].unsqueeze(2).broadcast_to([P, KEYS, TOP]), ALU.subtract))
                act.after(m_nb)
                for h in range(PH):
                    m_ep = act.did(A.activation(epair[:, h, :], pflat[:, h, :], ACT.Exp, bias=negbest[:, h:h + 1]))
                yield
                dve.after(dve.now())
                chf = chosen[:, :, :, :].rearrange("p h a b -> p h (a b)")
                m_ch = dve.did(V.tensor_tensor(chf, pair_r[:, :, :], pflat, ALU.is_lt))
                dve.after(m_ch)
                m = dve.did(V.tensor_reduce(cnt[:, :, :], chosen[:, :, :, :], AX.X, ALU.add))
                for h in range(PH):
                    dve.did(V.tensor_tensor(eqx[:, h, :, :], topf[:, h, :].unsqueeze(1).broadcast_to([P, XROWS, TOP]),
                                            small[:, 0:XROWS].unsqueeze(2).broadcast_to([P, XROWS, TOP]), ALU.is_equal))
                yield
                dve.after(dve.now())
                m = dve.did(V.tensor_tensor(eqx[:, :, :, :], eqx[:, :, :, :],
                                            cnt[:, :, :].unsqueeze(2).broadcast_to([P, PH, XROWS, TOP]), ALU.mult))
                dve.after(m_ep)
                dve.did(V.tensor_scalar(past[:, :, :], topf[:, 0:PH, :], float(XROWS), None, ALU.is_ge))
                dve.did(V.tensor_tensor(epair[:, :, :], epair[:, :, :], chf, ALU.mult))
                dve.after(dve.now())
                m = dve.did(V.tensor_reduce(esum[:, :], epair[:, :, :], AX.X, ALU.add))
                dve.did(V.tensor_tensor(zpast[:, :, :].rearrange("p h (a b) -> p h a b", a=TOP),
                                        epair[:, :, :].rearrange("p h (a b) -> p h a b", a=TOP),
                                        past[:, :, :].unsqueeze(3).broadcast_to([P, PH, TOP, TOP]), ALU.mult))
                yield
                dve.after(m)
                dve.did(V.reciprocal(rsum[:, :], esum[:, :]))
                dve.after(dve.now())
                m_zp = dve.did(V.tensor_tensor(zpast[:, :, :], zpast[:, :, :],
                                               rsum[:, :].unsqueeze(2).broadcast_to([P, PH, TOP * TOP]), ALU.mult))
                yield
                with nc.allow_low_precision(reason="counts and ranks up to 8 are exact; what is larger stays above 8"):
                    dve.did(V.tensor_reduce(code[:, :, 0:XROWS], eqx[:, :, :, :], AX.X, ALU.add))
                    dve.after(m_yd)
                    for h2 in range(2):
                        m_code = dve.did(V.tensor_reduce(code[:, 2 * h2:2 * h2 + 2, XROWS:], ydiff[:, 2 * h2:2 * h2 + 2, :, :], AX.X,
                                                         ALU.min, apply_absolute_value=True))
                        yield
                pe.after(m_code, m_gd)
                psT = b6[0:XROWS + KEYS, 0:PH * P // 2].bitcast(BF16).rearrange("q (h t) -> q h t", h=PH)
                for h in range(PH):
                    last = T.transpose(psT[:, h, :], code[:, h, :], identb[:, :])
                m = pe.did(last)
                yield
                act.after(m)
                m_ct = act.did(A.activation(codeT[:, :, :], psT, ACT.Copy))
                m_l_free, m_d_free = m_gd, m_ct
                yield
                for h in range(PH):
                    pe.after(m_l_free)
                    m_l = pe.did(T.matmul(b7[:, :], hT0[:, tok], mpair[:, h, :, :].rearrange("p i j -> p (i j)"), start=True, stop=True))
                    pe.after(m_ct, m_d_free)
                    m_d = pe.did(T.matmul(b6[:, :], codeT[:, h, :], sel[:, :], start=True, stop=True))
                    yield
                    act.after(m_l)
                    m_l_free = m_p = act.did(A.activation(prob[:, h, :], b7[:, :], ACT.Exp, bias=negbest[:, h:h + 1]))
                    yield
                    dve.after(m_p, m_d, m_gd)
                    m_d_free = dve.did(V.scalar_tensor_tensor(prob[:, h, :], b6[:, :], 0.0, prob[:, h, :], ALU.is_ge, ALU.mult))
                    dve.after(m_d_free)
                    m_z = dve.did(V.scalar_tensor_tensor(prob[:, h, :], prob[:, h, :], rsum[:, h:h + 1], gd[:, :], ALU.mult, ALU.mult))
                    yield
                act.after(m_z, m_zp)
                pflat_all = prob[:, :, :].rearrange("p h e -> p (h e)")
                for half in range(2):
                    m_w = act.did(A.activation(pflat_all[:, half * 2 * EXPERTS:(half + 1) * 2 * EXPERTS],
                                               pflat_all[:, half * 2 * EXPERTS:(half + 1) * 2 * EXPERTS], ACT.Silu))
                m_wp = act.did(A.activation(epair[:, :, :].rearrange("p h c -> p (h c)"), zpast[:, :, :].rearrange("p h c -> p (h c)"), ACT.Silu,
                                            scale=gd[:, EXPERTS - 1:EXPERTS], accum_out=wpast[:, 0:1]))
                yield
                pool.after(m_w)
                pool.after(pool.did(G.tensor_tensor(prob[:, 0:2, :], prob[:, 0:2, :], prob[:, 2:4, :], ALU.add)))
                pool.after(pool.did(G.tensor_tensor(wsum[:, :], prob[:, 0, :], prob[:, 1, :], ALU.add)))
                pool.after(m_wp)
                m_ws = pool.did(G.tensor_tensor(wsum[:, EXPERTS - 1:EXPERTS], wsum[:, EXPERTS - 1:EXPERTS], wpast[:, 0:1], ALU.add))
                pe.after(m_d_free, m_gT)
                for c in range(4):
                    T.matmul(b6[:, 0:D], gT[:, c, tok], w_down[:, c, :], start=(c == 0), stop=False)
                yield
                yield
                yield
                pe.after(m_ws, m_l_free)
                for c in range(4):
                    last = T.transpose(b7[:, c * P:(c + 1) * P], wsum[:, c * P:(c + 1) * P], ident[:, :])
                m = pe.did(last)
                yield
                dve.after(m)
                m_wT = dve.did(V.tensor_copy(wT[:, :, :], b7[:, :].rearrange("p (c t) -> p c t", c=4)))
                yield
                pe.after(m_wT)
                for c in range(4):
                    last = T.matmul(b6[:, 0:D], wT[:, c, :], up_e[:, c, :], start=False, stop=(c == 3))
                m_o = pe.did(last)
                yield
                dve.after(m_o)
                dve.after(dve.did(V.tensor_tensor(gated[:, :], b6[:, 0:D], modB[0][:, b, 3, :], ALU.mult)))
                dve.after(dve.did(V.tensor_tensor(x0[:, t, :], x0[:, t, :], gated[:, :], ALU.add)))
                yield

        def layer0(b):
            x_in.after(dve.now(), pool.now())
            m_x = x_in.did(nc.sync.dma_start(x0[:, :, :], a["x"][b].rearrange("(t p) d -> p t d", p=P)))
            yield
            yield
            dve.after(m_x)
            yield from convolutions(b)
            yield from feed_forward(b)
            m = yield from layernorm(x0, ln[0])
            yield from transposed(hT0, ln[0]["xhat"], [m], modT[1][:, 1, bass.ds(b, 1)], modT[1][:, 0, bass.ds(b, 1)], BANK_0[0])

        def attention():
            p_at = [0, P, 3 * P, 6 * P]
            s_of = [BANK_S[1][:, 0:P], BANK_S[0][:, 0:2 * P], BANK_S[1][:, P:4 * P], BANK_S[0][:, :]]
            pt_at = [0, 4 * P, 8 * P, 7 * P]
            t_bank, t_off = [0, 1, 0, 1], [0, 0, 0, 3 * P]
            st = {}

            def been(*keys):
                return [st[k] for k in keys if k in st]

            def project(kind, h):
                par = h % 2
                pe.after(*been("bm_free"))
                if kind == "v":
                    for t in range(NT):
                        last = T.matmul(BM[:, t * P:(t + 1) * P], hT1[:, t * P:(t + 1) * P], wv[:, h, :], start=True, stop=True)
                    m = pe.did(last)
                    yield
                    dve.after(m, *been(("pv", 0), ("pv", 1)))
                    st["v", par] = st["bm_free"] = dve.did(V.tensor_tensor(
                        vv[par][:, :, :, :].rearrange("p t m c -> p t (m c)"), tiles(BM[:, :]),
                        lam_row[:, :, :].rearrange("p m c -> p (m c)").unsqueeze(1).broadcast_to([P, NT, 2 * DH]), ALU.mult))
                    return
                w, dst, k = (wq, qT, DH ** -0.5) if kind == "q" else (wk, kT, 1.0)
                m = pe.did(T.matmul(BM[:, :], w[:, h, :], hT1[:, :], start=True, stop=True))
                yield
                act.after(m, *been(("scores", par)))
                st[kind, par] = st["bm_free"] = act.did(A.activation(dst[par][:, :], BM[:, :], ACT.Copy, scale=k))

            def scores(u, order):
                par, mp, buf = u // 2 % 2, u % 2, u % 2
                r = slice(DH * mp, DH * mp + DH)
                pe.after(st["q", par], st["k", par])
                ready = {}
                for qc in order:
                    pe.after(*been(("bank_s", 1 if qc in (0, 2) else 0)))
                    T.matmul(s_of[qc], qT[par][r, qc * P:(qc + 1) * P], kT[par][r, 0:(qc + 1) * P], start=True, stop=False)
                    ready[qc] = pe.did(T.matmul(s_of[qc][:, qc * P:(qc + 1) * P], identb[:, :], mask[:, :], start=False, stop=True))
                    st["scores", par] = ready[qc]
                if 2 in ready:
                    ready[2] = ready[0]
                for qc in order:
                    dve.after(ready[qc], *been(("sums", buf)))
                    ready[qc] = dve.did(V.tensor_reduce(negmax[buf][:, qc:qc + 1], s_of[qc], AX.X, ALU.max, negate=True))
                if 2 in ready:
                    ready[2] = ready[0]
                for qc in order:
                    act.after(ready[qc], *been(("tr", buf)))
                    m = act.did(A.activation(prb[buf][:, p_at[qc]:p_at[qc] + (qc + 1) * P], s_of[qc], ACT.Exp,
                                             bias=negmax[buf][:, qc:qc + 1], accum_out=rowsum[buf][:, qc:qc + 1]))
                    st["bank_s", 1 if qc in (0, 2) else 0] = m
                st["exp", buf] = m

            def normalise(u):
                buf = u % 2
                dve.after(st["exp", buf])
                dve.after(dve.did(V.reciprocal(rnorm[buf][:, :], rowsum[buf][:, :])))
                m = dve.did(V.tensor_scalar(rnorm[buf][:, :], rnorm[buf][:, :], 1.0 - LAMBDA_INIT, None, ALU.mult))
                pool.after(m)
                for qc in range(NT):
                    v = prb[buf][:, p_at[qc]:p_at[qc] + (qc + 1) * P]
                    m = pool.did(G.tensor_scalar(v, v, rnorm[buf][:, qc:qc + 1], 1.0, ALU.mult, ALU.mult))
                st["norm", buf] = m

            def turn(u, kcs, evac):
                buf = u % 2
                bk = t_bank[kcs[0]]
                pe.after(st["norm", buf], *been(("bank_t", bk)))
                for kc in kcs:
                    for qc in range(kc, NT):
                        c = t_off[kc] + (qc - kc) * P
                        last = T.transpose(BANK_T[bk][:, c:c + P], prb[buf][:, p_at[qc] + kc * P:p_at[qc] + (kc + 1) * P], ident[:, :])
                st["tr", buf] = m = pe.did(last)
                n = sum(NT - kc for kc in kcs) * P
                dst, src = prbT[buf][:, pt_at[kcs[0]]:pt_at[kcs[0]] + n], BANK_T[bk][:, 0:n]
                evac.after(m, *been(("pv", buf)))
                st["bank_t", bk] = st["pt", kcs[0]] = evac.did(V.tensor_copy(dst, src) if evac is dve else A.activation(dst, src, ACT.Copy))

            def apply(u):
                par, mp, buf = u // 2 % 2, u % 2, u % 2
                rows_o = slice(DH * par, DH * par + DH)
                pe.after(st["v", par], *been(("o", par)))
                for n, kc in enumerate((0, 1, 3, 2)):
                    pe.after(*been(("pt", kc)))
                    last = T.matmul(BO[rows_o, kc * P:S], vv[par][:, kc, mp, :], prbT[buf][:, pt_at[kc]:pt_at[kc] + (NT - kc) * P],
                                    start=(n == 0 and mp == 0), stop=(n == NT - 1 and mp == 1))
                st["pv", buf] = m = pe.did(last)
                if mp == 1:
                    act.after(m, *been("wo"))
                    st["o", par] = act.did(A.activation(oT[rows_o, :], BO[rows_o, :], ACT.Copy))

            def project_out(g):
                pe.after(st["o", 0], st["o", 1], st["bm_free"])
                for t in range(NT):
                    last = T.matmul(BM[:, t * D:(t + 1) * D], oT[:, t * P:(t + 1) * P], wo[:, g, :], start=True, stop=True)
                st["wo"] = m = pe.did(last)
                yield
                dve.after(m)
                if g == 0:
                    st["bm_free"] = dve.did(V.tensor_copy(attn[:, :, :], tiles(BM[:, :])))
                else:
                    st["bm_free"] = dve.did(V.tensor_tensor(attn[:, :, :], attn[:, :, :], tiles(BM[:, :]), ALU.add))

            maps = 2 * H1
            for kind in "qkv":
                yield from project(kind, 0)
            scores(0, (3, 2, 0))
            yield
            scores(0, (1,))
            normalise(0)
            yield
            for u in range(maps):
                nxt = u // 2 + 1
                if u + 1 < maps:
                    scores(u + 1, (3, 2, 0))
                    yield
                if nxt < H1:
                    yield from project("q" if u % 2 == 0 else "v", nxt)
                turn(u, (0,), dve)
                turn(u, (1, 3), act)
                yield
                if u + 1 < maps:
                    scores(u + 1, (1,))
                    yield
                if nxt < H1 and u % 2 == 0:
                    yield from project("k", nxt)
                turn(u, (2,), dve)
                if u + 1 < maps:
                    normalise(u + 1)
                yield
                if u % 4 == 0 and u:
                    yield from project_out(u // 4 - 1)
                apply(u)
                yield
            yield from project_out(PAIRS - 1)
            yield

        def mixture(b):
            xhat = ln[1]["xhat"]
            wdT = xhat[:, :, :].rearrange("p t d -> p (t d)")[0:E1, :]
            m = yield from layernorm(x1, ln[1])
            dve.after(m, out_stored.now())
            dve.after(dve.did(V.tensor_tensor(res[:, :, :], xhat[:, :, :], rows(modB[1][:, b, 2, :]), ALU.mult)))
            dve.after(dve.did(V.tensor_tensor(res[:, :, :], res[:, :, :], rows(modB[1][:, b, 1, :]), ALU.add)))
            yield
            m = yield from layernorm(res, ln[1])
            m_hT = yield from transposed(hT1, xhat, [m], gammaT[:, 0:1], gammaT[:, 1:2], BM)
            pe.after(m_hT)
            for t in range(NT):
                T.matmul(BO[:, t * D:(t + 1) * D], hT1[:, t * P:(t + 1) * P], abel_w[:, :], start=True, stop=True)
            for t in range(NT):
                last = T.matmul(BM[:, t * E1:(t + 1) * E1], hT1[:, t * P:(t + 1) * P], gate_w[:, :], start=True, stop=True)
            m_lg = pe.did(last)
            m_h1 = []

            def expand(j):
                bk = bank[j % 4]
                if j >= 4:
                    pe.after(m_h1[j - 4])
                m = pe.did(T.matmul(bk[:, :], ew1[:, j // HC, (j % HC) * P:(j % HC + 1) * P], hT1[:, :], start=True, stop=True))
                act.after(m)
                m_h1.append(act.did(A.activation(h1[:, j, :], bk[:, :], ACT.Gelu, bias=eb1T[:, j:j + 1])))

            expand(0)
            expand(1)
            yield
            dve.after(m_lg)
            m_ab = dve.did(V.tensor_tensor(abel[:, :, :], tiles(BO[:, :]), rows(abel_b[:, :]), ALU.add))
            dve.after(dve.did(V.tensor_tensor(logit[:, :, :], BM[:, 0:NT * E1].rearrange("p (t e) -> p t e", t=NT),
                                              gate_b[:, :].unsqueeze(1).broadcast_to([P, NT, E1]), ALU.add)))
            expand(2)
            expand(3)
            yield
            for t in range(NT):
                dve.did(V.max(ltop[:, t, :], logit[:, t, :]))
            dve.after(dve.now())
            for t in range(NT):
                dve.did(V.max_index(lidx[:, t, :], ltop[:, t, :], logit[:, t, :]))
            dve.did(V.tensor_tensor(lw[:, :, 1], ltop[:, :, 1], ltop[:, :, 0], ALU.subtract))
            dve.after(dve.now())
            m = dve.did(V.tensor_copy(lidf[:, :, :], lidx[:, :, 0:2]))
            for j in range(4, E1 * HC):
                expand(j)
                if j % 2:
                    yield
            act.after(m_ab)
            m_abel = act.did(A.activation(abel[:, :, :], abel[:, :, :], ACT.Gelu))
            act.after(m)
            m = act.did(A.activation(lw[:, :, 1], lw[:, :, 1], ACT.Exp))
            yield
            dve.after(m)
            dve.after(dve.did(V.tensor_scalar(lw[:, :, 0], lw[:, :, 1], 1.0, None, ALU.add)))
            dve.after(dve.did(V.reciprocal(lw[:, :, 0], lw[:, :, 0])))
            dve.after(dve.did(V.tensor_tensor(lw[:, :, 1], lw[:, :, 1], lw[:, :, 0], ALU.mult)))
            for k in range(K1):
                dve.did(V.tensor_tensor(wde[:, k, :, :], lidf[:, :, k].unsqueeze(2).broadcast_to([P, NT, E1]),
                                        small[:, 134:142].unsqueeze(1).broadcast_to([P, NT, E1]), ALU.is_equal))
            dve.after(dve.now())
            for k in range(K1):
                dve.did(V.tensor_tensor(wde[:, k, :, :], wde[:, k, :, :],
                                        lw[:, :, k].unsqueeze(2).broadcast_to([P, NT, E1]), ALU.mult))
            dve.after(dve.now())
            m = dve.did(V.tensor_tensor(wde[:, 0, :, :], wde[:, 0, :, :], wde[:, 1, :, :], ALU.add))
            pe.after(m)
            for t in range(NT):
                last = T.transpose(BM[0:E1, t * P:(t + 1) * P], wde[:, 0, t, :], ident[:, :])
            m = pe.did(last)
            yield
            dve.after(m)
            m_wdT = dve.did(V.tensor_copy(wdT, BM[0:E1, :]))
            pe.after(m_wdT, *m_h1[-4:])
            freed = [None, None]
            for t in range(NT):
                last = T.matmul(BM[:, t * D:(t + 1) * D], wdT[:, t * P:(t + 1) * P], eb2R[:, :], start=True, stop=True)
            m_b = pe.did(last)

            def contract(t):
                if freed[t % 2]:
                    pe.after(freed[t % 2])
                for e in range(E1):
                    for c in range(HC):
                        last = T.matmul(bank[t % 2 * 2 + e // 4][:, (e % 4) * D:(e % 4 + 1) * D], h1[:, e * HC + c, t * P:(t + 1) * P],
                                        ew2R[:, e, c, :], start=(c == 0), stop=(c == HC - 1))
                return pe.did(last)

            m_e = contract(0)
            yield
            dve.after(m_b)
            dve.after(dve.did(V.tensor_copy(moe[:, :, :], tiles(BM[:, :]))))
            for t in range(NT):
                m_next = contract(t + 1) if t + 1 < NT else None
                dve.after(m_e)
                for e in range(E1):
                    m = dve.did(V.scalar_tensor_tensor(moe[:, t, :], bank[t % 2 * 2 + e // 4][:, (e % 4) * D:(e % 4 + 1) * D],
                                                       wde[:, 0, t, e:e + 1], moe[:, t, :], ALU.mult, ALU.add))
                    dve.after(m)
                    if e % 4 == 3:
                        yield
                freed[t % 2] = m
                m_e = m_next
            dve.after(m_abel)
            for k, src in enumerate((abel, moe)):
                dve.after(dve.did(V.tensor_tensor(xhat[:, :, :], src[:, :, :], rows(gc_w[:, k * D:(k + 1) * D]), ALU.mult)))
                dve.after(dve.did(V.tensor_reduce(gdot[:, :, k], xhat[:, :, :], AX.X, ALU.add)))
                yield
            m = dve.did(V.tensor_scalar(gate[:, :], gdot[:, :, 0], gc_b[:, 0:1], None, ALU.add))
            dve.after(m)
            m = dve.did(V.tensor_tensor(gate[:, :], gate[:, :], gdot[:, :, 1], ALU.add))
            act.after(m)
            m = act.did(A.activation(gate[:, :], gate[:, :], ACT.Tanh, scale=0.5))
            dve.after(dve.did(V.tensor_tensor(moe[:, :, :], moe[:, :, :], abel[:, :, :], ALU.subtract)))
            dve.after(dve.did(V.tensor_tensor(res[:, :, :], res[:, :, :], abel[:, :, :], ALU.add)))
            yield
            dve.after(m)
            dve.after(dve.did(V.tensor_scalar(gate[:, :], gate[:, :], 1.0, 0.5, ALU.add, ALU.mult)))
            dve.after(dve.did(V.tensor_tensor(moe[:, :, :], moe[:, :, :], gate[:, :].unsqueeze(2).broadcast_to([P, NT, D]), ALU.mult)))
            dve.after(dve.did(V.tensor_tensor(moe[:, :, :], moe[:, :, :], res[:, :, :], ALU.add)))
            dve.after(dve.did(V.tensor_tensor(moe[:, :, :], moe[:, :, :], rows(modB[1][:, b, 3, :]), ALU.mult)))
            yield
            m = dve.did(V.tensor_tensor(res[:, :, :], moe[:, :, :], x1[:, :, :], ALU.add))
            out_stored.after(m)
            out_stored.did(nc.sync.dma_start(out[b].rearrange("(t p) d -> p t d", p=P), res[:, :, :]))

        def hand_over():
            m = act.did(A.activation(hT1[:, :], hT0[:, :], ACT.Copy))
            pool.did(G.tensor_copy(x1[:, :, :], x0[:, :, :]))
            pe.after(m)
            dve.after(pool.now(), m)
            act.after(m)

        def layer1(b):
            yield from attention()
            dve.after(dve.now())
            dve.after(dve.did(V.tensor_tensor(attn[:, :, :], attn[:, :, :], rows(modB[1][:, b, 0, :]), ALU.mult)))
            dve.after(dve.did(V.tensor_tensor(x1[:, :, :], x1[:, :, :], attn[:, :, :], ALU.add)))
            pe.after(act.now())
            yield from mixture(b)

        def beside(main, side, pace):
            due = 0.0
            for _ in main:
                due += pace
                while side is not None and due >= 1:
                    due -= 1
                    if next(side, StopIteration) is StopIteration:
                        side = None
            for _ in side or ():
                pass

        def settle():
            for e in (pe, dve, act, pool):
                e.after(e.now())

        main_engines = [pe, dve, act, pool]
        settle()
        nc.all_engine_barrier()
        for _ in layer0(0):
            pass
        settle()
        with loops.clearing("batches", B - 1, main_engines) as b:
            hand_over()
            beside(layer1(b), layer0(b + 1), PACE)
            settle()
        hand_over()
        for _ in layer1(B - 1):
            pass
        out_stored.after(out_stored.now())
        return loops.seen


def _layout(i):
    c = np.ascontiguousarray
    head_major = lambda w: c(w.reshape(D, 2, H1, DH).transpose(0, 2, 1, 3).reshape(D, 2 * H1 * DH))
    g = i["L1_ffn_gens"]
    return {
        "x": i["L0_attn_x"], "cT0": c(i["L0_c"].T), "cT1": c(i["L1_c"].T), "wmod0": i["L0_wmod"], "wmod1": i["L1_wmod"],
        "proj_w": i["L0_attn_proj_w"], "proj_b": i["L0_attn_proj_b"].reshape(1, -1),
        "filter": i["L0_attn_filter_time"].reshape(ORDER, TAPS, D),
        "W_upT": c(i["L0_ffn_W_up"].T), "W_downT": c(i["L0_ffn_W_down"].T), "W_q": i["L0_ffn_W_q"],
        "keysT": c(i["L0_ffn_keys"].transpose(2, 0, 3, 1).reshape(2 * PH * PN, KEYS)),
        "downT": c(i["L0_ffn_down_embed"].T), "up_embed": i["L0_ffn_up_embed"],
        "Wq": head_major(i["L1_attn_Wq"]), "Wk": head_major(i["L1_attn_Wk"]), "Wv": head_major(i["L1_attn_Wv"]),
        "Wo": i["L1_attn_Wo"],
        "lam": c(np.stack([i["L1_attn_lq1"], i["L1_attn_lk1"], i["L1_attn_lq2"], i["L1_attn_lk2"]])),
        "gammabetaT": c(np.stack([i["L1_ffn_ln_gamma"], i["L1_ffn_ln_beta"]], axis=1)),
        "abel_w": i["L1_ffn_abel_w"], "abel_b": i["L1_ffn_abel_b"].reshape(1, -1),
        "gate_w": i["L1_ffn_moe_gate_w"], "gate_b": i["L1_ffn_moe_gate_b"].reshape(1, -1),
        "ew1": i["L1_ffn_ew1"], "eb1T": c(i["L1_ffn_eb1"].reshape(E1 * HC, P).T),
        "ew2T": c(i["L1_ffn_ew2"].transpose(0, 2, 1)), "eb2T": c(i["L1_ffn_eb2"].T),
        "gens2": c(np.stack([g, g.transpose(0, 2, 1)], axis=1)),
        "gc_w": i["L1_ffn_gc_w"].reshape(1, -1), "gc_b": i["L1_ffn_gc_b"].reshape(1, 1),
    }


def kernel(**inputs):
    import concourse.bacc as bacc
    from concourse.bass_utils import run_bass_kernel_spmd

    arrays = {f"in_{k}": np.ascontiguousarray(v) for k, v in
              {**_layout({k: np.asarray(v) for k, v in inputs.items()}), **host_constants()}.items()}

    def program(per):
        nc = bacc.Bacc("TRN2", target_bir_lowering=False, num_devices=1)
        aps = {name[3:]: nc.dram_tensor(name, v.shape, mybir.dt.from_np(v.dtype), kind="ExternalInput").ap()
               for name, v in arrays.items()}
        out = nc.dram_tensor("out_0", (B, S, D), F32, kind="ExternalOutput").ap()
        return nc, build(nc, per, aps, out)

    _, per = program({})
    nc, _ = program(per)
    r = run_bass_kernel_spmd(nc, [arrays], core_ids=[0])
    return r.results[0]["out_0"]
```

```python
from contextlib import ExitStack, contextmanager
from itertools import chain

import numpy as np

import concourse.bass as bass
from concourse import mybir
from concourse.alu_op_type import AluOpType as ALU

F32 = mybir.dt.float32
BF16 = mybir.dt.bfloat16
F32R = mybir.dt.float32r
U32 = mybir.dt.uint32
ACT = mybir.ActivationFunctionType
AX = mybir.AxisListType
MAX_REDUCE = bass.bass_isa.ReduceOp.max

P = 128
B, S, D = 4, 512, 128
NT = S // P
TAPS = 256
ORDER = 2
I_UP = 512
PH, KEYS, TOP, PN = 4, 64, 8, 64
EXPERTS = 512
XROWS = EXPERTS // KEYS
H1, DH = 16, 64
PAIRS = H1 // 2
LAMBDA_INIT = 0.8
E1, HID1, K1 = 8, 256, 2
HC = HID1 // P
NROT = 3
EPS = 1e-5
MAX_SQUARINGS = 16
EXPM_THETA = 0.5
TAYLOR = [1.0, 1.0, 1 / 2, 1 / 6, 1 / 24, 1 / 120, 1 / 720, 1 / 5040, 1 / 40320]
CAUSAL_FILL = -1e30
PACE_SETUP = 0.6
PACE = 0.75


class Mark:

    def __init__(self, sem, base, n):
        self.sem, self.value = sem, base + n


class Progress:

    def __init__(self, name, sem, engine, step=1):
        self.name, self.sem, self.engine, self.step = name, sem, engine, step
        self.base, self.n = 0, 0

    def did(self, instruction):
        instruction.then_inc(self.sem, self.step)
        self.n += self.step
        return self.now()

    def now(self):
        return Mark(self.sem, self.base, self.n)

    def after(self, *marks):
        for m in marks:
            self.engine.wait_ge(m.sem, m.value)


class Loops:

    def __init__(self, nc, progresses, per):
        self.nc, self.progresses, self.per, self.seen = nc, progresses, per, {}

    @contextmanager
    def clearing(self, name, end, cleared):
        sems = [p.sem for p in cleared]
        first = min(s.num for s in sems)
        assert sorted(s.num for s in sems) == list(range(first, first + len(sems)))
        clear = range(first, first + len(sems))
        self.nc.all_engine_barrier(sems_to_clear=clear)
        for p in cleared:
            p.n = 0
        with self.loop(name, 0, end) as i:
            yield i
            self.nc.all_engine_barrier(sems_to_clear=clear)
            for p in cleared:
                p.n = 0
        for p in cleared:
            p.n = 0

    @contextmanager
    def loop(self, name, start, end):
        before = [(p.base, p.n) for p in self.progresses]
        turn = self.per.get(name, [0] * len(before))
        with self.nc.Fori(start, end) as i:
            for p, k in zip(self.progresses, turn):
                if k:
                    p.base = p.base + (i - start) * k if start else p.base + i * k
            yield i
        self.seen[name] = [p.n - n for p, (_, n) in zip(self.progresses, before)]
        for p, (base, n), k in zip(self.progresses, before, self.seen[name]):
            p.base, p.n = base, n + (end - start) * k


def host_constants():
    n = 2 * TAPS
    k = np.concatenate([np.arange(0, TAPS, 2), np.arange(1, TAPS, 2)])
    t = np.arange(n)
    ang = 2 * np.pi * ((k[:, None] * t[None, :]) % n) / n
    cos, sin = np.cos(ang), np.sin(ang)
    alt = np.where(t % 2 == 0, 1.0, -1.0)
    imag = -sin
    imag[0] = alt
    fwd = np.concatenate([cos, imag])
    inv_r, inv_i = 2 * cos / n, -2 * sin / n
    inv_r[0], inv_i[0] = 1 / n, alt / n
    inv = np.concatenate([inv_r, inv_i])[:, :TAPS]
    fd = cos.copy()
    fd[0] = alt
    filt = np.stack([cos, -sin, fd])[:, :, :TAPS]
    f = np.float32
    fwd_half = fwd[:, :TAPS]
    sel = np.zeros((XROWS + KEYS, XROWS, KEYS))
    for i in range(XROWS):
        sel[i, i, :] = 1
    for j in range(KEYS):
        sel[XROWS + j, :, j] = -1
    small = np.zeros((1, 256))
    small[0, 0:TOP] = np.arange(TOP)
    small[0, 8:16] = np.arange(TOP) + 1
    small[0, 16:80] = 32.0 * np.arange(KEYS)
    small[0, 80:96] = EXPM_THETA * 2.0 ** np.arange(MAX_SQUARINGS)
    small[0, 96:113] = 2.0 ** -np.arange(MAX_SQUARINGS + 1)
    small[0, 113:130] = np.arange(MAX_SQUARINGS + 1)
    small[0, 130:134] = -0.5
    small[0, 134:142] = np.arange(E1)
    q = np.arange(P)
    return {
        "c_fwd": fwd_half.T.astype(f),
        "c_inv": inv.astype(f),
        "c_filt": filt.transpose(0, 2, 1).astype(f).copy(),
        "c_ident": np.eye(P, dtype=f),
        "c_mask": np.where(q[None, :] > q[:, None], CAUSAL_FILL, 0.0).astype(f),
        "c_sel": sel.reshape(XROWS + KEYS, EXPERTS).astype(f),
        "c_small": small.astype(f),
    }


def build(nc, per, a, out):
    es = ExitStack()
    with es:
        def sb(name, shape, dt=F32):
            return es.enter_context(nc.sbuf_tensor(name, shape, dt))

        def progress(name, engine, step=1):
            return Progress(name, es.enter_context(nc.semaphore(name)), engine, step)

        bank = [es.enter_context(nc.psum_tensor(f"bank{i}", [P, 512], F32)) for i in range(8)]

        pe = progress("pe_done", nc.tensor)
        dve = progress("dve_done", nc.vector)
        act = progress("act_done", nc.scalar)
        pool = progress("pool_done", nc.gpsimd)
        setup_in = progress("setup_in", nc.sync, 16)
        layer0_in = progress("layer0_in", nc.sync, 16)
        layer1_in = progress("layer1_in", nc.sync, 16)
        x_in = progress("x_in", nc.sync, 16)
        out_stored = progress("out_stored", nc.sync, 16)
        V, A, T, G = nc.vector, nc.scalar, nc.tensor, nc.gpsimd
        loops = Loops(nc, [pe, dve, act, pool, x_in, out_stored], per)

        ARENA = (8192, 8192)
        arena = [sb(f"arena{i}", [P, words]) for i, words in enumerate(ARENA)]
        carved = {}

        def carve(i, phase, shape):
            words = int(np.prod(shape[1:]))
            at = carved.get((i, phase), 0)
            carved[i, phase] = at + words
            assert at + words <= ARENA[i], (i, phase)
            names = "abcd"[:len(shape) - 1]
            v = arena[i][:, at:at + words]
            if len(shape) == 2:
                return v
            return v.rearrange(f"p ({' '.join(names)}) -> p {' '.join(names)}", **dict(zip(names, shape[1:])))

        def load(name, shape, src, place=None):
            tile = sb(name, shape) if place is None else place
            stream.did(nc.sync.dma_start(tile[tuple(slice(None) for _ in shape)], src))
            return tile

        stream = setup_in
        small = load("small", [P, 256], a["c_small"][0:1, :].broadcast_to([P, 256]))
        ident = load("ident", [P, P], a["c_ident"])
        cT = [load(f"cT{l}", [P, B], a[f"cT{l}"]) for l in range(2)]
        wmod = [load(f"wmod{l}", [P, 6 * D], a[f"wmod{l}"], carve(0, "setup", [P, 6 * D])) for l in range(2)]
        taps = load("taps", [P, ORDER, TAPS // P, D], a["filter"].rearrange("o (c p) d -> p o c d", p=P), carve(0, "setup", [P, ORDER, TAPS // P, D]))
        c_filt = load("c_filt_sb", [P, 3, TAPS // P, TAPS], a["c_filt"].rearrange("m (c p) r -> p m c r", p=P), carve(0, "setup", [P, 3, TAPS // P, TAPS]))
        w_q = load("w_q", [P, 4, D], a["W_q"].rearrange("(c p) d -> p c d", p=P), carve(0, "setup", [P, 4, D]))
        keysT = load("keysT", [P, 4, KEYS], a["keysT"].rearrange("(c p) k -> p c k", p=P), carve(0, "setup", [P, 4, KEYS]))
        lam_in = load("lam_in", [P, 4, DH], a["lam"].rearrange("(o q) c -> o q c", o=1).broadcast_to([P, 4, DH]), carve(0, "setup", [P, 4, DH]))
        maskf = load("maskf", [P, P], a["c_mask"], carve(0, "setup", [P, P]))
        self_ = load("self", [XROWS + KEYS, EXPERTS], a["c_sel"], carve(0, "setup", [P, EXPERTS])[0:XROWS + KEYS, :])
        stream = layer0_in
        x0 = load("x0", [P, NT, D], a["x"][0].rearrange("(t p) d -> p t d", p=P))
        proj_w = load("proj_w", [P, (ORDER + 1) * D], a["proj_w"])
        proj_b = load("proj_b", [P, (ORDER + 1) * D], a["proj_b"][0:1, :].broadcast_to([P, 3 * D]))
        c_fwd = load("c_fwd_sb", [P, TAPS // P, S], a["c_fwd"].rearrange("(c p) r -> p c r", p=P))
        c_inv = load("c_inv_sb", [P, S // P, TAPS], a["c_inv"].rearrange("(c p) t -> p c t", p=P))
        w_up = load("w_up", [P, I_UP], a["W_upT"])
        w_down = load("w_down", [P, I_UP // P, D], a["W_downT"].rearrange("(c p) d -> p c d", p=P))
        downT = load("downT", [P, EXPERTS], a["downT"])
        up_e = load("up_e", [P, EXPERTS // P, D], a["up_embed"].rearrange("(c p) d -> p c d", p=P))
        stream = layer1_in
        xb = load("gens_sb", [P, NROT, 2, D], a["gens2"].rearrange("i t p d -> p i t d"), carve(1, "setup", [P, NROT, 2, D]))
        eb2T = load("eb2T", [P, E1], a["eb2T"])
        wqkT = load("wqkT", [P, 2, H1, D], a["WqkT"].rearrange("p (w h d) -> p w h d", w=2, h=H1), carve(1, "setup", [P, 2, H1, D]))
        wv = load("wv", [P, H1, 2 * DH], a["Wv"].rearrange("d (h c) -> d h c", h=H1))
        wo = load("wo", [P, PAIRS, D], a["Wo"].rearrange("(g p) d -> p g d", p=P))
        gammaT = load("gammaT", [P, 2], a["gammabetaT"])
        abel_w = load("abel_w", [P, D], a["abel_w"])
        abel_b = load("abel_b", [P, D], a["abel_b"][0:1, :].broadcast_to([P, D]))
        gate_w = load("gate_w", [P, E1], a["gate_w"])
        gate_b = load("gate_b", [P, E1], a["gate_b"][0:1, :].broadcast_to([P, E1]))
        ew1 = load("ew1", [P, E1, HID1], a["ew1"].rearrange("e d h -> d e h"))
        eb1T = load("eb1T", [P, E1 * HC], a["eb1T"])
        gc_w = load("gc_w", [P, 2 * D], a["gc_w"][0:1, :].broadcast_to([P, 2 * D]))
        gc_b = load("gc_b", [P, 1], a["gc_b"][0:1, :].broadcast_to([P, 1]))

        m_layer1 = layer1_in.now()

        identb = sb("identb", [P, P], BF16)
        mask = sb("mask", [P, P], BF16)
        sel = sb("sel", [XROWS + KEYS, EXPERTS], BF16)
        silT = sb("silT", [P, 2, B])
        silB = carve(0, "setup", [P, 2, B, P])
        modT = [sb(f"modT{l}", [P, 6, B]) for l in range(2)]
        MOD_ROWS = (2, 4)
        modB = [sb(f"modB{l}", [P, B, n, D]) for l, n in enumerate(MOD_ROWS)]
        signs = silB
        gate_neg = carve(0, "setup", [P, 2, B, D])
        filt = sb("filt", [P, ORDER, 3, 2, D])
        msim = sb("msim", [P, 2, PH, KEYS])
        mpair = sb("mpair", [P, PH, XROWS, KEYS])
        lam_p = sb("lam_p", [P, 2, DH])
        lam_s = sb("lam_s", [P, 2])
        lam_row = sb("lam_row", [P, 2, DH])
        mqk = sb("mqk", [P, H1, 2, D])
        ew2R = sb("ew2R", [P, E1, HC, D])
        eb2R = sb("eb2R", [E1, D])

        for e in (pe, dve, act, pool):
            e.after(setup_in.now())
        m_sil = [act.did(A.activation(silT[:, l, :], cT[l][:, :], ACT.Silu)) for l in range(2)]
        dve.did(V.tensor_copy(identb[:, :], ident[:, :]))
        dve.did(V.tensor_copy(mask[:, :], maskf[:, :]))
        dve.did(V.tensor_copy(sel[:, :], self_[:, :]))
        dve.after(m_sil[1])
        m_silB = dve.did(V.tensor_copy(silB[:, :, :, :].rearrange("p l b q -> p (l b) q"),
                                       silT[:, :, :].rearrange("p l b -> p (l b)").unsqueeze(2).broadcast_to([P, 2 * B, P])))
        pe.after(m_sil[1], m_silB)
        for l in range(2):
            for s in range(6):
                T.matmul(bank[0][:, (l * 6 + s) * B:(l * 6 + s + 1) * B], wmod[l][:, s * D:(s + 1) * D],
                         silT[:, l, :], start=True, stop=True)
        m_bc = []
        for l in range(2):
            for b in range(B):
                m_bc.append(pe.did(T.matmul(bank[1 + (l * B + b) % 4][:, :], silB[:, l, b, :], wmod[l][:, 2 * D:6 * D],
                                            start=True, stop=True)))
                if l == 0 and b == B - 1:
                    m_first = [None] * B
                    for bb in range(B):
                        dve.after(m_bc[bb])
                        m_first[bb] = dve.did(V.tensor_copy(modB[0][:, bb, :, :], bank[1 + bb][:, :].rearrange("p (s d) -> p s d", s=4)[:, 0::3, :]))
                    pe.after(m_first[B - 1])
        for bb in range(B):
            dve.after(m_bc[B + bb])
            dve.did(V.tensor_copy(modB[1][:, bb, :, :], bank[1 + bb][:, :].rearrange("p (s d) -> p s d", s=4)))
        for l in range(2):
            m_t = dve.did(V.tensor_copy(modT[l][:, :, :], bank[0][:, l * 6 * B:(l + 1) * 6 * B].rearrange("p (s b) -> p s b", s=6)))
        dve.after(m_t)
        for l in range(2):
            for s in (1, 4):
                dve.did(V.tensor_scalar(modT[l][:, s, :], modT[l][:, s, :], 1.0, None, ALU.add))
        dve.did(V.tensor_scalar(modB[1][:, :, 2, :], modB[1][:, :, 2, :], 1.0, None, ALU.add))
        for l in range(2):
            for k, s in enumerate((0, MOD_ROWS[l] - 1)):
                g = modB[l][:, :, s, :]
                m = dve.did(V.tensor_scalar(signs[:, k, :, :], g, 0.0, 2.0, ALU.is_ge, ALU.mult))
                neg = gate_neg[:, k, :, :]
                dve.after(dve.did(V.tensor_scalar(neg, g, -1.0, 0.25, ALU.mult, ALU.max)))
                m = dve.did(V.tensor_tensor(g, g, neg, ALU.max))
                dve.after(m)
                m = dve.did(V.scalar_tensor_tensor(g, signs[:, k, :, :], -1.0, g, ALU.add, ALU.mult))
                dve.after(m)

        dve.after(dve.did(V.tensor_tensor(lam_p[:, :, :], lam_in[:, 0::2, :], lam_in[:, 1::2, :], ALU.mult)))
        m = dve.did(V.tensor_reduce(lam_s[:, :], lam_p[:, :, :], AX.X, ALU.add))
        act.after(m)
        m = act.did(A.activation(lam_s[:, :], lam_s[:, :], ACT.Exp))
        dve.after(m)
        m = dve.did(V.tensor_tensor(lam_s[:, 0:1], lam_s[:, 1:2], lam_s[:, 0:1], ALU.subtract))
        dve.did(V.memset(lam_row[:, 0, :], 1.0 - LAMBDA_INIT))
        dve.did(V.memset(lam_row[:, 1, :], -LAMBDA_INIT))
        dve.after(dve.now())
        dve.did(V.tensor_scalar(lam_row[:, 1, :], lam_row[:, 1, :], lam_s[:, 0:1], 1.0 - LAMBDA_INIT, ALU.add, ALU.mult))

        for o in range(ORDER):
            for f in range(3):
                for c in range(2):
                    for kt in range(TAPS // P):
                        last = T.matmul(bank[5 + o][:, ((f * 2 + c) % 4) * D:((f * 2 + c) % 4 + 1) * D] if f < 2 else
                                        bank[7][:, (o * 2 + c) * D:(o * 2 + c + 1) * D],
                                        c_filt[:, f, kt, c * P:(c + 1) * P], taps[:, o, kt, :],
                                        start=(kt == 0), stop=(kt == TAPS // P - 1))
        m = pe.did(last)
        dve.after(m)
        for o in range(ORDER):
            dve.did(V.tensor_copy(filt[:, o, 0:2, :, :], bank[5 + o][:, :].rearrange("p (f c d) -> p f c d", f=2, c=2)))
            dve.did(V.tensor_copy(filt[:, o, 2, :, :], bank[7][:, o * 2 * D:(o + 1) * 2 * D].rearrange("p (c d) -> p c d", c=2)))
        m_filt = dve.now()

        pe.after(m_filt)
        for ph in range(2):
            for h in range(PH):
                r = slice(PN * (h % 2), PN * (h % 2) + PN)
                c = ph * 2 + h // 2
                last = T.matmul(bank[5 + h % 2][:, (ph * PH + h) // 2 * KEYS:((ph * PH + h) // 2 + 1) * KEYS],
                                w_q[r, c, :], keysT[r, c, :], start=True, stop=True)
        m = pe.did(last)
        dve.after(m)
        for h2 in range(2):
            dve.did(V.tensor_copy(msim[:, 0, h2::2, :], bank[5 + h2][:, 0:2 * KEYS].rearrange("p (h k) -> p h k", h=2)))
            dve.did(V.tensor_copy(msim[:, 1, h2::2, :], bank[5 + h2][:, 2 * KEYS:4 * KEYS].rearrange("p (h k) -> p h k", h=2)))
        dve.after(dve.now())
        for h in range(PH):
            dve.did(V.tensor_tensor(mpair[:, h, :, :],
                                    msim[:, 0, h, 0:XROWS].unsqueeze(2).broadcast_to([P, XROWS, KEYS]),
                                    msim[:, 1, h, :].unsqueeze(1).broadcast_to([P, XROWS, KEYS]), ALU.add))

        ew2T = wqkT[:, 0, :, :].rearrange("p h d -> p (h d)").rearrange("p (e k) -> p e k", e=E1)
        xb2, xb3, xp, xe = (carve(1, "setup", [P, NROT, 2, D]) for _ in range(4))
        norm = sb("xm_norm", [P, NROT])
        normall = sb("xm_normall", [P, NROT])
        over = sb("xm_over", [P, MAX_SQUARINGS, NROT])
        keep = sb("xm_keep", [P, MAX_SQUARINGS, NROT])
        steps = sb("xm_steps", [P, NROT])
        onehot = sb("xm_onehot", [P, NROT, MAX_SQUARINGS + 1])
        scale = sb("xm_scale", [P, NROT])

        def tiles(ap):
            return ap.rearrange("p (t d) -> p t d", t=NT)

        def folded_scores():
            pe.after(m_layer1)
            dve.after(m_layer1)
            act.after(m_layer1)
            pool.after(m_layer1)
            freed = [None] * 3
            for j in range(2 * H1 // 4):
                if freed[j % 3]:
                    pe.after(freed[j % 3])
                mp, heads = j % 2, slice(4 * (j // 2), 4 * (j // 2) + 4)
                r = slice(DH * mp, DH * mp + DH)
                for n in range(4):
                    last = T.matmul(bank[3 + j % 3][:, n * D:(n + 1) * D], wqkT[r, 0, heads, :][:, n, :], wqkT[r, 1, heads, :][:, n, :],
                                    start=True, stop=True)
                m = pe.did(last)
                yield
                act.after(m)
                freed[j % 3] = act.did(A.activation(mqk[:, :, mp, :][:, heads, :], tiles(bank[3 + j % 3][:, :]),
                                                    ACT.Copy, scale=DH ** -0.5))
            layer1_in.after(m)
            layer1_in.did(nc.sync.dma_start(ew2T, a["ew2T"].rearrange("e m k -> m e k")))

        def rotations():
            m = dve.did(V.tensor_reduce(norm[:, :], xb[:, :, 0, :], AX.X, ALU.add, apply_absolute_value=True))
            pool.after(m)
            m = pool.did(G.partition_all_reduce(normall[:, :], norm[:, :], P, MAX_REDUCE))
            yield
            dve.after(m)
            dve.after(dve.did(V.tensor_tensor(over[:, :, :], normall[:, :].unsqueeze(1).broadcast_to([P, MAX_SQUARINGS, NROT]),
                                              small[:, 80:96].unsqueeze(2).broadcast_to([P, MAX_SQUARINGS, NROT]), ALU.is_gt)))
            dve.did(V.tensor_scalar(keep[:, :, :], over[:, :, :], -1.0, 1.0, ALU.mult, ALU.add))
            dve.after(dve.did(V.tensor_reduce(steps[:, :], over[:, :, :].rearrange("p k g -> p g k"), AX.X, ALU.add)))
            yield
            dve.after(dve.did(V.tensor_tensor(onehot[:, :, :], steps[:, :].unsqueeze(2).broadcast_to([P, NROT, MAX_SQUARINGS + 1]),
                                              small[:, 113:130].unsqueeze(1).broadcast_to([P, NROT, MAX_SQUARINGS + 1]), ALU.is_equal)))
            dve.after(dve.did(V.tensor_tensor(onehot[:, :, :], onehot[:, :, :],
                                              small[:, 96:113].unsqueeze(1).broadcast_to([P, NROT, MAX_SQUARINGS + 1]), ALU.mult)))
            dve.after(dve.did(V.tensor_reduce(scale[:, :], onehot[:, :, :], AX.X, ALU.add)))
            yield
            for i in range(NROT):
                m = dve.did(V.tensor_scalar(xb[:, i, :, :], xb[:, i, :, :], scale[:, i:i + 1], None, ALU.mult))
            yield

            def products(left, right, ready):
                pe.after(ready)
                for i in range(NROT):
                    for side in range(2):
                        last = T.matmul(bank[i][:, side * D:(side + 1) * D], left[:, i, 1 - side, :], right[:, i, side, :],
                                        start=True, stop=True)
                return pe.did(last)

            def product(i):
                return bank[i][:, 0:2 * D].rearrange("p (s d) -> p s d", s=2)

            def flat(t):
                return t[:, :, :, :].rearrange("p i s d -> p (i s) d")

            for dst, left in ((xb2, xb), (xb3, xb2)):
                done = products(left, xb, m)
                yield
                dve.after(done)
                for i in range(NROT):
                    m = dve.did(V.tensor_copy(dst[:, i, :, :], product(i)))
                yield
            dve.after(m)

            def poly(dst, c0, c1, c2):
                m1 = dve.did(V.tensor_scalar(flat(dst), flat(xb), c1, None, ALU.mult))
                yield
                dve.after(m1)
                m2 = dve.did(V.scalar_tensor_tensor(flat(dst), flat(xb2), c2, flat(dst), ALU.mult, ALU.add))
                yield
                dve.after(m2)
                for j in range(2 * NROT):
                    v = flat(dst)[:, j, :]
                    m3 = dve.did(V.scalar_tensor_tensor(v, ident[:, :], c0, v, ALU.mult, ALU.add))
                yield
                return m3

            m = yield from poly(xp, *TAYLOR[6:9])
            done = products(xb3, xp, m)
            m = yield from poly(xe, *TAYLOR[3:6])
            dve.after(m, done)
            for i in range(NROT):
                m = dve.did(V.tensor_tensor(xe[:, i, :, :], xe[:, i, :, :], product(i), ALU.add))
            yield
            done = products(xb3, xe, m)
            m = yield from poly(xp, *TAYLOR[0:3])
            dve.after(m, done)
            for i in range(NROT):
                m = dve.did(V.tensor_tensor(xe[:, i, :, :], xp[:, i, :, :], product(i), ALU.add))
            yield

            kept = [xp, xb2]
            for k in range(MAX_SQUARINGS):
                old = kept[k % 2]
                pool.after(m)
                m_old = pool.did(G.tensor_tensor(old[:, :, :, :].rearrange("p i s d -> p i (s d)"),
                                                 xe[:, :, :, :].rearrange("p i s d -> p i (s d)"),
                                                 keep[:, k, :].unsqueeze(2).broadcast_to([P, NROT, 2 * D]), ALU.mult))
                done = products(xe, xe, m)
                yield
                yield
                dve.after(done, m_old)
                for i in range(NROT):
                    m = dve.did(V.scalar_tensor_tensor(xe[:, i, :, :], product(i), over[:, k, i:i + 1], old[:, i, :, :],
                                                       ALU.mult, ALU.add))
                yield
            rotT, rot = xb3[:, 0, 0, :], xb3[:, 0, 1, :]
            pe.after(m)
            m = pe.did(T.matmul(bank[0][:, 0:D], xe[:, 1, 0, :], xe[:, 0, 1, :], start=True, stop=True))
            yield
            dve.after(m)
            m = dve.did(V.tensor_copy(rotT, bank[0][:, 0:D]))
            yield
            pe.after(m)
            m = pe.did(T.matmul(bank[0][:, 0:D], rotT, xe[:, 2, 0, :], start=True, stop=True))
            yield
            dve.after(m)
            m = dve.did(V.tensor_copy(rot, bank[0][:, 0:D]))
            yield
            pe.after(m, layer1_in.now())
            for j in range(E1 * HC // 4):
                for n in range(4):
                    e, c = (j * 4 + n) // HC, n % HC
                    last = T.matmul(bank[1 + j][:, n * D:(n + 1) * D], ew2T[:, e, c * P:(c + 1) * P], rot, start=True, stop=True)
                m = pe.did(last)
                yield
                dve.after(m)
                dve.did(V.tensor_copy(ew2R[:, 2 * j:2 * j + 2, :, :], bank[1 + j][:, :].rearrange("p (e c d) -> p e c d", e=2, c=HC)))
            m = pe.did(T.matmul(bank[5][0:E1, 0:D], eb2T[:, :], rot, start=True, stop=True))
            yield
            dve.after(m)
            dve.did(V.tensor_copy(eb2R[:, :], bank[5][0:E1, 0:D]))

        x1 = sb("x1", [P, NT, D])
        hT0 = sb("hT0", [P, S])
        hT1 = sb("hT1", [P, S])
        attn = sb("attn", [P, NT, D])
        ln = [{"stats": sb(f"stats{l}", [P, NT, 6]), "mv": sb(f"mv{l}", [P, NT, 2]), "rstd": sb(f"rstd{l}", [P, NT]),
               "xhat": sb(f"xhat{l}", [P, NT, D])} for l in range(2)]

        pv = carve(0, "conv", [P, NT, ORDER + 1, D])
        fold_s = carve(0, "conv", [P, 2, 2, D])
        spec = carve(0, "conv", [P, 2, 2, D])
        spec_t = carve(0, "conv", [P, 2, 2, D])
        spec_o = carve(0, "conv", [P, 2, 2, D])

        ex = lambda shape: carve(0, "experts", shape)
        gT = ex([P, I_UP // P, S])
        sim = ex([P, 2 * PH, KEYS])
        gd = ex([P, EXPERTS])
        pair = ex([P, PH, TOP, TOP])
        pair_r = ex([P, PH, TOP * TOP])
        chosen = ex([P, PH, TOP, TOP])
        eqx = ex([P, PH, XROWS, TOP])
        ydiff = ex([P, PH, KEYS, TOP])
        epair = ex([P, PH, TOP * TOP])
        zpast = ex([P, PH, TOP * TOP])
        wsum = ex([P, EXPERTS])
        wT = gdT = sb("wT", [P, EXPERTS // P, P])
        prob = sb("prob", [P, PH, EXPERTS])
        tops = sb("tops", [P, 2 * PH, TOP])
        topi = sb("topi", [P, 2 * PH, TOP], U32)
        topf = sb("topf", [P, 2 * PH, TOP])
        best = sb("best", [P, PH, TOP])
        negbest = sb("negbest", [P, PH])
        cnt = sb("cnt", [P, PH, TOP])
        yval = sb("yval", [P, PH, TOP])
        code = sb("code", [P, PH, XROWS + KEYS], BF16)
        codeT = sb("codeT", [XROWS + KEYS, PH, P], BF16)
        esum = sb("esum", [P, PH])
        rsum = sb("rsum", [P, PH])
        past = sb("past", [P, PH, TOP])
        wpast = sb("wpast", [P, 1])
        gated = sb("gated", [P, D])

        at = lambda shape: carve(1, "attention", shape)
        TRI = P * NT * (NT + 1) // 2
        aT = [[sb(f"aT{i}{n}", [P, S], F32R) for n in ("hi", "lo")] for i in range(2)]
        vv = [at([P, NT, 2, DH]) for _ in range(2)]
        prb = [at([P, TRI]) for _ in range(2)]
        prbT = [at([P, TRI]) for _ in range(2)]
        negmax = [sb(f"negmax{i}", [P, NT]) for i in range(2)]
        rowsum = [sb(f"rowsum{i}", [P, NT]) for i in range(2)]
        rnorm = [sb(f"rnorm{i}", [P, NT]) for i in range(2)]
        oT = sb("oT", [P, S])
        hTs = [sb(f"hTs{i}", [P, S], F32R) for i in range(2)]

        h1 = carve(1, "mixture", [P, E1 * HC, S])
        res = sb("res", [P, NT, D])
        abel = oT[:, :].rearrange("p (t d) -> p t d", t=NT)
        moe = attn
        logit = sb("logit", [P, NT, E1])
        ltop = sb("ltop", [P, NT, TOP])
        lidx = sb("lidx", [P, NT, TOP], U32)
        lidf = sb("lidf", [P, NT, 2])
        lw = sb("lw", [P, NT, 2])
        wde = sb("wde", [P, 2, NT, E1])
        gdot = sb("gdot", [P, NT, 2])
        gate = sb("gate", [P, NT])

        BANK_S, BANK_T, BO, BM, BANK_0 = bank[0:2], bank[2:4], bank[4], bank[5], bank[6:8]

        def rows(ap):
            return ap.unsqueeze(1).broadcast_to([P, NT, D])

        def layernorm(src, buf):
            stats, mv, rstd, xhat = buf["stats"], buf["mv"], buf["rstd"], buf["xhat"]
            for t in range(NT):
                dve.did(V.bn_stats(stats[:, t, :], src[:, t, :]))
            dve.after(dve.now())
            for t in range(NT):
                dve.did(V.bn_aggr(mv[:, t, :], stats[:, t, :]))
            dve.after(dve.now())
            m = dve.did(V.tensor_scalar(rstd[:, :], mv[:, :, 1], EPS, None, ALU.add))
            pool.after(m)
            m = pool.did(G.tensor_tensor(rstd[:, :], rstd[:, :], small[:, 130:134], ALU.pow))
            yield
            dve.after(m)
            for t in range(NT):
                m = dve.did(V.tensor_scalar(xhat[:, t, :], src[:, t, :], mv[:, t, 0:1], rstd[:, t:t + 1], ALU.subtract, ALU.mult))
            yield
            return m

        def transposed(dst, src, ready, scale_ap, shift_ap, into):
            pe.after(*ready)
            for t in range(NT):
                last = T.transpose(into[:, t * P:(t + 1) * P], src[:, t, :], ident[:, :])
            m = pe.did(last)
            yield
            dve.after(m)
            m = dve.did(V.tensor_scalar(dst[:, :], into[:, :], scale_ap, shift_ap, ALU.mult, ALU.add))
            yield
            return m

        def convolutions(b):
            bf, bi = BANK_0
            m = yield from layernorm(x0, ln[0])
            m = yield from transposed(hT0, ln[0]["xhat"], [m], modT[0][:, 1, bass.ds(b, 1)], modT[0][:, 0, bass.ds(b, 1)], bf)
            pe.after(m)
            freed = [m, m]
            for t in range(NT):
                bk = BANK_0[t % 2]
                pe.after(freed[t % 2])
                m = pe.did(T.matmul(bk[:, 0:3 * D], hT0[:, t * P:(t + 1) * P], proj_w[:, :], start=True, stop=True))
                yield
                dve.after(m)
                freed[t % 2] = dve.did(V.tensor_tensor(pv[:, t, :, :].rearrange("p o d -> p (o d)"), bk[:, 0:3 * D], proj_b[:, :], ALU.add))
            for o in range(ORDER):
                v = pv[:, :, o, :]
                dve.after(dve.now())
                dve.did(V.tensor_tensor(fold_s[:, 0, :, :], v[:, 0:2, :], v[:, 2:4, :], ALU.add))
                m = dve.did(V.tensor_tensor(fold_s[:, 1, :, :], v[:, 0:2, :], v[:, 2:4, :], ALU.subtract))
                yield
                pe.after(m)
                for c in range(4):
                    for kt in range(2):
                        last = T.matmul(bf[:, c * D:(c + 1) * D], c_fwd[:, kt, c * P:(c + 1) * P], fold_s[:, c % 2, kt, :],
                                        start=(kt == 0), stop=(kt == 1))
                m = pe.did(last)
                yield
                act.after(m)
                m = act.did(A.activation(spec[:, :, :, :].rearrange("p r c d -> p (r c d)"), bf[:, :], ACT.Copy))
                yield
                dve.after(m)
                re, im = spec[:, 0, :, :], spec[:, 1, :, :]
                fa, fb, fd = (filt[:, o, i, :, :] for i in range(3))
                dve.did(V.tensor_tensor(spec_o[:, 0, :, :], re, fa, ALU.mult))
                dve.did(V.tensor_tensor(spec_t[:, 0, :, :], im, fb, ALU.mult))
                dve.did(V.tensor_tensor(spec_o[:, 1, :, :], re, fb, ALU.mult))
                m = dve.did(V.tensor_tensor(spec_t[:, 1, :, :], im, fd, ALU.mult))
                yield
                dve.after(m)
                dve.did(V.tensor_tensor(spec_o[:, 0, :, :], spec_o[:, 0, :, :], spec_t[:, 0, :, :], ALU.subtract))
                m = dve.did(V.tensor_tensor(spec_o[:, 1, :, :], spec_o[:, 1, :, :], spec_t[:, 1, :, :], ALU.add))
                yield
                pe.after(m)
                for odd in range(2):
                    for t in range(2):
                        for part in range(2):
                            last = T.matmul(bi[:, (odd * 2 + t) * D:(odd * 2 + t + 1) * D], c_inv[:, part * 2 + odd, t * P:(t + 1) * P],
                                            spec_o[:, part, odd, :], start=(part == 0), stop=(part == 1))
                    m = pe.did(last)
                yield
                act.after(m)
                m = act.did(A.activation(spec_t[:, 0, :, :], tiles(bi[:, :])[:, 0:2, :], ACT.Copy))
                yield
                dve.after(m)
                dve.did(V.tensor_tensor(spec[:, 0, :, :], spec_t[:, 0, :, :], tiles(bi[:, :])[:, 2:4, :], ALU.add))
                m = dve.did(V.tensor_tensor(spec[:, 1, :, :], spec_t[:, 0, :, :], tiles(bi[:, :])[:, 2:4, :], ALU.subtract))
                yield
                dve.after(m)
                m = dve.did(V.tensor_tensor(pv[:, :, o + 1, :], spec[:, :, :, :].rearrange("p h t d -> p (h t) d"), pv[:, :, o + 1, :], ALU.mult))
                yield
            dve.after(m)
            dve.after(dve.did(V.tensor_tensor(pv[:, :, 0, :], pv[:, :, ORDER, :], rows(modB[0][:, b, 0, :]), ALU.mult)))
            dve.after(dve.did(V.tensor_tensor(x0[:, :, :], x0[:, :, :], pv[:, :, 0, :], ALU.add)))
            yield

        def feed_forward(b):
            b6, b7 = BANK_0
            m = yield from layernorm(x0, ln[0])
            m_hT = yield from transposed(hT0, ln[0]["xhat"], [m], modT[0][:, 4, bass.ds(b, 1)], modT[0][:, 3, bass.ds(b, 1)], b6)
            pe.after(m_hT)
            freed = [m_hT, m_hT]
            for c in range(I_UP // P):
                bk = BANK_0[c % 2]
                pe.after(freed[c % 2])
                m = pe.did(T.matmul(bk[:, :], w_up[:, c * P:(c + 1) * P], hT0[:, :], start=True, stop=True))
                yield
                act.after(m)
                freed[c % 2] = m_gT = act.did(A.activation(gT[:, c, :], bk[:, :], ACT.Silu))
            for t in range(NT):
                tok = slice(t * P, (t + 1) * P)
                pe.after(dve.now(), act.now())
                m_s = pe.did(T.matmul(b6[:, :], hT0[:, tok], msim[:, :, :, :].rearrange("p a h k -> p (a h k)"), start=True, stop=True))
                m_g = pe.did(T.matmul(b7[:, :], hT0[:, tok], downT[:, :], start=True, stop=True))
                yield
                act.after(m_s, dve.now())
                m_sim = act.did(A.activation(sim[:, :, :].rearrange("p g k -> p (g k)"), b6[:, :], ACT.Copy))
                act.after(m_g)
                m_gd = act.did(A.activation(gd[:, :], b7[:, :], ACT.Copy))
                yield
                dve.after(m_sim)
                for g in range(2 * PH):
                    dve.did(V.max(tops[:, g, :], sim[:, g, :]))
                yield
                dve.after(dve.now())
                for g in range(2 * PH):
                    dve.did(V.max_index(topi[:, g, :], tops[:, g, :], sim[:, g, :]))
                m = dve.did(V.tensor_tensor(pair[:, :, :, :], tops[:, 0:PH, :].unsqueeze(3).broadcast_to([P, PH, TOP, TOP]),
                                            tops[:, PH:, :].unsqueeze(2).broadcast_to([P, PH, TOP, TOP]), ALU.add))
                yield
                dve.after(m)
                dve.did(V.tensor_copy(topf[:, :, :], topi[:, :, :]))
                pflat = pair[:, :, :, :].rearrange("p h a b -> p h (a b)")
                for h in range(PH):
                    dve.did(V.max(best[:, h, :], pflat[:, h, :]))
                dve.after(dve.now())
                m_yv = dve.did(V.scalar_tensor_tensor(yval[:, :, :], topf[:, PH:, :], 32.0,
                                               small[:, 8:16].unsqueeze(1).broadcast_to([P, PH, TOP]), ALU.mult, ALU.add))
                m_nb = dve.did(V.tensor_scalar(negbest[:, :], best[:, :, 0], -1.0, None, ALU.mult))
                yield
                for h in range(PH):
                    dve.did(V.match_replace(pair_r[:, h, :], best[:, h, :], pflat[:, h, :], -3e38))
                pool.after(m_yv)
                for h in range(PH):
                    m_yd = pool.did(G.tensor_tensor(ydiff[:, h, :, :], yval[:, h, :].unsqueeze(1).broadcast_to([P, KEYS, TOP]),
                                                    small[:, 16:80].unsqueeze(2).broadcast_to([P, KEYS, TOP]), ALU.subtract))
                act.after(m_nb)
                for h in range(PH):
                    m_ep = act.did(A.activation(epair[:, h, :], pflat[:, h, :], ACT.Exp, bias=negbest[:, h:h + 1]))
                yield
                dve.after(dve.now())
                chf = chosen[:, :, :, :].rearrange("p h a b -> p h (a b)")
                m_ch = dve.did(V.tensor_tensor(chf, pair_r[:, :, :], pflat, ALU.is_lt))
                dve.after(m_ch)
                m = dve.did(V.tensor_reduce(cnt[:, :, :], chosen[:, :, :, :], AX.X, ALU.add))
                for h in range(PH):
                    dve.did(V.tensor_tensor(eqx[:, h, :, :], topf[:, h, :].unsqueeze(1).broadcast_to([P, XROWS, TOP]),
                                            small[:, 0:XROWS].unsqueeze(2).broadcast_to([P, XROWS, TOP]), ALU.is_equal))
                yield
                dve.after(dve.now())
                m = dve.did(V.tensor_tensor(eqx[:, :, :, :], eqx[:, :, :, :],
                                            cnt[:, :, :].unsqueeze(2).broadcast_to([P, PH, XROWS, TOP]), ALU.mult))
                dve.after(m_ep)
                dve.did(V.tensor_scalar(past[:, :, :], topf[:, 0:PH, :], float(XROWS), None, ALU.is_ge))
                dve.did(V.tensor_tensor(epair[:, :, :], epair[:, :, :], chf, ALU.mult))
                dve.after(dve.now())
                m = dve.did(V.tensor_reduce(esum[:, :], epair[:, :, :], AX.X, ALU.add))
                dve.did(V.tensor_tensor(zpast[:, :, :].rearrange("p h (a b) -> p h a b", a=TOP),
                                        epair[:, :, :].rearrange("p h (a b) -> p h a b", a=TOP),
                                        past[:, :, :].unsqueeze(3).broadcast_to([P, PH, TOP, TOP]), ALU.mult))
                yield
                dve.after(m)
                dve.did(V.reciprocal(rsum[:, :], esum[:, :]))
                dve.after(dve.now())
                m_zp = dve.did(V.tensor_tensor(zpast[:, :, :], zpast[:, :, :],
                                               rsum[:, :].unsqueeze(2).broadcast_to([P, PH, TOP * TOP]), ALU.mult))
                yield
                with nc.allow_low_precision(reason="counts and ranks up to 8 are exact; what is larger stays above 8"):
                    dve.did(V.tensor_reduce(code[:, :, 0:XROWS], eqx[:, :, :, :], AX.X, ALU.add))
                    dve.after(m_yd)
                    for h2 in range(2):
                        m_code = dve.did(V.tensor_reduce(code[:, 2 * h2:2 * h2 + 2, XROWS:], ydiff[:, 2 * h2:2 * h2 + 2, :, :], AX.X,
                                                         ALU.min, apply_absolute_value=True))
                        yield
                pe.after(m_code, m_gd)
                psT = b6[0:XROWS + KEYS, 0:PH * P // 2].bitcast(BF16).rearrange("q (h t) -> q h t", h=PH)
                for h in range(PH):
                    last = T.transpose(psT[:, h, :], code[:, h, :], identb[:, :])
                m = pe.did(last)
                yield
                act.after(m)
                m_ct = act.did(A.activation(codeT[:, :, :], psT, ACT.Copy))
                m_l_free, m_d_free = m_gd, m_ct
                yield
                for h in range(PH):
                    pe.after(m_l_free)
                    m_l = pe.did(T.matmul(b7[:, :], hT0[:, tok], mpair[:, h, :, :].rearrange("p i j -> p (i j)"), start=True, stop=True))
                    pe.after(m_ct, m_d_free)
                    m_d = pe.did(T.matmul(b6[:, :], codeT[:, h, :], sel[:, :], start=True, stop=True))
                    yield
                    act.after(m_l)
                    m_l_free = m_p = act.did(A.activation(prob[:, h, :], b7[:, :], ACT.Exp, bias=negbest[:, h:h + 1]))
                    yield
                    dve.after(m_p, m_d, m_gd)
                    m_d_free = dve.did(V.scalar_tensor_tensor(prob[:, h, :], b6[:, :], 0.0, prob[:, h, :], ALU.is_ge, ALU.mult))
                    dve.after(m_d_free)
                    m_z = dve.did(V.scalar_tensor_tensor(prob[:, h, :], prob[:, h, :], rsum[:, h:h + 1], gd[:, :], ALU.mult, ALU.mult))
                    yield
                act.after(m_z, m_zp)
                pflat_all = prob[:, :, :].rearrange("p h e -> p (h e)")
                for half in range(2):
                    m_w = act.did(A.activation(pflat_all[:, half * 2 * EXPERTS:(half + 1) * 2 * EXPERTS],
                                               pflat_all[:, half * 2 * EXPERTS:(half + 1) * 2 * EXPERTS], ACT.Silu))
                m_wp = act.did(A.activation(epair[:, :, :].rearrange("p h c -> p (h c)"), zpast[:, :, :].rearrange("p h c -> p (h c)"), ACT.Silu,
                                            scale=gd[:, EXPERTS - 1:EXPERTS], accum_out=wpast[:, 0:1]))
                yield
                pool.after(m_w)
                pool.after(pool.did(G.tensor_tensor(prob[:, 0:2, :], prob[:, 0:2, :], prob[:, 2:4, :], ALU.add)))
                pool.after(pool.did(G.tensor_tensor(wsum[:, :], prob[:, 0, :], prob[:, 1, :], ALU.add)))
                pool.after(m_wp)
                m_ws = pool.did(G.tensor_tensor(wsum[:, EXPERTS - 1:EXPERTS], wsum[:, EXPERTS - 1:EXPERTS], wpast[:, 0:1], ALU.add))
                pe.after(m_d_free, m_gT)
                for c in range(4):
                    T.matmul(b6[:, 0:D], gT[:, c, tok], w_down[:, c, :], start=(c == 0), stop=False)
                yield
                yield
                yield
                pe.after(m_ws, m_l_free)
                for c in range(4):
                    last = T.transpose(b7[:, c * P:(c + 1) * P], wsum[:, c * P:(c + 1) * P], ident[:, :])
                m = pe.did(last)
                yield
                dve.after(m)
                m_wT = dve.did(V.tensor_copy(wT[:, :, :], b7[:, :].rearrange("p (c t) -> p c t", c=4)))
                yield
                pe.after(m_wT)
                for c in range(4):
                    last = T.matmul(b6[:, 0:D], wT[:, c, :], up_e[:, c, :], start=False, stop=(c == 3))
                m_o = pe.did(last)
                yield
                dve.after(m_o)
                dve.after(dve.did(V.tensor_tensor(gated[:, :], b6[:, 0:D], modB[0][:, b, 1, :], ALU.mult)))
                dve.after(dve.did(V.tensor_tensor(x0[:, t, :], x0[:, t, :], gated[:, :], ALU.add)))
                yield

        def read_batch(b):
            x_in.after(pool.now())
            m_x = x_in.did(nc.sync.dma_start(x0[:, :, :], a["x"][b].rearrange("(t p) d -> p t d", p=P)))
            yield
            yield
            dve.after(m_x)

        def layer0(b):
            yield from convolutions(b)
            yield from feed_forward(b)
            m = yield from layernorm(x0, ln[0])
            yield from transposed(hT0, ln[0]["xhat"], [m], modT[1][:, 1, bass.ds(b, 1)], modT[1][:, 0, bass.ds(b, 1)], BANK_0[0])

        def attention():
            p_at = [0, P, 3 * P, 6 * P]
            s_of = [BANK_S[1][:, 0:P], BANK_S[0][:, 0:2 * P], BANK_S[1][:, P:4 * P], BANK_S[0][:, :]]
            pt_at = [0, 4 * P, 8 * P, 7 * P]
            t_bank, t_off = [0, 1, 0, 1], [0, 0, 0, 3 * P]
            st = {}

            def been(*keys):
                return [st[k] for k in keys if k in st]

            def project_map(u):
                pe.after(*been("bm_free"))
                m = pe.did(T.matmul(BM[:, :], mqk[:, u // 2, u % 2, :], hT1[:, :], start=True, stop=True))
                yield
                hi, lo = aT[u % 2]
                act.after(m, *been(("scores", u % 2)))
                m = act.did(A.activation(hi[:, :], BM[:, :], ACT.Copy))
                dve.after(m)
                st["a", u % 2] = st["bm_free"] = dve.did(V.tensor_tensor(lo[:, :], BM[:, :], hi[:, :].bitcast(F32), ALU.subtract))

            def project_v(h):
                par = h % 2
                pe.after(*been("bm_free"))
                for t in range(NT):
                    last = T.matmul(BM[:, t * P:(t + 1) * P], hT1[:, t * P:(t + 1) * P], wv[:, h, :], start=True, stop=True)
                m = pe.did(last)
                yield
                dve.after(m, *been(("pv", 0), ("pv", 1)))
                st["v", par] = st["bm_free"] = dve.did(V.tensor_tensor(
                    vv[par][:, :, :, :].rearrange("p t m c -> p t (m c)"), tiles(BM[:, :]),
                    lam_row[:, :, :].rearrange("p m c -> p (m c)").unsqueeze(1).broadcast_to([P, NT, 2 * DH]), ALU.mult))

            def scores(u, order):
                buf = u % 2
                a_hi, a_lo = aT[buf]
                pe.after(st["a", buf])
                ready = {}
                for qc in order:
                    pe.after(*been(("bank_s", 1 if qc in (0, 2) else 0)))
                    for n, (left, right) in enumerate(((a_hi, hTs[0]), (a_hi, hTs[1]), (a_lo, hTs[0]))):
                        T.matmul(s_of[qc], left[:, qc * P:(qc + 1) * P], right[:, 0:(qc + 1) * P], start=(n == 0), stop=False)
                    ready[qc] = pe.did(T.matmul(s_of[qc][:, qc * P:(qc + 1) * P], identb[:, :], mask[:, :], start=False, stop=True))
                    st["scores", buf] = ready[qc]
                if 2 in ready:
                    ready[2] = ready[0]
                for qc in order:
                    dve.after(ready[qc], *been(("sums", buf)))
                    ready[qc] = dve.did(V.tensor_reduce(negmax[buf][:, qc:qc + 1], s_of[qc], AX.X, ALU.max, negate=True))
                if 2 in ready:
                    ready[2] = ready[0]
                for qc in order:
                    act.after(ready[qc], *been(("tr", buf)))
                    m = act.did(A.activation(prb[buf][:, p_at[qc]:p_at[qc] + (qc + 1) * P], s_of[qc], ACT.Exp,
                                             bias=negmax[buf][:, qc:qc + 1], accum_out=rowsum[buf][:, qc:qc + 1]))
                    st["bank_s", 1 if qc in (0, 2) else 0] = m
                st["exp", buf] = m

            def normalise(u):
                buf = u % 2
                dve.after(st["exp", buf])
                m = dve.did(V.reciprocal(rnorm[buf][:, :], rowsum[buf][:, :]))
                pool.after(m)
                for qc in range(NT):
                    v = prb[buf][:, p_at[qc]:p_at[qc] + (qc + 1) * P]
                    m = pool.did(G.tensor_scalar(v, v, rnorm[buf][:, qc:qc + 1], 1.0, ALU.mult, ALU.mult))
                st["norm", buf] = m

            def turn(u, kcs, evac):
                buf = u % 2
                bk = t_bank[kcs[0]]
                pe.after(st["norm", buf], *been(("bank_t", bk)))
                for kc in kcs:
                    for qc in range(kc, NT):
                        c = t_off[kc] + (qc - kc) * P
                        last = T.transpose(BANK_T[bk][:, c:c + P], prb[buf][:, p_at[qc] + kc * P:p_at[qc] + (kc + 1) * P], ident[:, :])
                st["tr", buf] = m = pe.did(last)
                n = sum(NT - kc for kc in kcs) * P
                dst, src = prbT[buf][:, pt_at[kcs[0]]:pt_at[kcs[0]] + n], BANK_T[bk][:, 0:n]
                evac.after(m, *been(("pv", buf)))
                st["bank_t", bk] = st["pt", kcs[0]] = evac.did(V.tensor_copy(dst, src) if evac is dve else A.activation(dst, src, ACT.Copy))

            def apply(u):
                par, mp, buf = u // 2 % 2, u % 2, u % 2
                rows_o = slice(DH * par, DH * par + DH)
                pe.after(st["v", par], *been(("o", par)))
                for n, kc in enumerate((0, 1, 3, 2)):
                    pe.after(*been(("pt", kc)))
                    last = T.matmul(BO[rows_o, kc * P:S], vv[par][:, kc, mp, :], prbT[buf][:, pt_at[kc]:pt_at[kc] + (NT - kc) * P],
                                    start=(n == 0 and mp == 0), stop=(n == NT - 1 and mp == 1))
                st["pv", buf] = m = pe.did(last)
                if mp == 1:
                    act.after(m, *been("wo"))
                    st["o", par] = act.did(A.activation(oT[rows_o, :], BO[rows_o, :], ACT.Copy))

            def project_out(g):
                pe.after(st["o", 0], st["o", 1], st["bm_free"])
                for t in range(NT):
                    last = T.matmul(BM[:, t * D:(t + 1) * D], oT[:, t * P:(t + 1) * P], wo[:, g, :], start=True, stop=True)
                st["wo"] = m = pe.did(last)
                yield
                dve.after(m)
                if g == 0:
                    st["bm_free"] = dve.did(V.tensor_copy(attn[:, :, :], tiles(BM[:, :])))
                else:
                    st["bm_free"] = dve.did(V.tensor_tensor(attn[:, :, :], attn[:, :, :], tiles(BM[:, :]), ALU.add))

            maps = 2 * H1
            yield from project_map(0)
            yield from project_v(0)
            yield from project_map(1)
            scores(0, (3, 2, 0))
            yield
            scores(0, (1,))
            normalise(0)
            yield
            for u in range(maps):
                nxt = u // 2 + 1
                if u + 1 < maps:
                    scores(u + 1, (3, 2, 0))
                    yield
                turn(u, (0,), dve)
                turn(u, (1, 3), act)
                yield
                if u + 2 < maps:
                    yield from project_map(u + 2)
                if u + 1 < maps:
                    scores(u + 1, (1,))
                    yield
                turn(u, (2,), dve)
                if u + 1 < maps:
                    normalise(u + 1)
                yield
                if u % 4 == 0 and u:
                    yield from project_out(u // 4 - 1)
                apply(u)
                yield
                if nxt < H1 and u % 2:
                    yield from project_v(nxt)
            yield from project_out(PAIRS - 1)
            yield

        def mixture(b):
            xhat = ln[1]["xhat"]
            wdT = xhat[:, :, :].rearrange("p t d -> p (t d)")[0:E1, :]
            m = yield from layernorm(x1, ln[1])
            dve.after(m, out_stored.now())
            dve.after(dve.did(V.tensor_tensor(res[:, :, :], xhat[:, :, :], rows(modB[1][:, b, 2, :]), ALU.mult)))
            dve.after(dve.did(V.tensor_tensor(res[:, :, :], res[:, :, :], rows(modB[1][:, b, 1, :]), ALU.add)))
            yield
            m = yield from layernorm(res, ln[1])
            m_hT = yield from transposed(hT1, xhat, [m], gammaT[:, 0:1], gammaT[:, 1:2], BM)
            pe.after(m_hT)
            for t in range(NT):
                T.matmul(BO[:, t * D:(t + 1) * D], hT1[:, t * P:(t + 1) * P], abel_w[:, :], start=True, stop=True)
            for t in range(NT):
                last = T.matmul(BM[:, t * E1:(t + 1) * E1], hT1[:, t * P:(t + 1) * P], gate_w[:, :], start=True, stop=True)
            m_lg = pe.did(last)
            m_h1 = []

            def expand(j):
                bk = bank[j % 4]
                if j >= 4:
                    pe.after(m_h1[j - 4])
                m = pe.did(T.matmul(bk[:, :], ew1[:, j // HC, (j % HC) * P:(j % HC + 1) * P], hT1[:, :], start=True, stop=True))
                act.after(m)
                m_h1.append(act.did(A.activation(h1[:, j, :], bk[:, :], ACT.Gelu, bias=eb1T[:, j:j + 1])))

            expand(0)
            expand(1)
            yield
            dve.after(m_lg)
            m_ab = dve.did(V.tensor_tensor(abel[:, :, :], tiles(BO[:, :]), rows(abel_b[:, :]), ALU.add))
            dve.after(dve.did(V.tensor_tensor(logit[:, :, :], BM[:, 0:NT * E1].rearrange("p (t e) -> p t e", t=NT),
                                              gate_b[:, :].unsqueeze(1).broadcast_to([P, NT, E1]), ALU.add)))
            expand(2)
            expand(3)
            yield
            for t in range(NT):
                dve.did(V.max(ltop[:, t, :], logit[:, t, :]))
            dve.after(dve.now())
            for t in range(NT):
                dve.did(V.max_index(lidx[:, t, :], ltop[:, t, :], logit[:, t, :]))
            dve.did(V.tensor_tensor(lw[:, :, 1], ltop[:, :, 1], ltop[:, :, 0], ALU.subtract))
            dve.after(dve.now())
            m = dve.did(V.tensor_copy(lidf[:, :, :], lidx[:, :, 0:2]))
            for j in range(4, E1 * HC):
                expand(j)
                if j % 2:
                    yield
            act.after(m_ab)
            m_abel = act.did(A.activation(abel[:, :, :], abel[:, :, :], ACT.Gelu))
            act.after(m)
            m = act.did(A.activation(lw[:, :, 1], lw[:, :, 1], ACT.Exp))
            yield
            dve.after(m)
            dve.after(dve.did(V.tensor_scalar(lw[:, :, 0], lw[:, :, 1], 1.0, None, ALU.add)))
            dve.after(dve.did(V.reciprocal(lw[:, :, 0], lw[:, :, 0])))
            dve.after(dve.did(V.tensor_tensor(lw[:, :, 1], lw[:, :, 1], lw[:, :, 0], ALU.mult)))
            for k in range(K1):
                dve.did(V.tensor_tensor(wde[:, k, :, :], lidf[:, :, k].unsqueeze(2).broadcast_to([P, NT, E1]),
                                        small[:, 134:142].unsqueeze(1).broadcast_to([P, NT, E1]), ALU.is_equal))
            dve.after(dve.now())
            for k in range(K1):
                dve.did(V.tensor_tensor(wde[:, k, :, :], wde[:, k, :, :],
                                        lw[:, :, k].unsqueeze(2).broadcast_to([P, NT, E1]), ALU.mult))
            dve.after(dve.now())
            m = dve.did(V.tensor_tensor(wde[:, 0, :, :], wde[:, 0, :, :], wde[:, 1, :, :], ALU.add))
            pe.after(m)
            for t in range(NT):
                last = T.transpose(BM[0:E1, t * P:(t + 1) * P], wde[:, 0, t, :], ident[:, :])
            m = pe.did(last)
            yield
            dve.after(m)
            m_wdT = dve.did(V.tensor_copy(wdT, BM[0:E1, :]))
            pe.after(m_wdT, *m_h1[-4:])
            freed = [None, None]
            for t in range(NT):
                last = T.matmul(BM[:, t * D:(t + 1) * D], wdT[:, t * P:(t + 1) * P], eb2R[:, :], start=True, stop=True)
            m_b = pe.did(last)

            def contract(t):
                if freed[t % 2]:
                    pe.after(freed[t % 2])
                for e in range(E1):
                    for c in range(HC):
                        last = T.matmul(bank[t % 2 * 2 + e // 4][:, (e % 4) * D:(e % 4 + 1) * D], h1[:, e * HC + c, t * P:(t + 1) * P],
                                        ew2R[:, e, c, :], start=(c == 0), stop=(c == HC - 1))
                return pe.did(last)

            m_e = contract(0)
            yield
            dve.after(m_b)
            dve.after(dve.did(V.tensor_copy(moe[:, :, :], tiles(BM[:, :]))))
            for t in range(NT):
                m_next = contract(t + 1) if t + 1 < NT else None
                dve.after(m_e)
                for e in range(E1):
                    m = dve.did(V.scalar_tensor_tensor(moe[:, t, :], bank[t % 2 * 2 + e // 4][:, (e % 4) * D:(e % 4 + 1) * D],
                                                       wde[:, 0, t, e:e + 1], moe[:, t, :], ALU.mult, ALU.add))
                    dve.after(m)
                    if e % 4 == 3:
                        yield
                freed[t % 2] = m
                m_e = m_next
            dve.after(m_abel)
            for k, src in enumerate((abel, moe)):
                dve.after(dve.did(V.tensor_tensor(xhat[:, :, :], src[:, :, :], rows(gc_w[:, k * D:(k + 1) * D]), ALU.mult)))
                dve.after(dve.did(V.tensor_reduce(gdot[:, :, k], xhat[:, :, :], AX.X, ALU.add)))
                yield
            m = dve.did(V.tensor_scalar(gate[:, :], gdot[:, :, 0], gc_b[:, 0:1], None, ALU.add))
            dve.after(m)
            m = dve.did(V.tensor_tensor(gate[:, :], gate[:, :], gdot[:, :, 1], ALU.add))
            act.after(m)
            m = act.did(A.activation(gate[:, :], gate[:, :], ACT.Tanh, scale=0.5))
            dve.after(dve.did(V.tensor_tensor(moe[:, :, :], moe[:, :, :], abel[:, :, :], ALU.subtract)))
            dve.after(dve.did(V.tensor_tensor(res[:, :, :], res[:, :, :], abel[:, :, :], ALU.add)))
            yield
            dve.after(m)
            dve.after(dve.did(V.tensor_scalar(gate[:, :], gate[:, :], 1.0, 0.5, ALU.add, ALU.mult)))
            dve.after(dve.did(V.tensor_tensor(moe[:, :, :], moe[:, :, :], gate[:, :].unsqueeze(2).broadcast_to([P, NT, D]), ALU.mult)))
            dve.after(dve.did(V.tensor_tensor(moe[:, :, :], moe[:, :, :], res[:, :, :], ALU.add)))
            dve.after(dve.did(V.tensor_tensor(moe[:, :, :], moe[:, :, :], rows(modB[1][:, b, 3, :]), ALU.mult)))
            yield
            m = dve.did(V.tensor_tensor(res[:, :, :], moe[:, :, :], x1[:, :, :], ALU.add))
            out_stored.after(m)
            out_stored.did(nc.sync.dma_start(out[b].rearrange("(t p) d -> p t d", p=P), res[:, :, :]))

        def hand_over():
            m_hi = act.did(A.activation(hTs[0][:, :], hT0[:, :], ACT.Copy))
            m = act.did(A.activation(hT1[:, :], hT0[:, :], ACT.Copy))
            pool.did(G.tensor_copy(x1[:, :, :], x0[:, :, :]))
            dve.after(m_hi)
            m_lo = dve.did(V.tensor_tensor(hTs[1][:, :], hT0[:, :], hTs[0][:, :].bitcast(F32), ALU.subtract))
            pe.after(m, m_lo)
            dve.after(pool.now(), m)
            act.after(m)

        def layer1(b):
            yield from attention()
            dve.after(dve.now())
            dve.after(dve.did(V.tensor_tensor(attn[:, :, :], attn[:, :, :], rows(modB[1][:, b, 0, :]), ALU.mult)))
            dve.after(dve.did(V.tensor_tensor(x1[:, :, :], x1[:, :, :], attn[:, :, :], ALU.add)))
            pe.after(act.now())
            yield from mixture(b)

        def beside(main, side, pace):
            due = 0.0
            for _ in main:
                due += pace
                while side is not None and due >= 1:
                    due -= 1
                    if next(side, StopIteration) is StopIteration:
                        side = None
            for _ in side or ():
                pass

        def settle():
            for e in (pe, dve, act, pool):
                e.after(e.now())

        main_engines = [pe, dve, act, pool]
        for e in main_engines:
            e.after(*(f.now() for f in main_engines), layer0_in.now())
        beside(layer0(0), chain(folded_scores(), rotations()), PACE_SETUP)
        settle()
        with loops.clearing("batches", B - 1, main_engines) as b:
            hand_over()
            beside(layer1(b), chain(read_batch(b + 1), layer0(b + 1)), PACE)
            settle()
        hand_over()
        for _ in layer1(B - 1):
            pass
        out_stored.after(out_stored.now())
        return loops.seen


def _layout(i):
    c = np.ascontiguousarray
    head_major = lambda w: c(w.reshape(D, 2, H1, DH).transpose(0, 2, 1, 3).reshape(D, 2 * H1 * DH))
    width_first = lambda w: w.reshape(D, 2, H1, DH).transpose(1, 3, 2, 0).reshape(2 * DH, H1 * D)
    g = i["L1_ffn_gens"]
    return {
        "x": i["L0_attn_x"], "cT0": c(i["L0_c"].T), "cT1": c(i["L1_c"].T), "wmod0": i["L0_wmod"], "wmod1": i["L1_wmod"],
        "proj_w": i["L0_attn_proj_w"], "proj_b": i["L0_attn_proj_b"].reshape(1, -1),
        "filter": i["L0_attn_filter_time"].reshape(ORDER, TAPS, D),
        "W_upT": c(i["L0_ffn_W_up"].T), "W_downT": c(i["L0_ffn_W_down"].T), "W_q": i["L0_ffn_W_q"],
        "keysT": c(i["L0_ffn_keys"].transpose(2, 0, 3, 1).reshape(2 * PH * PN, KEYS)),
        "downT": c(i["L0_ffn_down_embed"].T), "up_embed": i["L0_ffn_up_embed"],
        "WqkT": c(np.concatenate([width_first(i["L1_attn_Wq"]), width_first(i["L1_attn_Wk"])], axis=1)), "Wv": head_major(i["L1_attn_Wv"]),
        "Wo": i["L1_attn_Wo"],
        "lam": c(np.stack([i["L1_attn_lq1"], i["L1_attn_lk1"], i["L1_attn_lq2"], i["L1_attn_lk2"]])),
        "gammabetaT": c(np.stack([i["L1_ffn_ln_gamma"], i["L1_ffn_ln_beta"]], axis=1)),
        "abel_w": i["L1_ffn_abel_w"], "abel_b": i["L1_ffn_abel_b"].reshape(1, -1),
        "gate_w": i["L1_ffn_moe_gate_w"], "gate_b": i["L1_ffn_moe_gate_b"].reshape(1, -1),
        "ew1": i["L1_ffn_ew1"], "eb1T": c(i["L1_ffn_eb1"].reshape(E1 * HC, P).T),
        "ew2T": c(i["L1_ffn_ew2"].transpose(0, 2, 1)), "eb2T": c(i["L1_ffn_eb2"].T),
        "gens2": c(np.stack([g, g.transpose(0, 2, 1)], axis=1)),
        "gc_w": i["L1_ffn_gc_w"].reshape(1, -1), "gc_b": i["L1_ffn_gc_b"].reshape(1, 1),
    }


def kernel(**inputs):
    import concourse.bacc as bacc
    from concourse.bass_utils import run_bass_kernel_spmd

    arrays = {f"in_{k}": np.ascontiguousarray(v) for k, v in
              {**_layout({k: np.asarray(v) for k, v in inputs.items()}), **host_constants()}.items()}

    def program(per):
        nc = bacc.Bacc("TRN2", target_bir_lowering=False, num_devices=1)
        aps = {name[3:]: nc.dram_tensor(name, v.shape, mybir.dt.from_np(v.dtype), kind="ExternalInput").ap()
               for name, v in arrays.items()}
        out = nc.dram_tensor("out_0", (B, S, D), F32, kind="ExternalOutput").ap()
        return nc, build(nc, per, aps, out)

    _, per = program({})
    nc, _ = program(per)
    r = run_bass_kernel_spmd(nc, [arrays], core_ids=[0])
    return r.results[0]["out_0"]
```
